# Optimizing a Trainium2 kernel written in Bass

```python
import numpy as np
import jax
import jax.numpy as jnp

def _softmax(x, axis=-1):
    return jax.nn.softmax(x, axis=axis)

def _gelu(x):
    return jax.nn.gelu(x, approximate=True)

def _silu(x):
    return jax.nn.silu(x)

def _sigmoid(x):
    return jax.nn.sigmoid(x)

def _layernorm(x, axis=-1, eps=1e-05):
    m = jnp.mean(x, axis=axis, keepdims=True)
    v = jnp.var(x, axis=axis, keepdims=True)
    return (x - m) / jnp.sqrt(v + eps)

def _scatter_add(tgt, idx, src, axis=0):
    return tgt.at[idx].add(src)

def _segment_sum(src, seg, n):
    return jax.ops.segment_sum(src, seg, n)
kernel_name = 'mk_gnn_preln_d4_gnn_r64_c40446'

def setup_inputs(seed: int=0):
    np.random.seed(seed)
    _w = jnp.asarray

    def _rec_inputs():
        import jax
        import jax.numpy as jnp
        _gk = jax.random.key(seed)
        x = -0.000202 + 1 * jax.random.normal(jax.random.fold_in(_gk, 1), (100000, 64), jnp.float32)
        src = jax.random.randint(jax.random.fold_in(_gk, 2), (50000,), 0, 100000, jnp.int32)
        dst = jax.random.randint(jax.random.fold_in(_gk, 3), (50000,), 0, 100000, jnp.int32)
        _o = jnp.argsort(dst, stable=True)
        src = src[_o]
        dst = dst[_o]
        edge_attr_64 = -8.16379e-05 + 0.999858 * jax.random.normal(jax.random.fold_in(_gk, 12), (50000, 64), jnp.float32)
        return (x, src, dst, edge_attr_64)
    x, src, dst, edge_attr_64 = _rec_inputs()

    def _L0_gnn_setup():
        import jax, jax.numpy as jnp
        import numpy as np
        N_NODES = 100000
        N_EDGES = 18750
        D_FEAT = 64
        key = jax.random.key(seed)
        k1, k2, k3 = jax.random.split(key, 3)
        feat = jax.random.normal(k1, (N_NODES, D_FEAT), dtype=jnp.float32)
        eps = jnp.zeros((1,), dtype=jnp.float32)
        edge_src = jax.random.randint(k2, (N_EDGES,), 0, N_NODES, dtype=jnp.int32)
        edge_dst = jax.random.randint(k3, (N_EDGES,), 0, N_NODES, dtype=jnp.int32)
        return {'feat': feat, 'eps': eps, 'edge_src': edge_src, 'edge_dst': edge_dst}
    _L0_gnn_all = _L0_gnn_setup()
    _L0_gnn_in = {k: v for k, v in _L0_gnn_all.items() if k in ('eps',)}
    del _L0_gnn_all

    def _L1_gnn_setup():
        import jax, jax.numpy as jnp
        import numpy as np
        N = 100000
        E = 25000
        D = 64
        H = 128
        L = 3
        BN_EPS = 1e-05
        key = jax.random.key(seed)
        ks = jax.random.split(key, 9)
        x = jax.random.normal(ks[0], (N, D), jnp.float32)
        edge_index = jax.random.randint(ks[1], (2, E), 0, N, dtype=jnp.int64)
        W1 = jax.random.normal(ks[2], (L, D, H), jnp.float32) * (1.0 / np.sqrt(D))
        b1 = jnp.zeros((L, H), jnp.float32)
        gamma = jnp.ones((L, H), jnp.float32)
        beta = jnp.zeros((L, H), jnp.float32)
        W2 = jax.random.normal(ks[3], (L, H, D), jnp.float32) * (1.0 / np.sqrt(H))
        b2 = jnp.zeros((L, D), jnp.float32)
        eps = jnp.zeros((L,), jnp.float32)
        return {'x': x, 'W1': W1, 'b1': b1, 'gamma': gamma, 'beta': beta, 'W2': W2, 'b2': b2, 'eps': eps, 'edge_index': edge_index}
    _L1_gnn_all = _L1_gnn_setup()
    _L1_gnn_in = {k: v for k, v in _L1_gnn_all.items() if k in ('W1', 'b1', 'gamma', 'beta', 'W2', 'b2', 'eps')}
    del _L1_gnn_all

    def _L2_gnn_setup():
        import jax, jax.numpy as jnp
        import numpy as np
        N = 100000
        NE = 25000
        IN_DIM = 64
        OUT_DIM = 64
        H = 8
        D = OUT_DIM // H
        key = jax.random.key(seed)
        ks = jax.random.split(key, 12)
        s = 1.0 / np.sqrt(IN_DIM)
        x = jax.random.normal(ks[0], (N, IN_DIM), jnp.float32)
        edge_attr = jax.random.normal(ks[1], (NE, IN_DIM), jnp.float32)
        edge_index = jax.random.randint(ks[2], (2, NE), 0, N, dtype=jnp.int32)
        WQ = jax.random.normal(ks[3], (IN_DIM, OUT_DIM), jnp.float32) * s
        WK = jax.random.normal(ks[4], (IN_DIM, OUT_DIM), jnp.float32) * s
        WE = jax.random.normal(ks[5], (IN_DIM, OUT_DIM), jnp.float32) * s
        WV = jax.random.normal(ks[6], (IN_DIM, OUT_DIM), jnp.float32) * s
        bQ = jax.random.normal(ks[7], (OUT_DIM,), jnp.float32) * 0.01
        bK = jax.random.normal(ks[8], (OUT_DIM,), jnp.float32) * 0.01
        bE = jax.random.normal(ks[9], (OUT_DIM,), jnp.float32) * 0.01
        bV = jax.random.normal(ks[10], (OUT_DIM,), jnp.float32) * 0.01
        return {'x': x, 'edge_attr': edge_attr, 'edge_index': edge_index, 'WQ': WQ, 'bQ': bQ, 'WK': WK, 'bK': bK, 'WE': WE, 'bE': bE, 'WV': WV, 'bV': bV}
    _L2_gnn_all = _L2_gnn_setup()
    _L2_gnn_in = {k: v for k, v in _L2_gnn_all.items() if k in ('WQ', 'bQ', 'WK', 'bK', 'WE', 'bE', 'WV', 'bV')}
    del _L2_gnn_all

    def _L3_gnn_setup():
        import jax, jax.numpy as jnp
        import numpy as np
        BN_EPS = 1e-05
        key = jax.random.key(seed)
        k1, k2, k3 = jax.random.split(key, 3)
        N, C_IN, C_OUT, E = (50000, 64, 64, 12500)
        x = jax.random.normal(k1, (N, C_IN), dtype=jnp.float32)
        edge_index = jax.random.randint(k2, (2, E), 0, N, dtype=jnp.int64)
        W = jax.random.normal(k3, (C_OUT, 2 * C_IN), dtype=jnp.float32) * (1.0 / np.sqrt(2 * C_IN))
        gamma = jnp.ones((C_OUT,), dtype=jnp.float32)
        beta = jnp.zeros((C_OUT,), dtype=jnp.float32)
        running_mean = jnp.zeros((C_OUT,), dtype=jnp.float32)
        running_var = jnp.ones((C_OUT,), dtype=jnp.float32)
        return {'x': x, 'edge_index': edge_index, 'W': W, 'gamma': gamma, 'beta': beta, 'running_mean': running_mean, 'running_var': running_var}
    _L3_gnn_all = _L3_gnn_setup()
    _L3_gnn_in = {k: v for k, v in _L3_gnn_all.items() if k in ('W', 'gamma', 'beta', 'running_mean', 'running_var')}
    del _L3_gnn_all
    return {'x': x, 'src': src, 'dst': dst, 'edge_attr_64': edge_attr_64, 'L0_gnn_eps': _L0_gnn_in['eps'], 'L1_gnn_W1': _L1_gnn_in['W1'], 'L1_gnn_b1': _L1_gnn_in['b1'], 'L1_gnn_gamma': _L1_gnn_in['gamma'], 'L1_gnn_beta': _L1_gnn_in['beta'], 'L1_gnn_W2': _L1_gnn_in['W2'], 'L1_gnn_b2': _L1_gnn_in['b2'], 'L1_gnn_eps': _L1_gnn_in['eps'], 'L2_gnn_WQ': _L2_gnn_in['WQ'], 'L2_gnn_bQ': _L2_gnn_in['bQ'], 'L2_gnn_WK': _L2_gnn_in['WK'], 'L2_gnn_bK': _L2_gnn_in['bK'], 'L2_gnn_WE': _L2_gnn_in['WE'], 'L2_gnn_bE': _L2_gnn_in['bE'], 'L2_gnn_WV': _L2_gnn_in['WV'], 'L2_gnn_bV': _L2_gnn_in['bV'], 'L3_gnn_W': _L3_gnn_in['W'], 'L3_gnn_gamma': _L3_gnn_in['gamma'], 'L3_gnn_beta': _L3_gnn_in['beta'], 'L3_gnn_running_mean': _L3_gnn_in['running_mean'], 'L3_gnn_running_var': _L3_gnn_in['running_var']}

def reference(x, src, dst, edge_attr_64, L0_gnn_eps, L1_gnn_W1, L1_gnn_b1, L1_gnn_gamma, L1_gnn_beta, L1_gnn_W2, L1_gnn_b2, L1_gnn_eps, L2_gnn_WQ, L2_gnn_bQ, L2_gnn_WK, L2_gnn_bK, L2_gnn_WE, L2_gnn_bE, L2_gnn_WV, L2_gnn_bV, L3_gnn_W, L3_gnn_gamma, L3_gnn_beta, L3_gnn_running_mean, L3_gnn_running_var):
    import jax
    import jax.numpy as jnp

    def _L0_gnn_ref(feat, eps, edge_src, edge_dst):
        import jax, jax.numpy as jnp
        import numpy as np
        N_NODES = 100000
        N_EDGES = 18750
        D_FEAT = 64
        messages = feat[edge_src]
        neigh = jax.ops.segment_sum(messages, edge_dst, num_segments=N_NODES)
        return (1.0 + eps) * feat + neigh

    def _L1_gnn_ref(x, W1, b1, gamma, beta, W2, b2, eps, edge_index):
        import jax, jax.numpy as jnp
        import numpy as np
        N = 100000
        E = 25000
        D = 64
        H = 128
        L = 3
        BN_EPS = 1e-05
        src, dst = (edge_index[0], edge_index[1])
        for l in range(L):
            agg = jax.ops.segment_sum(x[src], dst, num_segments=N)
            h = (1.0 + eps[l]) * x + agg
            h = h @ W1[l] + b1[l]
            mu = jnp.mean(h, axis=0)
            var = jnp.var(h, axis=0)
            h = (h - mu) * jax.lax.rsqrt(var + BN_EPS) * gamma[l] + beta[l]
            h = jax.nn.relu(h)
            x = h @ W2[l] + b2[l]
        return x

    def _L2_gnn_ref(x, edge_attr, edge_index, WQ, bQ, WK, bK, WE, bE, WV, bV):
        import jax, jax.numpy as jnp
        import numpy as np
        N = 100000
        NE = 25000
        IN_DIM = 64
        OUT_DIM = 64
        H = 8
        D = OUT_DIM // H
        n = x.shape[0]
        Qh = (x @ WQ + bQ).reshape(n, H, D)
        Kh = (x @ WK + bK).reshape(n, H, D)
        Vh = (x @ WV + bV).reshape(n, H, D)
        Eh = (edge_attr @ WE + bE).reshape(-1, H, D)
        src = edge_index[0]
        dst = edge_index[1]
        inv_sqrt_d = jnp.float32(1.0 / np.sqrt(D))
        score = Kh[src] * Qh[dst] * inv_sqrt_d * Eh
        score = jnp.exp(jnp.clip(score.sum(-1, keepdims=True), -5.0, 5.0))
        msg = Vh[src] * score
        wV = jax.ops.segment_sum(msg, dst, num_segments=n)
        return wV.reshape(n, H * D)

    def _L3_gnn_ref(x, edge_index, W, gamma, beta, running_mean, running_var):
        import jax, jax.numpy as jnp
        import numpy as np
        BN_EPS = 1e-05
        num_nodes = x.shape[0]
        row, col = (edge_index[0], edge_index[1])
        x_i = x[row]
        x_j = x[col]
        edge_feat = jnp.concatenate([x_i, x_j - x_i], axis=1)
        h = jnp.einsum('ec,oc->eo', edge_feat, W)
        inv_std = jax.lax.rsqrt(running_var + BN_EPS)
        h = (h - running_mean) * (gamma * inv_std) + beta
        h = h * jax.nn.sigmoid(h)
        return jax.ops.segment_sum(h, row, num_segments=num_nodes)
    edge_index = jnp.stack([src, dst])
    h = jnp.maximum(_layernorm(x, axis=-1), 0.0)
    x = x + _L0_gnn_ref(h, L0_gnn_eps, src, dst)
    h = jnp.maximum(_layernorm(x, axis=-1), 0.0)
    x = x + _L1_gnn_ref(h, L1_gnn_W1, L1_gnn_b1, L1_gnn_gamma, L1_gnn_beta, L1_gnn_W2, L1_gnn_b2, L1_gnn_eps, edge_index)
    h = jnp.maximum(_layernorm(x, axis=-1), 0.0)
    x = x + _L2_gnn_ref(h, edge_attr_64, edge_index, L2_gnn_WQ, L2_gnn_bQ, L2_gnn_WK, L2_gnn_bK, L2_gnn_WE, L2_gnn_bE, L2_gnn_WV, L2_gnn_bV)
    h = jnp.maximum(_layernorm(x, axis=-1), 0.0)
    x = x + _L3_gnn_ref(h, edge_index, L3_gnn_W, L3_gnn_gamma, L3_gnn_beta, L3_gnn_running_mean, L3_gnn_running_var)
    return x

_drawn_inputs = setup_inputs


def setup_inputs(seed=0):
    import zlib

    import numpy as np

    out = dict(_drawn_inputs(seed))
    spreads = {'L1_gnn_b1': (0.0, 0.8),
     'L1_gnn_gamma': (1.0, 0.2),
     'L1_gnn_beta': (0.0, 0.1),
     'L1_gnn_b2': (0.0, 0.1),
     'L1_gnn_eps': (0.0, 0.568),
     'L3_gnn_gamma': (1.0, 0.2),
     'L3_gnn_beta': (0.0, 0.438),
     'L3_gnn_running_mean': (0.0, 0.392),
     'L3_gnn_running_var': (1.0, 0.6)}
    factors = {'L2_gnn_bQ': 8.0, 'L2_gnn_bK': 8.0, 'L2_gnn_bE': 8.0, 'L2_gnn_bV': 7.603}
    for name, (base, spread) in spreads.items():
        noise = np.random.default_rng([zlib.crc32(name.encode()), seed]).standard_normal(out[name].shape)
        drawn = base * np.exp(spread * noise) if base else spread * noise
        out[name] = jnp.asarray(drawn.astype(out[name].dtype))
    for name, factor in factors.items():
        out[name] = (out[name] * factor).astype(out[name].dtype)
    return out
```

```python
import concourse.bass as bass
from concourse import mybir
from contextlib import ExitStack, contextmanager

FP32 = mybir.dt.float32
INT32 = mybir.dt.int32
ALU = mybir.AluOpType
ACT = mybir.ActivationFunctionType
AX = mybir.AxisListType

P = 128
N_NODES, N_EDGES, D, HID, HEADS = 100000, 50000, 64, 128, 8
PLACES = 800
ROWS = P * PLACES
NODE_PARTS = N_NODES // PLACES
assert NODE_PARTS * PLACES == N_NODES and ROWS - N_NODES >= P
CH = 16
STEPS = PLACES // CH // 2
CHW = CH * D
TILES = -(-N_EDGES // P)
QT = 4
ESTEPS = -(-TILES // (2 * QT))
COLS = 400
assert COLS >= (ESTEPS * 2 + 1) * QT
LN_EPS = 1e-5
BN_EPS = 1e-5


class Stage:

    def __init__(self, nc, name):
        self.nc, self.name, self.ctx, self.sems = nc, name, ExitStack(), []

    def __enter__(self):
        self.ctx.__enter__()
        return self

    def sem(self, name):
        self.sems.append(self.nc.alloc_semaphore(name=f"{self.name}_{name}"))
        return self.sems[-1]

    def pair(self, name):
        return [self.sem(f"{name}0"), self.sem(f"{name}1")]

    def sb(self, name, shape, dt=FP32):
        return self.ctx.enter_context(self.nc.sbuf_tensor(f"{self.name}_{name}", shape, dt))

    def ps(self, name, shape):
        return self.ctx.enter_context(self.nc.psum_tensor(f"{self.name}_{name}", shape, FP32))

    def block(self):
        return self.nc.Block()

    def __exit__(self, *a):
        self.ctx.__exit__(*a)
        if a[0] is None:
            self.nc.clear_and_free_semaphores(self.sems)
            self.nc.all_engine_barrier()


def wait(eng, sem, value):
    if not (isinstance(value, int) and value <= 0):
        eng.wait_ge(sem, value)


def loop(eng, steps, step):
    step(0)
    with eng.Fori(1, steps) as i:
        step(i)


def places(table):
    return table.rearrange("(p j) f -> p j f", p=P)


def chunk(view, c):
    return view[:, bass.ds(c * CH, CH), :]


def setup(nc, st, I, C, src_rows, dst_rows):
    stage, loaded, built, turned = (st.sem(x) for x in ("stg_filled", "params_loaded", "consts_built", "turned"))
    rows_loaded, rows_stored, cols_ready = st.sem("rows_loaded"), st.sem("rows_stored"), st.sem("cols_ready")
    var_ready, std_ready, dve_done = st.sem("var_ready"), st.sem("std_ready"), st.sem("dve_done")
    NB = COLS // 4
    rows = [st.sb(f"idx_rows{k}", [NB, 4, P], INT32) for k in range(2)]
    rows_f = [st.sb(f"idx_rows_f{k}", [NB, 4, P]) for k in range(2)]
    cols_ps = [st.ps(f"cols_ps{k}", [P, 512]) for k in range(2)]
    w3 = st.sb("w3_rows", [D, 2 * D])
    w3_ps = st.ps("w3_ps", [P, 512])
    one_eps = st.sb("eps_raw", [P, 4])
    iden0 = st.sb("iden0", [P, P])
    row1 = lambda a: a.rearrange("(a n) -> a n", a=1)
    NLOAD = 0

    loads = [(w3[:, :], I["L3_gnn_W"])]
    for l in range(3):
        for half in range(2):
            loads.append((C["w1"][l][half * D:(half + 1) * D, :], I["L1_gnn_W1"][l, :, :]))
        loads.append((C["w2"][l][:, :], I["L1_gnn_W2"][l, :, :]))
        loads.append((C["b2"][l][:, :], I["L1_gnn_b2"][l:l + 1, :].partition_broadcast(P)))
        for k, name in enumerate(("b1", "gamma", "beta")):
            loads.append((C["bn"][:, 4 * l + k:4 * l + k + 1],
                          I["L1_gnn_" + name][l, :].rearrange("(p a) -> p a", a=1)))
    loads.append((one_eps[:, 0:1], row1(I["L0_gnn_eps"]).partition_broadcast(P)))
    loads.append((one_eps[:, 1:4], row1(I["L1_gnn_eps"]).partition_broadcast(P)))
    for half in range(2):
        loads.append((C["we"][half * D:(half + 1) * D, :], I["L2_gnn_WE"]))
    loads.append((C["kvq"][0:D, 0:D], I["L2_gnn_WK"]))
    loads.append((C["kvq"][0:D, D:2 * D], I["L2_gnn_WV"]))
    loads.append((C["kvq"][D:2 * D, 2 * D:3 * D], I["L2_gnn_WQ"]))
    for k, name in enumerate(("bK", "bV", "bQ", "bE")):
        loads.append((C["kvqe_b"][:, k * D:(k + 1) * D], row1(I["L2_gnn_" + name]).partition_broadcast(P)))
    for k, name in enumerate(("running_mean", "gamma", "beta", "running_var")):
        loads.append((C["ec"][:, k * D:(k + 1) * D], row1(I["L3_gnn_" + name]).partition_broadcast(P)))
    NL = len(loads)
    full = N_EDGES // P
    tail = N_EDGES - full * P

    with st.block() as block:
        @block.gpsimd
        def _(pool):
            for k in range(2):
                nc.gpsimd.iota(rows[k][:, :, :], pattern=[[0, 4], [1, P]], base=N_NODES,
                               channel_multiplier=0).then_inc(stage, 1)
            nc.gpsimd.iota(C["spare_i"][:, :], pattern=[[0, 1]], base=N_NODES, channel_multiplier=1).then_inc(stage, 1)
            nc.gpsimd.memset(iden0[:, :], 0.0).then_inc(stage, 1)
            nc.gpsimd.memset(C["lower"][:, :], 1.0).then_inc(stage, 1)
            nc.gpsimd.memset(C["zeros"][:, :], 0.0).then_inc(stage, 1)
            nc.gpsimd.memset(C["ones"][:, :], 1.0).then_inc(stage, 1)
            nc.gpsimd.memset(C["kvq"][:, :], 0.0).then_inc(stage, 1)
            pool.wait_ge(stage, 8)
            nc.gpsimd.affine_select(out=C["iden"][:, :], in_=iden0[:, :], compare_op=ALU.not_equal, fill=1.0,
                                    base=0, pattern=[[-1, P]], channel_multiplier=1).then_inc(built, 1)
            nc.gpsimd.affine_select(out=C["lower"][:, :], in_=C["lower"][:, :], compare_op=ALU.is_gt, fill=0.0,
                                    base=0, pattern=[[-1, P]], channel_multiplier=1).then_inc(built, 1)

        @block.sync
        def _(sp):
            sp.wait_ge(stage, 8)
            for k, name in enumerate(("src", "dst")):
                whole = I[name][0:full * P].rearrange("(t e) -> t e", e=P)
                sp.dma_start(rows[k][:, 0:3, :], whole[0:3 * NB, :].rearrange("(b t) e -> t b e", b=3)).then_inc(rows_loaded, 16)
                sp.dma_start(rows[k][0:full - 3 * NB, 3, :], whole[3 * NB:full, :]).then_inc(rows_loaded, 16)
                sp.dma_start(rows[k][full - 3 * NB:full - 3 * NB + 1, 3, 0:tail], row1(I[name][full * P:N_EDGES])).then_inc(rows_loaded, 16)
            for to, of in loads:
                sp.dma_start(to, of).then_inc(loaded, 16)
            sp.wait_ge(rows_loaded, 96)
            for k, table in enumerate((src_rows, dst_rows)):
                sp.dma_start(table.rearrange("(b t) e -> t b e", b=4), rows[k][:, :, :]).then_inc(rows_stored, 16)
            sp.wait_ge(rows_stored, 32)
            sp.wait_ge(loaded, 16 * NL)

        @block.tensor
        def _(pe):
            pe.wait_ge(built, 2)
            for k in range(2):
                pe.wait_ge(cols_ready, k + 1)
                for b in range(4):
                    last = nc.tensor.transpose(cols_ps[k][:, b * NB:(b + 1) * NB], rows_f[k][:, b, :], C["iden"][0:NB, 0:NB])
                last.then_inc(turned, 1)
            pe.wait_ge(loaded, 16 * NL)
            nc.tensor.transpose(w3_ps[:, 0:D], w3[:, :], C["iden"][0:D, 0:D]).then_inc(turned, 1)

        @block.vector
        def _(dve):
            dve.wait_ge(rows_loaded, 96)
            for k in range(2):
                nc.vector.tensor_copy(rows_f[k][:, :, :], rows[k][:, :, :]).then_inc(cols_ready, 1)
            for k, name in enumerate(("src", "dst")):
                dve.wait_ge(turned, k + 1)
                nc.vector.tensor_copy(C[name + "_f"][:, :], cols_ps[k][:, 0:COLS])
                nc.vector.tensor_copy(C[name + "_i"][:, :], cols_ps[k][:, 0:COLS])
            dve.wait_ge(stage, 8)
            nc.vector.tensor_copy(C["spare"][:, :], C["spare_i"][:, :])
            dve.wait_ge(turned, 3)
            nc.vector.tensor_copy(C["w3"][:, :], w3_ps[:, 0:D])
            nc.vector.tensor_scalar(C["eps1"][:, :], one_eps[:, :], 1.0, None, ALU.add)
            var, gam = C["ec"][:, 3 * D:4 * D], C["ec"][:, D:2 * D]
            nc.vector.tensor_scalar(var, var, BN_EPS, None, ALU.add).then_inc(var_ready, 1)
            dve.wait_ge(std_ready, 1)
            nc.vector.reciprocal(var, var).then_inc(dve_done, 1)
            dve.wait_ge(dve_done, 1)
            nc.vector.tensor_tensor(gam, gam, var, ALU.mult)

        @block.scalar
        def _(act):
            act.wait_ge(var_ready, 1)
            nc.scalar.activation(C["ec"][:, 3 * D:4 * D], C["ec"][:, 3 * D:4 * D], ACT.Sqrt).then_inc(std_ready, 1)


def duplicates(nc, st, C, rows_dram, name):
    loaded, equal, masked, counted, used = (st.pair(x) for x in ("rows_loaded", "equal", "masked", "counted", "rows_used"))
    done = st.sem("scatter_cols")
    rows = [st.sb(f"row_bc{s}", [P, QT, P], INT32) for s in range(2)]
    eq = [st.sb(f"eq{s}", [P, QT, P]) for s in range(2)]
    count = st.sb("count", [P, COLS])
    dist = st.sb("dist", [P, COLS])

    with st.block() as block:
        @block.sync
        def _(sp):
            def step(i):
                for s in range(2):
                    wait(sp, used[s], i)
                    sp.dma_start(rows[s][:, :, :], rows_dram[bass.ds((2 * i + s) * QT, QT), :].rearrange("(a t) e -> a t e", a=1).partition_broadcast(P)).then_inc(loaded[s], 16)

            loop(sp, COLS // QT // 2, step)

        @block.vector
        def _(dve):
            def step(i):
                for s in range(2):
                    cols = C[name + "_f"][:, bass.ds((2 * i + s) * QT, QT)].unsqueeze(2).to_broadcast([P, QT, P])
                    wait(dve, loaded[s], 16 * i + 16)
                    wait(dve, counted[s], i)
                    nc.vector.tensor_tensor(eq[s][:, :, :], rows[s][:, :, :], cols, ALU.is_equal).then_inc(used[s], 1)
                for s in range(2):
                    wait(dve, used[s], i + 1)
                    nc.vector.tensor_tensor(eq[s][:, :, :], eq[s][:, :, :], C["lower"][:, :].unsqueeze(1).to_broadcast([P, QT, P]), ALU.mult).then_inc(masked[s], 1)
                for s in range(2):
                    wait(dve, masked[s], i + 1)
                    nc.vector.tensor_reduce(count[:, bass.ds((2 * i + s) * QT, QT)], eq[s][:, :, :], AX.X, ALU.add).then_inc(counted[s], 1)

            loop(dve, COLS // QT // 2, step)
            for s in range(2):
                dve.wait_ge(counted[s], COLS // QT // 2)
            nc.vector.tensor_scalar(count[:, :], count[:, :], 0.0, None, ALU.is_gt).then_inc(done, 1)
            nc.vector.tensor_scalar(dist[:, :], C[name + "_f"][:, :], -1.0, C["spare"][:, 0:1], ALU.mult, ALU.add).then_inc(done, 1)
            dve.wait_ge(done, 2)
            nc.vector.tensor_tensor(dist[:, :], dist[:, :], count[:, :], ALU.mult).then_inc(done, 1)
            dve.wait_ge(done, 3)
            nc.vector.tensor_tensor(C["scatter_" + name][:, :], dist[:, :], C[name + "_f"][:, :], ALU.add)


def layernorm(nc, st, C, source, h_table, base_table=None, eps_col=None, add_source=False):
    loaded, used, summed, mean_ready, centred, squared, ssum, var_ready, std_ready, rstd_ready, h_ready, base_ready, h_stored, base_stored = (
        st.pair(x) for x in ("x_loaded", "x_used", "summed", "mean_ready", "centred", "squared", "ssum", "var_ready",
                             "std_ready", "rstd_ready", "h_ready", "base_ready", "h_stored", "base_stored"))
    cleared = st.sem("cleared")
    x = [st.sb(f"x{s}", [P, CH, D]) for s in range(2)]
    xc = [st.sb(f"xc{s}", [P, CH, D]) for s in range(2)]
    sq = [st.sb(f"sq{s}", [P, CH, D]) for s in range(2)]
    h = [st.sb(f"h{s}", [P, CH, D]) for s in range(2)]
    base = [st.sb(f"base{s}", [P, CH, D]) for s in range(2)]
    s1, mean, s2, var, rstd = ([st.sb(f"{x}{s}", [P, CH]) for s in range(2)] for x in ("s1", "mean", "s2", "var", "rstd"))
    padded = source.shape[0] == ROWS
    src = source.rearrange("(p j) f -> p j f", j=PLACES)
    hv, bv = places(h_table), places(base_table) if base_table is not None else None
    wide = lambda t: t[:, :].unsqueeze(2).to_broadcast([P, CH, D])
    parts = [(0, P)] if padded else [(0, 112), (112, NODE_PARTS)]

    with st.block() as block:
        @block.sync
        def _(sp):
            if not padded:
                sp.wait_ge(cleared, 1)
            def step(i):
                for s in range(2):
                    wait(sp, used[s], i)
                    for a, b in parts:
                        sp.dma_start(x[s][a:b, :, :], src[a:b, bass.ds((2 * i + s) * CH, CH), :]).then_inc(loaded[s], 16)

            loop(sp, STEPS, step)

        @block.vector
        def _(dve):
            if not padded:
                for s in range(2):
                    last = nc.vector.memset(x[s][:, :, :], 0.0)
                last.then_inc(cleared, 1)
            def step(i):
                for s in range(2):
                    wait(dve, loaded[s], 16 * len(parts) * i + 16 * len(parts))
                    wait(dve, h_ready[s], i)
                    nc.vector.tensor_reduce(s1[s][:, :], x[s][:, :, :], AX.X, ALU.add).then_inc(summed[s], 1)
                    wait(dve, summed[s], i + 1)
                    nc.vector.tensor_scalar(mean[s][:, :], s1[s][:, :], 1.0 / D, None, ALU.mult).then_inc(mean_ready[s], 1)
                    wait(dve, mean_ready[s], i + 1)
                    last = nc.vector.tensor_tensor(xc[s][:, :, :], x[s][:, :, :], wide(mean[s]), ALU.subtract)
                    last.then_inc(centred[s], 1)
                    if not add_source:
                        wait(dve, centred[s], i + 1)
                        nc.vector.sem_inc(used[s], 1)
                for s in range(2):
                    wait(dve, squared[s], i + 1)
                    nc.vector.tensor_reduce(s2[s][:, :], sq[s][:, :, :], AX.X, ALU.add).then_inc(ssum[s], 1)
                    wait(dve, ssum[s], i + 1)
                    nc.vector.tensor_scalar(var[s][:, :], s2[s][:, :], 1.0 / D, LN_EPS, ALU.mult, ALU.add).then_inc(var_ready[s], 1)
                for s in range(2):
                    wait(dve, std_ready[s], i + 1)
                    nc.vector.reciprocal(rstd[s][:, :], var[s][:, :]).then_inc(rstd_ready[s], 1)
                    wait(dve, rstd_ready[s], i + 1)
                    wait(dve, h_stored[s], 16 * i)
                    nc.vector.scalar_tensor_tensor(h[s][:, :, :], xc[s][:, :, :], 0.0, wide(rstd[s]), ALU.max, ALU.mult).then_inc(h_ready[s], 1)
                    if add_source:
                        wait(dve, h_ready[s], i + 1)
                        wait(dve, base_stored[s], 16 * i)
                        nc.vector.scalar_tensor_tensor(base[s][:, :, :], h[s][:, :, :], eps_col, x[s][:, :, :], ALU.mult, ALU.add).then_inc(base_ready[s], 1)
                        wait(dve, base_ready[s], i + 1)
                        nc.vector.sem_inc(used[s], 1)

            loop(dve, STEPS, step)

        @block.scalar
        def _(act):
            def step(i):
                for s in range(2):
                    wait(act, centred[s], i + 1)
                    nc.scalar.activation(sq[s][:, :, :], xc[s][:, :, :], ACT.Square).then_inc(squared[s], 1)
                for s in range(2):
                    wait(act, var_ready[s], i + 1)
                    nc.scalar.activation(var[s][:, :], var[s][:, :], ACT.Sqrt).then_inc(std_ready[s], 1)
                for s in range(2):
                    wait(act, h_ready[s], i + 1)
                    act.dma_start(chunk(hv, 2 * i + s), h[s][:, :, :]).then_inc(h_stored[s], 16)
                    if bv is not None:
                        if not add_source:
                            wait(act, base_stored[s], 16 * i)
                            nc.scalar.activation(base[s][:, :, :], h[s][:, :, :], ACT.Copy, scale=eps_col).then_inc(base_ready[s], 1)
                        wait(act, base_ready[s], i + 1)
                        act.dma_start(chunk(bv, 2 * i + s), base[s][:, :, :]).then_inc(base_stored[s], 16)

            loop(act, STEPS, step)
            for s in range(2):
                act.wait_ge(h_stored[s], 16 * STEPS)
                if bv is not None:
                    act.wait_ge(base_stored[s], 16 * STEPS)


def batch_stats(nc, st, C, table, l):
    loaded, used = st.pair("t_loaded"), st.pair("t_used")
    summed, tail = st.sem("summed"), st.sem("tail")
    mm, std_ready = st.sem("mm"), st.sem("std_ready")
    t = [st.sb(f"t{s}", [P, CHW]) for s in range(2)]
    gram_sb = st.sb("gram_sb", [P, P])
    sum_sb = st.sb("sum_sb", [P, 1])
    prod = st.sb("prod", [P, HID])
    cols = st.sb("cols", [P, 8])
    gram, tsum, wg, moments = (st.ps(x, [P, 512]) for x in ("gram", "tsum", "wg", "moments"))
    tv = places(table).rearrange("p j f -> p (j f)")
    bn, w1 = C["bn"], C["w1"][l]
    PAIR = 2 * D

    with st.block() as block:
        @block.sync
        def _(sp):
            def step(i):
                for s in range(2):
                    wait(sp, used[s], i)
                    sp.dma_start(t[s][:, :], tv[:, bass.ds((2 * i + s) * CHW, CHW)]).then_inc(loaded[s], 16)

            loop(sp, STEPS, step)

        @block.tensor
        def _(pe):
            nc.tensor.matmul(gram[:, 0:P], C["zeros"][:, :], C["zeros"][:, :], start=True, stop=False)
            nc.tensor.matmul(tsum[:, 0:1], C["zeros"][:, :], C["zeros"][:, 0:1], start=True, stop=False)
            def step(i):
                for s in range(2):
                    wait(pe, loaded[s], 16 * i + 16)
                    for q in range(CH // 2):
                        two = t[s][0:NODE_PARTS, q * PAIR:(q + 1) * PAIR]
                        nc.tensor.matmul(gram[:, 0:P], two, two, start=False, stop=False)
                        last = nc.tensor.matmul(tsum[:, 0:1], two, C["ones"][0:NODE_PARTS, 0:1], start=False, stop=False)
                    last.then_inc(used[s], 1)

            loop(pe, STEPS, step)
            nc.tensor.matmul(gram[:, 0:P], C["zeros"][:, :], C["zeros"][:, :], start=False, stop=True)
            nc.tensor.matmul(tsum[:, 0:1], C["zeros"][:, :], C["zeros"][:, 0:1], start=False, stop=True).then_inc(summed, 1)
            pe.wait_ge(tail, 2)
            nc.tensor.matmul(wg[:, 0:HID], gram_sb[:, :], w1[:, :], start=True, stop=True)
            nc.tensor.matmul(moments[:, 0:1], w1[:, :], sum_sb[:, :], start=True, stop=True).then_inc(mm, 1)
            pe.wait_ge(tail, 3)
            nc.tensor.matmul(wg[:, HID:HID + 1], prod[:, :], C["ones"][:, 0:1], start=True, stop=True).then_inc(mm, 1)

        @block.vector
        def _(dve):
            n = [0]

            def link(ins):
                n[0] += 1
                ins.then_inc(tail, 1)
                dve.wait_ge(tail, n[0])

            nc.vector.memset(gram_sb[:, :], 0.0).then_inc(mm, 1)
            dve.wait_ge(mm, 1)
            dve.wait_ge(summed, 1)
            nc.vector.tensor_copy(gram_sb[0:D, 0:D], gram[0:D, 0:D])
            link(nc.vector.tensor_copy(gram_sb[D:P, D:P], gram[D:P, D:P]))
            link(nc.vector.tensor_copy(sum_sb[:, :], tsum[:, 0:1]))
            dve.wait_ge(mm, 2)
            link(nc.vector.tensor_tensor(prod[:, :], wg[:, 0:HID], w1[:, :], ALU.mult))
            dve.wait_ge(mm, 3)
            c = lambda k: cols[:, k:k + 1]
            link(nc.vector.tensor_scalar(c(0), moments[:, 0:1], 1.0 / N_NODES, None, ALU.mult))
            link(nc.vector.tensor_scalar(c(1), wg[:, HID:HID + 1], 1.0 / N_NODES, None, ALU.mult))
            link(nc.vector.tensor_tensor(c(2), c(0), c(0), ALU.mult))
            link(nc.vector.tensor_tensor(c(2), c(1), c(2), ALU.subtract))
            link(nc.vector.tensor_scalar(c(2), c(2), 0.0, BN_EPS, ALU.max, ALU.add))
            dve.wait_ge(std_ready, 1)
            link(nc.vector.reciprocal(c(2), c(2)))
            link(nc.vector.tensor_tensor(C["bn_scale"][:, :], c(2), bn[:, 4 * l + 1:4 * l + 2], ALU.mult))
            link(nc.vector.tensor_tensor(c(4), c(0), bn[:, 4 * l:4 * l + 1], ALU.add))
            link(nc.vector.tensor_tensor(c(5), bn[:, 4 * l:4 * l + 1], c(4), ALU.subtract))
            link(nc.vector.tensor_tensor(c(6), c(5), C["bn_scale"][:, :], ALU.mult))
            link(nc.vector.tensor_tensor(C["bn_shift"][:, :], c(6), bn[:, 4 * l + 2:4 * l + 3], ALU.add))

        @block.scalar
        def _(act):
            act.wait_ge(tail, 8)
            nc.scalar.activation(cols[:, 2:3], cols[:, 2:3], ACT.Sqrt).then_inc(std_ready, 1)


def mlp(nc, st, C, table, l, h_table=None, base_table=None, eps_col=None, residual=None, out=None):
    final = out is not None
    loaded, t_used = st.pair("t_loaded"), st.pair("t_used")
    x_loaded, x_used = st.pair("x_loaded"), st.pair("x_used")
    y_stored, b_stored, y_ready, b_ready = st.pair("y_stored"), st.pair("b_stored"), st.pair("y_ready"), st.pair("b_ready")
    units = lambda n: [[st.sem(f"{n}{s}{r}") for r in range(2)] for s in range(2)]
    turned, tt_ready, hid_ps_ready, hid_ready, y_ps_ready, y_done = (
        units(n) for n in ("turned", "tt_ready", "hid_ps_ready", "hid_ready", "y_ps_ready", "y_done"))
    t = [st.sb(f"t{s}", [P, CHW]) for s in range(2)]
    y = [st.sb(f"y{s}", [P, CHW]) for s in range(2)]
    b = [st.sb(f"b{s}", [P, CHW]) for s in range(2)]
    tt = [st.sb(f"tt{r}", [P, 512]) for r in range(2)]
    hid = [[st.sb(f"hid{r}{e}", [P, 512]) for e in range(2)] for r in range(2)]
    t_ps = [st.ps(f"t_ps{r}", [P, 512]) for r in range(2)]
    hid_ps = [[st.ps(f"hid_ps{r}{e}", [P, 512]) for e in range(2)] for r in range(2)]
    y_ps = [st.ps(f"y_ps{r}", [P, 512]) for r in range(2)]
    flat = lambda table: places(table).rearrange("p j f -> p (j f)")
    tv = flat(table)
    part = lambda v, c: v[:, bass.ds(c * CHW, CHW)]
    w1, w2, b2 = C["w1"][l], C["w2"][l], C["b2"][l]
    PAIR, HALF = 2 * D, CHW // 2
    UNITS = [(s, r) for s in range(2) for r in range(2)]

    with st.block() as block:
        @block.sync
        def _(sp):
            def step(i):
                for s in range(2):
                    wait(sp, t_used[s], 2 * i)
                    sp.dma_start(t[s][:, :], part(tv, 2 * i + s)).then_inc(loaded[s], 16)
                    if final:
                        wait(sp, y_stored[s], 16 * i)
                        sp.dma_start(b[s][:, :], part(flat(residual), 2 * i + s)).then_inc(x_loaded[s], 16)

            loop(sp, STEPS, step)

        @block.tensor
        def _(pe):
            def turn(i, s, r):
                wait(pe, loaded[s], 16 * i + 16)
                wait(pe, tt_ready[1 - s][r], i + s)
                for q in range(4):
                    lo = r * HALF + q * PAIR
                    last = nc.tensor.transpose(t_ps[r][:, q * P:(q + 1) * P], t[s][:, lo:lo + PAIR], C["iden"][:, :])
                last.then_inc(turned[s][r], 1)

            def hidden(i, s, r):
                wait(pe, tt_ready[s][r], i + 1)
                wait(pe, hid_ready[1 - s][r], i + s)
                for e in range(2):
                    last = nc.tensor.matmul(hid_ps[r][e][:, :], w1[e * D:(e + 1) * D, :], tt[r][e * D:(e + 1) * D, :], start=True, stop=True)
                last.then_inc(hid_ps_ready[s][r], 1)

            def output(i, s, r):
                wait(pe, hid_ready[s][r], i + 1)
                wait(pe, y_done[1 - s][r], i + s)
                for q in range(4):
                    for e in range(2):
                        k = 2 * q + e
                        last = nc.tensor.matmul(y_ps[r][:, k * D:(k + 1) * D], hid[r][e][:, q * P:(q + 1) * P], w2[:, :], start=True, stop=True)
                last.then_inc(y_ps_ready[s][r], 1)

            def step(i, first, last):
                for k, (s, r) in enumerate(UNITS):
                    if k < 3:
                        turn(i, *UNITS[k + 1])
                    elif not last:
                        turn(i + 1, *UNITS[0])
                    hidden(i, s, r)
                    if k:
                        output(i, *UNITS[k - 1])
                    elif not first:
                        output(i - 1, *UNITS[3])

            turn(0, *UNITS[0])
            step(0, True, False)
            with pe.Fori(1, STEPS - 1) as i:
                step(i, False, False)
            step(STEPS - 1, False, True)
            output(STEPS - 1, *UNITS[3])

        @block.scalar
        def _(act):
            def relu(i, s, r):
                wait(act, hid_ps_ready[s][r], i + 1)
                wait(act, y_ps_ready[1 - s][r], i + s)
                for e in range(2):
                    last = nc.scalar.activation(hid[r][e][:, :], hid_ps[r][e][:, :], ACT.Relu, bias=C["bn_shift"][:, 0:1], scale=C["bn_scale"][:, 0:1])
                last.then_inc(hid_ready[s][r], 1)

            def step(i):
                for s, r in UNITS:
                    relu(i, s, r)

            loop(act, STEPS, step)

        @block.vector
        def _(dve):
            def evict(i, s, r):
                wait(dve, turned[s][r], i + 1)
                wait(dve, hid_ps_ready[1 - s][r], i + s)
                nc.vector.tensor_copy(tt[r][:, :], t_ps[r][:, :]).then_inc(tt_ready[s][r], 1)
                wait(dve, tt_ready[s][r], i + 1)
                nc.vector.sem_inc(t_used[s], 1)

            def finish(i, s, r):
                wait(dve, y_ps_ready[s][r], i + 1)
                half = slice(r * HALF, (r + 1) * HALF)
                if final:
                    wait(dve, x_loaded[s], 16 * i + 16)
                elif r == 0:
                    wait(dve, b_stored[s], 16 * i)
                if r == 0:
                    wait(dve, y_stored[s], 16 * i)
                yh = y[s][:, half]
                nc.vector.tensor_tensor(yh.rearrange("p (k f) -> p k f", f=D), y_ps[r][:, :].rearrange("p (k f) -> p k f", f=D),
                                        b2[:, :].unsqueeze(1).to_broadcast([P, 8, D]), ALU.add).then_inc(y_done[s][r], 1)
                if final:
                    wait(dve, y_done[s][r], i + 1)
                    nc.vector.tensor_tensor(b[s][:, half], yh, b[s][:, half], ALU.add).then_inc(b_ready[s], 1)
                else:
                    wait(dve, y_done[s][r], i + 1)
                    nc.vector.tensor_scalar(b[s][:, half], yh, eps_col, None, ALU.mult).then_inc(b_ready[s], 1)

            def step(i, first, last):
                for k, (s, r) in enumerate(UNITS):
                    if k < 3:
                        evict(i, *UNITS[k + 1])
                    elif not last:
                        evict(i + 1, *UNITS[0])
                    if k:
                        finish(i, *UNITS[k - 1])
                    elif not first:
                        finish(i - 1, *UNITS[3])

            evict(0, *UNITS[0])
            step(0, True, False)
            with dve.Fori(1, STEPS - 1) as i:
                step(i, False, False)
            step(STEPS - 1, False, True)
            finish(STEPS - 1, *UNITS[3])

        @block.gpsimd
        def _(pool):
            def step(i):
                for s in range(2):
                    wait(pool, b_ready[s], 2 * i + 2)
                    if final:
                        pool.dma_start(part(flat(out), 2 * i + s), b[s][:, :]).then_inc(y_stored[s], 16)
                    else:
                        pool.dma_start(part(flat(h_table), 2 * i + s), y[s][:, :]).then_inc(y_stored[s], 16)
                        pool.dma_start(part(flat(base_table), 2 * i + s), b[s][:, :]).then_inc(b_stored[s], 16)

            loop(pool, STEPS, step)
            for s in range(2):
                pool.wait_ge(y_stored[s], 16 * STEPS)
                if not final:
                    pool.wait_ge(b_stored[s], 16 * STEPS)


def edges(nc, st, C, kind, h_table, base_table, rows_dram, gather_cols, target, edge_attr=None):
    K = len(gather_cols)
    WIDE = K * D
    gathered = [st.pair(f"gathered_{name}") for name in gather_cols]
    admitted = st.sem("admitted")
    scattered, g_idx, s_idx = st.pair("scattered"), st.pair("gather_idx"), st.pair("scatter_idx")
    rows_loaded, eq_ready, merged_ps, merged_ready = (st.pair(x) for x in ("rows_loaded", "eq_ready", "merged_ps", "merged_ready"))
    rows = [st.sb(f"row_bc{s}", [P, QT, P], INT32) for s in range(2)]
    eq = [st.sb(f"eq{s}", [P, QT, P]) for s in range(2)]
    G = [st.sb(f"G{s}", [P, QT, WIDE]) for s in range(2)]
    gi = [[st.sb(f"gi{s}{g}", [P, QT], INT32) for g in range(K)] for s in range(2)]
    si = [st.sb(f"si{s}", [P, QT], INT32) for s in range(2)]
    merged = [st.sb(f"merged{s}", [P, QT, D]) for s in range(2)]
    m_ps = [st.ps(f"m_ps{s}", [P, 512]) for s in range(2)]
    tiles = lambda c: bass.ds(c * QT, QT)
    if K == 2:
        turned, gt_ready, prod_ps, read, act_in, act_out, msg_ready, worked = (
            st.pair(x) for x in ("turned", "gt_ready", "prod_ps", "prod_read", "act_in", "act_out", "msg_ready", "worked"))
        GT = [st.sb(f"GT{s}", [P, QT * P]) for s in range(2)]
        msg = [st.sb(f"msg{s}", [P, QT, D]) for s in range(2)]
        gt_ps = st.ps("gt_ps", [P, 512])
        g_free = turned
    else:
        msg, g_free = G, merged_ps
    if kind == "attention":
        scored = st.pair("scored")
        ea_loaded, et_ready = st.pair("ea_loaded"), st.pair("et_ready")
        ea = [st.sb(f"ea{s}", [P, QT, D]) for s in range(2)]
        ET = [st.sb(f"ET{s}", [P, 2 * P]) for s in range(2)]
        et_ps, e_ps = st.ps("et_ps", [P, 512]), [st.ps(f"e_ps{x}", [P, 512]) for x in range(2)]
        kvq_ps = [st.ps(f"kvq_ps{x}", [P, 512]) for x in range(2)]
        kvq = [st.sb(f"kvq{s}", [P, QT, 3 * D]) for s in range(2)]
        ee = [st.sb(f"ee{s}", [P, QT, D]) for s in range(2)]
        score = [st.sb(f"score{s}", [P, QT * HEADS]) for s in range(2)]
        ex = [st.sb(f"ex{s}", [P, QT * HEADS]) for s in range(2)]
    if kind == "conv":
        diff_ready = st.pair("diff_ready")
        z_ps = st.ps("z_ps", [P, 512])
        z = [st.sb(f"z{s}", [P, QT, D]) for s in range(2)]
        sg = [st.sb(f"sg{s}", [P, QT, D]) for s in range(2)]

    with st.block() as block:
        @block.sync
        def _(sp):
            def attributes(i, s):
                wait(sp, turned[s], i)
                first = (2 * i + s) * QT
                if not isinstance(i, int):
                    sp.dma_start(ea[s][:, :, :], edge_attr[bass.ds(first * P, QT * P), :].rearrange("(t p) f -> p t f", p=P)).then_inc(ea_loaded[s], 16 * QT)
                else:
                    for k in range(QT):
                        n = min(N_EDGES - (first + k) * P, P)
                        at = (first + k) * P if n > 0 else 0
                        n = n if n > 0 else P
                        sp.dma_start(ea[s][0:n, k, :], edge_attr[at:at + n, :]).then_inc(ea_loaded[s], 16)

            def load(i, s):
                wait(sp, eq_ready[s], i)
                sp.dma_start(rows[s][:, :, :], rows_dram[tiles(2 * i + s), :].rearrange("(a t) e -> a t e", a=1).partition_broadcast(P)).then_inc(rows_loaded[s], 16)
                if kind == "attention":
                    attributes(i, s)

            def step(i):
                for s in range(2):
                    load(i, s)

            loop(sp, ESTEPS - 1, step)
            for s in range(2):
                load(ESTEPS - 1, s)

        @block.gpsimd
        def _(pool):
            def gather(i, s, k):
                if k == 0:
                    wait(pool, g_idx[s], i + 1)
                    wait(pool, g_free[s], i)
                    nc.gpsimd.sem_inc(admitted, 1)
                for g in range(K):
                    pool.indirect_dma_start(out=G[s][:, k, g * D:(g + 1) * D], out_offset=None, in_=h_table,
                                            in_offset=bass.IndirectOffsetOnAxis(ap=gi[s][g][:, k:k + 1], axis=0)).then_inc(gathered[g][s], 16)

            def scatter(i, s, k):
                if k == 0:
                    wait(pool, s_idx[s], i + 1)
                    wait(pool, merged_ready[s], i + 1)
                    wait(pool, scattered[1 - s], 16 * QT * (i + s))
                else:
                    wait(pool, scattered[s], 16 * (QT * i + k))
                nc.gpsimd.sem_inc(admitted, 1)
                pool.indirect_dma_start(out=base_table, out_offset=bass.IndirectOffsetOnAxis(ap=si[s][:, k:k + 1], axis=0),
                                        in_=merged[s][:, k, :], in_offset=None, compute_op=ALU.add).then_inc(scattered[s], 16)

            for k in range(QT):
                gather(0, 0, k)
            def step(i):
                for s in range(2):
                    gather(i + s, 1 - s, 0)
                    gather(i + s, 1 - s, 1)
                    for k in range(QT):
                        if k + 2 < QT:
                            gather(i + s, 1 - s, k + 2)
                        scatter(i, s, k)

            loop(pool, ESTEPS, step)
            for s in range(2):
                pool.wait_ge(scattered[s], 16 * QT * ESTEPS)
            for g in range(K):
                pool.wait_ge(gathered[g][0], 16 * QT * (ESTEPS + 1))

        @block.scalar
        def _(act):
            def gather_columns(i, s):
                wait(act, g_free[s], i)
                for g, name in enumerate(gather_cols):
                    last = nc.scalar.copy(gi[s][g][:, :], C[name + "_i"][:, tiles(2 * i + s)])
                    last.then_inc(g_idx[s], 1) if g == K - 1 else None

            def scatter_columns(i, s):
                wait(act, scattered[s], 16 * QT * i)
                nc.scalar.copy(si[s][:, :], C["scatter_" + target][:, tiles(2 * i + s)]).then_inc(s_idx[s], 1)

            def turned_rows(i, s):
                wait(act, turned[s], i + 1)
                wait(act, prod_ps[s], i)
                nc.scalar.copy(GT[s][:, :], gt_ps[:, :]).then_inc(gt_ready[s], 1)
                if kind == "attention":
                    nc.scalar.copy(ET[s][:, :], et_ps[:, 0:2 * P]).then_inc(et_ready[s], 1)

            gather_columns(0, 0)
            def step(i):
                for s in range(2):
                    gather_columns(i + s, 1 - s)
                    scatter_columns(i, s)
                    if K == 2:
                        turned_rows(i, s)
                        wait(act, act_in[s], i + 1)
                    if kind == "attention":
                        nc.scalar.activation(ex[s][:, :], score[s][:, :], ACT.Exp).then_inc(act_out[s], 1)
                    if kind == "conv":
                        nc.scalar.activation(sg[s][:, :, :], z[s][:, :, :], ACT.Sigmoid).then_inc(act_out[s], 1)

            loop(act, ESTEPS, step)

        @block.tensor
        def _(pe):
            def merge(i, s):
                wait(pe, eq_ready[s], i + 1)
                wait(pe, merged_ready[s], i)
                if K == 2:
                    wait(pe, msg_ready[s], i + 1)
                else:
                    wait(pe, gathered[0][s], 16 * QT * (i + 1))
                for k in range(QT):
                    last = nc.tensor.matmul(m_ps[s][:, k * D:(k + 1) * D], eq[s][:, k, :], msg[s][:, k, :], start=True, stop=True)
                last.then_inc(merged_ps[s], 1)

            def turn(i, s):
                wait(pe, gt_ready[1 - s], i + s)
                if kind == "attention":
                    for g in range(K):
                        wait(pe, gathered[g][s], 16 * QT * (i + 1))
                    wait(pe, ea_loaded[s], 16 * QT * (i + 1))
                    wait(pe, et_ready[1 - s], i + s)
                    for k in range(QT // 2):
                        two = ea[s][:, 2 * k:2 * k + 2, :].rearrange("p t f -> p (t f)")
                        nc.tensor.transpose(et_ps[:, k * P:(k + 1) * P], two, C["iden"][:, :])
                else:
                    wait(pe, diff_ready[s], i + 1)
                for k in range(QT):
                    last = nc.tensor.transpose(gt_ps[:, k * P:(k + 1) * P], G[s][:, k, :], C["iden"][:, :])
                last.then_inc(turned[s], 1)

            def products(i, s):
                wait(pe, gt_ready[s], i + 1)
                wait(pe, read[1 - s], i + s)
                if kind == "attention":
                    wait(pe, et_ready[s], i + 1)
                    for k in range(QT):
                        half = slice((k % 2) * D, (k % 2 + 1) * D)
                        nc.tensor.matmul(kvq_ps[k // 2][:, (k % 2) * 3 * D:(k % 2 + 1) * 3 * D], GT[s][:, k * P:(k + 1) * P], C["kvq"][:, :], start=True, stop=True)
                        last = nc.tensor.matmul(e_ps[k % 2][:, (k // 2) * D:(k // 2 + 1) * D], ET[s][half, (k // 2) * P:(k // 2 + 1) * P], C["we"][half, :], start=True, stop=True)
                else:
                    for k in range(QT):
                        last = nc.tensor.matmul(z_ps[:, k * D:(k + 1) * D], GT[s][:, k * P:(k + 1) * P], C["w3"][:, :], start=True, stop=True)
                last.then_inc(prod_ps[s], 1)

            def step(i):
                for s in range(2):
                    if K == 2:
                        turn(i, s)
                        products(i, s)
                    merge(i, s)

            loop(pe, ESTEPS, step)

        @block.vector
        def _(dve):
            def equal(i, s):
                wait(dve, rows_loaded[s], 16 * i + 16)
                wait(dve, merged_ps[s], i)
                cols = C[target + "_f"][:, tiles(2 * i + s)].unsqueeze(2).to_broadcast([P, QT, P])
                nc.vector.tensor_tensor(eq[s][:, :, :], rows[s][:, :, :], cols, ALU.is_equal).then_inc(eq_ready[s], 1)

            def evict(i, s):
                wait(dve, merged_ps[s], i + 1)
                wait(dve, scattered[s], 16 * QT * i)
                nc.vector.tensor_copy(merged[s][:, :, :].rearrange("p t f -> p (t f)"), m_ps[s][:, 0:QT * D]).then_inc(merged_ready[s], 1)

            def attention(i, s):
                wait(dve, prod_ps[s], i + 1)
                bias = C["kvqe_b"]
                for x in range(2):
                    nc.vector.tensor_tensor(kvq[s][:, 2 * x:2 * x + 2, :], kvq_ps[x][:, 0:6 * D].rearrange("p (t f) -> p t f", t=2),
                                            bias[:, 0:3 * D].unsqueeze(1).to_broadcast([P, 2, 3 * D]), ALU.add)
                    last = nc.vector.tensor_tensor(ee[s][:, x:QT:2, :], e_ps[x][:, 0:2 * D].rearrange("p (t f) -> p t f", t=2),
                                                   bias[:, 3 * D:4 * D].unsqueeze(1).to_broadcast([P, 2, D]), ALU.add)
                last.then_inc(read[s], 1)
                wait(dve, read[s], i + 1)
                q = kvq[s][:, :, 2 * D:3 * D]
                nc.vector.tensor_tensor(q, kvq[s][:, :, 0:D], q, ALU.mult).then_inc(worked[s], 1)
                wait(dve, worked[s], 2 * i + 1)
                nc.vector.scalar_tensor_tensor(ee[s][:, :, :], q, float((D // HEADS) ** -0.5), ee[s][:, :, :], ALU.mult, ALU.mult).then_inc(worked[s], 1)
                wait(dve, worked[s], 2 * i + 2)
                nc.vector.tensor_reduce(score[s][:, :], ee[s][:, :, :].rearrange("p t (h d) -> p (t h) d", h=HEADS), AX.X, ALU.add).then_inc(scored[s], 1)
                wait(dve, scored[s], i + 1)
                nc.vector.tensor_scalar(score[s][:, :], score[s][:, :], -5.0, 5.0, ALU.max, ALU.min).then_inc(act_in[s], 1)
                wait(dve, act_out[s], i + 1)
                wait(dve, merged_ps[s], i)
                for k in range(QT):
                    last = nc.vector.tensor_tensor(msg[s][:, k, :].rearrange("p (h d) -> p h d", h=HEADS),
                                                   kvq[s][:, k, D:2 * D].rearrange("p (h d) -> p h d", h=HEADS),
                                                   ex[s][:, k * HEADS:(k + 1) * HEADS].unsqueeze(2).to_broadcast([P, HEADS, D // HEADS]), ALU.mult)
                last.then_inc(msg_ready[s], 1)

            def difference(i, s):
                for g in range(K):
                    wait(dve, gathered[g][s], 16 * QT * (i + 1))
                nc.vector.tensor_tensor(G[s][:, :, D:2 * D], G[s][:, :, D:2 * D], G[s][:, :, 0:D], ALU.subtract).then_inc(diff_ready[s], 1)

            def convolution(i, s):
                wait(dve, prod_ps[s], i + 1)
                row = lambda k: C["ec"][:, k * D:(k + 1) * D].unsqueeze(1).to_broadcast([P, QT, D])
                nc.vector.tensor_tensor(z[s][:, :, :], z_ps[:, 0:QT * D].rearrange("p (t f) -> p t f", t=QT), row(0), ALU.subtract).then_inc(read[s], 1)
                wait(dve, read[s], i + 1)
                nc.vector.tensor_tensor(z[s][:, :, :], z[s][:, :, :], row(1), ALU.mult).then_inc(worked[s], 1)
                wait(dve, worked[s], i + 1)
                nc.vector.tensor_tensor(z[s][:, :, :], z[s][:, :, :], row(2), ALU.add).then_inc(act_in[s], 1)
                wait(dve, act_out[s], i + 1)
                wait(dve, merged_ps[s], i)
                nc.vector.tensor_tensor(msg[s][:, :, :], z[s][:, :, :], sg[s][:, :, :], ALU.mult).then_inc(msg_ready[s], 1)

            def step(i):
                for s in range(2):
                    equal(i, s)
                    if kind == "attention":
                        attention(i, s)
                    if kind == "conv":
                        difference(i, s)
                        convolution(i, s)
                    evict(i, s)

            loop(dve, ESTEPS, step)


def build(nc, I, out, stop=None):
    ctx = ExitStack()
    with ctx:
        sb = lambda name, shape, dt=FP32: ctx.enter_context(nc.sbuf_tensor(name, shape, dt))
        table = lambda name: nc.dram_tensor(name, (ROWS, D), FP32, kind="Internal").ap()
        h_table, sum_table, x_table = table("h_table"), table("sum_table"), table("x_table")
        src_rows, dst_rows = (nc.dram_tensor(n, (COLS, P), INT32, kind="Internal").ap() for n in ("src_rows", "dst_rows"))
        C = {n: sb(n, [P, P]) for n in ("iden", "lower", "zeros")}
        C["ones"] = sb("ones", [P, 2])
        C["spare_i"], C["spare"] = sb("spare_i", [P, 1], INT32), sb("spare", [P, 1])
        for n in ("src", "dst"):
            C[n + "_f"], C[n + "_i"], C["scatter_" + n] = sb(n + "_f", [P, COLS]), sb(n + "_i", [P, COLS], INT32), sb("scatter_" + n, [P, COLS], INT32)
        C["w1"] = [sb(f"w1_{l}", [P, HID]) for l in range(3)]
        C["w2"] = [sb(f"w2_{l}", [HID, D]) for l in range(3)]
        C["b2"] = [sb(f"b2_{l}", [P, D]) for l in range(3)]
        C["bn"] = sb("bn", [P, 12])
        C["bn_scale"], C["bn_shift"] = sb("bn_scale", [P, 1]), sb("bn_shift", [P, 1])
        C["eps1"] = sb("eps1", [P, 4])
        C["we"], C["kvq"], C["kvqe_b"] = sb("we", [P, D]), sb("kvq", [P, 3 * D]), sb("kvqe_b", [P, 4 * D])
        C["w3"], C["ec"] = sb("w3", [P, D]), sb("ec", [P, 4 * D])
        eps = lambda k: C["eps1"][:, k:k + 1]

        names = (f"stage{n}" for n in range(99))

        def run(f, *a, **k):
            with Stage(nc, next(names)) as st:
                f(nc, st, *a, **k)

        run(setup, I, C, src_rows, dst_rows)
        run(duplicates, C, src_rows, "src")
        run(duplicates, C, dst_rows, "dst")
        run(layernorm, C, I["x"], h_table, x_table, eps(0), add_source=True)
        run(edges, C, "sum", h_table, x_table, dst_rows, ["src"], "dst")
        run(layernorm, C, x_table, h_table, sum_table, eps(1))
        for l in range(3):
            run(edges, C, "sum", h_table, sum_table, dst_rows, ["src"], "dst")
            run(batch_stats, C, sum_table, l)
            if l < 2:
                run(mlp, C, sum_table, l, h_table=h_table, base_table=sum_table, eps_col=eps(l + 2))
            else:
                run(mlp, C, sum_table, l, residual=x_table, out=out)
        run(layernorm, C, out, h_table)
        run(edges, C, "attention", h_table, out, dst_rows, ["src", "dst"], "dst", edge_attr=I["edge_attr_64"])
        run(layernorm, C, out, h_table)
        run(edges, C, "conv", h_table, out, src_rows, ["src", "dst"], "src")


_INS = ["x", "src", "dst", "edge_attr_64", "L0_gnn_eps", "L1_gnn_W1", "L1_gnn_b1", "L1_gnn_gamma", "L1_gnn_beta",
        "L1_gnn_W2", "L1_gnn_b2", "L1_gnn_eps", "L2_gnn_WQ", "L2_gnn_bQ", "L2_gnn_WK", "L2_gnn_bK", "L2_gnn_WE",
        "L2_gnn_bE", "L2_gnn_WV", "L2_gnn_bV", "L3_gnn_W", "L3_gnn_gamma", "L3_gnn_beta", "L3_gnn_running_mean",
        "L3_gnn_running_var"]


def kernel(**inputs):
    import numpy as _np
    import concourse.bacc as _bacc
    from concourse.bass_utils import run_bass_kernel_spmd as _run

    nc = _bacc.Bacc("TRN2", target_bir_lowering=False, num_devices=1)
    arrays, I = {}, {}
    for name in _INS:
        a = _np.ascontiguousarray(inputs[name])
        arrays[f"in_{name}"] = a
        I[name] = nc.dram_tensor(f"in_{name}", a.shape, mybir.dt.from_np(a.dtype), kind="ExternalInput").ap()
    out = nc.dram_tensor("out_nodes", (ROWS, D), FP32, kind="ExternalOutput").ap()
    build(nc, I, out)
    r = _run(nc, [arrays], core_ids=[0])
    return r.results[0]["out_nodes"][:N_NODES]
```

```python
import concourse.bass as bass
from concourse import mybir
from contextlib import ExitStack, contextmanager

FP32 = mybir.dt.float32
INT32 = mybir.dt.int32
BF16 = mybir.dt.bfloat16
FP16 = mybir.dt.float16
ALU = mybir.AluOpType
ACT = mybir.ActivationFunctionType
AX = mybir.AxisListType

P = 128
N_NODES, N_EDGES, D, HID, HEADS = 100000, 50000, 64, 128, 8
CH = 16
CHUNK = P * CH
STEPS = 25
CHUNKS = 2 * STEPS
ROWS = CHUNKS * CHUNK
CHW = CH * D
NODE_CHUNKS = N_NODES // CHUNK
NODE_PARTS = (N_NODES - NODE_CHUNKS * CHUNK) // CH
assert NODE_CHUNKS == CHUNKS - 2 and NODE_CHUNKS * CHUNK + NODE_PARTS * CH == N_NODES and ROWS - N_NODES >= P
TILES = -(-N_EDGES // P)
QT = 4
ESTEPS = -(-TILES // (2 * QT))
COLS = 400
assert COLS >= (ESTEPS * 2 + 1) * QT
NPP = 4
WIN = NPP * P
WPC = CHUNK // WIN
WINDOWS = CHUNKS * WPC
WT = 4
NODE_SPLIT = N_EDGES // 400
GROUP = 8
RING_GROUPS = 10
RT = RING_GROUPS * GROUP
assert GROUP * CHUNKS == COLS and WINDOWS % 4 == 0 and N_EDGES * CHUNK == N_NODES * GROUP * P
LN_EPS = 1e-5
BN_EPS = 1e-5


class Stage:

    def __init__(self, nc, name):
        self.nc, self.name, self.ctx, self.sems = nc, name, ExitStack(), []

    def __enter__(self):
        self.ctx.__enter__()
        return self

    def sem(self, name):
        self.sems.append(self.nc.alloc_semaphore(name=f"{self.name}_{name}"))
        return self.sems[-1]

    def pair(self, name):
        return [self.sem(f"{name}0"), self.sem(f"{name}1")]

    def sb(self, name, shape, dt=FP32):
        return self.ctx.enter_context(self.nc.sbuf_tensor(f"{self.name}_{name}", shape, dt))

    def ps(self, name, shape):
        return self.ctx.enter_context(self.nc.psum_tensor(f"{self.name}_{name}", shape, FP32))

    def block(self):
        return self.nc.Block()

    def __exit__(self, *a):
        self.ctx.__exit__(*a)
        if a[0] is None:
            self.nc.clear_and_free_semaphores(self.sems)
            self.nc.all_engine_barrier()


def wait(eng, sem, value):
    if not (isinstance(value, int) and value <= 0):
        eng.wait_ge(sem, value)


def loop(eng, steps, step, peel_last=False):
    step(0)
    with eng.Fori(1, steps - peel_last) as i:
        step(i)
    if peel_last:
        step(steps - 1)


def chunk(table, c):
    return table[bass.ds(c * CHUNK, CHUNK), :].rearrange("(p j) f -> p j f", p=P)


def flat_chunk(table, c):
    return table[bass.ds(c * CHUNK, CHUNK), :].rearrange("(p j) f -> p (j f)", p=P)


def setup(nc, st, I, C, src_rows, dst_rows):
    stage, loaded, built, turned = (st.sem(x) for x in ("stg_filled", "params_loaded", "consts_built", "turned"))
    rows_loaded, rows_stored, cols_ready = st.sem("rows_loaded"), st.sem("rows_stored"), st.sem("cols_ready")
    var_ready, std_ready, dve_done = st.sem("var_ready"), st.sem("std_ready"), st.sem("dve_done")
    NB = COLS // 4
    rows = [st.sb(f"idx_rows{k}", [NB, 4, P], INT32) for k in range(2)]
    rows_f = [st.sb(f"idx_rows_f{k}", [NB, 4, P]) for k in range(2)]
    cols_ps = [st.ps(f"cols_ps{k}", [P, 512]) for k in range(2)]
    w3 = st.sb("w3_rows", [D, 2 * D])
    w3_ps = st.ps("w3_ps", [P, 512])
    one_eps = st.sb("eps_raw", [P, 4])
    iden0 = st.sb("iden0", [P, P])
    row1 = lambda a: a.rearrange("(a n) -> a n", a=1)
    NLOAD = 0

    loads = [(w3[:, :], I["L3_gnn_W"])]
    for l in range(3):
        for half in range(2):
            loads.append((C["w1"][l][half * D:(half + 1) * D, :], I["L1_gnn_W1"][l, :, :]))
        loads.append((C["w2"][l][:, :], I["L1_gnn_W2"][l, :, :]))
        loads.append((C["b2"][l][:, :], I["L1_gnn_b2"][l:l + 1, :].partition_broadcast(P)))
        for k, name in enumerate(("b1", "gamma", "beta")):
            loads.append((C["bn"][:, 4 * l + k:4 * l + k + 1],
                          I["L1_gnn_" + name][l, :].rearrange("(p a) -> p a", a=1)))
    loads.append((one_eps[:, 0:1], row1(I["L0_gnn_eps"]).partition_broadcast(P)))
    loads.append((one_eps[:, 1:4], row1(I["L1_gnn_eps"]).partition_broadcast(P)))
    for half in range(2):
        loads.append((C["we"][half * D:(half + 1) * D, :], I["L2_gnn_WE"]))
    loads.append((C["kvq"][0:D, 0:D], I["L2_gnn_WK"]))
    loads.append((C["kvq"][0:D, D:2 * D], I["L2_gnn_WV"]))
    loads.append((C["kvq"][D:2 * D, 2 * D:3 * D], I["L2_gnn_WQ"]))
    for k, name in enumerate(("bK", "bV", "bQ", "bE")):
        loads.append((C["kvqe_b"][:, k * D:(k + 1) * D], row1(I["L2_gnn_" + name]).partition_broadcast(P)))
    for k, name in enumerate(("running_mean", "gamma", "beta", "running_var")):
        loads.append((C["ec"][:, k * D:(k + 1) * D], row1(I["L3_gnn_" + name]).partition_broadcast(P)))
    NL = len(loads)
    full = N_EDGES // P
    tail = N_EDGES - full * P

    with st.block() as block:
        @block.gpsimd
        def _(pool):
            for k in range(2):
                nc.gpsimd.iota(rows[k][:, :, :], pattern=[[0, 4], [1, P]], base=N_NODES,
                               channel_multiplier=0).then_inc(stage, 1)
            nc.gpsimd.iota(C["spare_i"][:, :], pattern=[[0, 1]], base=N_NODES, channel_multiplier=1).then_inc(stage, 1)
            nc.gpsimd.memset(iden0[:, :], 0.0).then_inc(stage, 1)
            nc.gpsimd.memset(C["lower"][:, :], 1.0).then_inc(stage, 1)
            nc.gpsimd.memset(C["zeros"][:, :], 0.0).then_inc(stage, 1)
            nc.gpsimd.memset(C["ones"][:, :], 1.0).then_inc(stage, 1)
            nc.gpsimd.memset(C["ones_sq"][:, :], 1.0).then_inc(stage, 1)
            nc.gpsimd.memset(C["kvq"][:, :], 0.0).then_inc(stage, 1)
            pool.wait_ge(stage, 9)
            nc.gpsimd.affine_select(out=C["iden"][:, :], in_=iden0[:, :], compare_op=ALU.not_equal, fill=1.0,
                                    base=0, pattern=[[-1, P]], channel_multiplier=1).then_inc(built, 1)
            nc.gpsimd.affine_select(out=C["lower"][:, :], in_=C["lower"][:, :], compare_op=ALU.is_gt, fill=0.0,
                                    base=0, pattern=[[-1, P]], channel_multiplier=1).then_inc(built, 1)

        @block.sync
        def _(sp):
            sp.wait_ge(stage, 9)
            for k, name in enumerate(("src", "dst")):
                whole = I[name][0:full * P].rearrange("(t e) -> t e", e=P)
                sp.dma_start(rows[k][:, 0:3, :], whole[0:3 * NB, :].rearrange("(b t) e -> t b e", b=3)).then_inc(rows_loaded, 16)
                sp.dma_start(rows[k][0:full - 3 * NB, 3, :], whole[3 * NB:full, :]).then_inc(rows_loaded, 16)
                sp.dma_start(rows[k][full - 3 * NB:full - 3 * NB + 1, 3, 0:tail], row1(I[name][full * P:N_EDGES])).then_inc(rows_loaded, 16)
            for to, of in loads:
                sp.dma_start(to, of).then_inc(loaded, 16)
            sp.wait_ge(rows_loaded, 96)
            for k, table in enumerate((src_rows, dst_rows)):
                sp.dma_start(table.rearrange("(b t) e -> t b e", b=4), rows[k][:, :, :]).then_inc(rows_stored, 16)
            sp.wait_ge(rows_stored, 32)
            sp.wait_ge(loaded, 16 * NL)

        @block.tensor
        def _(pe):
            pe.wait_ge(built, 2)
            for k in range(2):
                pe.wait_ge(cols_ready, k + 1)
                for b in range(4):
                    last = nc.tensor.transpose(cols_ps[k][:, b * NB:(b + 1) * NB], rows_f[k][:, b, :], C["iden"][0:NB, 0:NB])
                last.then_inc(turned, 1)
            pe.wait_ge(loaded, 16 * NL)
            nc.tensor.transpose(w3_ps[:, 0:D], w3[:, :], C["iden"][0:D, 0:D]).then_inc(turned, 1)

        @block.vector
        def _(dve):
            dve.wait_ge(rows_loaded, 96)
            for k in range(2):
                nc.vector.tensor_copy(rows_f[k][:, :, :], rows[k][:, :, :]).then_inc(cols_ready, 1)
            for k, name in enumerate(("src", "dst")):
                dve.wait_ge(turned, k + 1)
                nc.vector.tensor_copy(C[name + "_f"][:, :], cols_ps[k][:, 0:COLS])
                nc.vector.tensor_copy(C[name + "_i"][:, :], cols_ps[k][:, 0:COLS])
            dve.wait_ge(stage, 9)
            nc.vector.tensor_copy(C["spare"][:, :], C["spare_i"][:, :])
            dve.wait_ge(turned, 3)
            nc.vector.tensor_copy(C["w3"][:, :], w3_ps[:, 0:D])
            nc.vector.tensor_scalar(C["eps1"][:, :], one_eps[:, :], 1.0, None, ALU.add)
            var, gam = C["ec"][:, 3 * D:4 * D], C["ec"][:, D:2 * D]
            nc.vector.tensor_scalar(var, var, BN_EPS, None, ALU.add).then_inc(var_ready, 1)
            dve.wait_ge(std_ready, 1)
            nc.vector.reciprocal(var, var).then_inc(dve_done, 1)
            dve.wait_ge(dve_done, 1)
            nc.vector.tensor_tensor(gam, gam, var, ALU.mult)

        @block.scalar
        def _(act):
            act.wait_ge(var_ready, 1)
            nc.scalar.activation(C["ec"][:, 3 * D:4 * D], C["ec"][:, 3 * D:4 * D], ACT.Sqrt).then_inc(std_ready, 1)


def plan(nc, st, I, C, dst_rows):
    loaded, loaded2, laid, tail, summed, packed = (st.sem(x) for x in ("loaded", "loaded2", "laid", "tail", "summed", "packed"))
    rel_done = st.sem("rel_done")
    NB, W = COLS // 4, WINDOWS
    rows = st.sb("rows", [NB, 4, P], INT32)
    ends = st.sb("ends", [NB, 4, 2])
    a, b = st.sb("a", [NODE_SPLIT, COLS], INT32), st.sb("b", [NODE_SPLIT, COLS], INT32)
    a_gt_b = st.sb("a_gt_b", [P, COLS])
    bad = st.sb("bad", [P, 4])
    thr_i, thr = st.sb("thr_i", [P, W + 1], INT32), st.sb("thr", [P, W + 1])
    lo_i, hi_i = st.sb("lo_i", [P, W], INT32), st.sb("hi_i", [P, W], INT32)
    below = [st.sb(f"below{k}", [NB, W + 1]) for k in range(8)]
    full, begun = st.ps("full", [P, 512]), st.ps("begun", [P, 512])
    verdict = st.ps("verdict", [P, 512])
    f, t0, x, q, wrap = (st.sb(n, [P, W]) for n in ("f", "t0", "x", "q", "wrap"))
    t0_i = st.sb("t0_i", [1, W], INT32)
    off = st.sb("off", [P, W, WT])

    with st.block() as block:
        @block.sync
        def _(sp):
            sp.dma_start(rows[:, :, :], dst_rows.rearrange("(b t) e -> t b e", b=4)).then_inc(loaded, 16)
            sp.dma_start(a[:, :], I["dst"].rearrange("(p j) -> p j", j=COLS)).then_inc(loaded, 16)
            sp.dma_start(b[:, :], I["dst"].rearrange("(p j) -> p j", j=COLS)).then_inc(loaded, 16)
            sp.wait_ge(loaded, 48)
            n = NODE_SPLIT - 1
            sp.dma_start(b[0:n, :], I["dst"][1:1 + n * COLS].rearrange("(p j) -> p j", j=COLS)).then_inc(loaded2, 16)
            sp.dma_start(b[n:n + 1, 0:COLS - 1], I["dst"][1 + n * COLS:N_EDGES].rearrange("(p j) -> p j", p=1)).then_inc(loaded2, 16)
            sp.wait_ge(loaded2, 32)

        @block.gpsimd
        def _(pool):
            nc.gpsimd.iota(thr_i[:, :], pattern=[[WIN, W + 1]], base=0, channel_multiplier=0).then_inc(laid, 1)
            nc.gpsimd.iota(lo_i[:, :], pattern=[[GROUP, CHUNKS], [0, WPC]], base=-GROUP, channel_multiplier=0).then_inc(laid, 1)
            nc.gpsimd.iota(hi_i[:, :], pattern=[[GROUP, CHUNKS], [0, WPC]], base=2 * GROUP - WT, channel_multiplier=0).then_inc(laid, 1)
            nc.gpsimd.iota(C["place_i"][:, :], pattern=[[1, NPP], [NPP, P]], base=0, channel_multiplier=0).then_inc(laid, 1)

        @block.tensor
        def _(pe):
            pe.wait_ge(tail, 12)
            for k in range(8):
                ps = full if k < 4 else begun
                last = nc.tensor.matmul(ps[:, 0:W + 1], C["ones_sq"][0:NB, :], below[k][:, :], start=k % 4 == 0, stop=k % 4 == 3)
            last.then_inc(summed, 1)
            pe.wait_ge(packed, 1)
            nc.tensor.matmul(verdict[:, 0:4], C["ones_sq"][:, :], bad[:, :], start=True, stop=True).then_inc(summed, 1)

        @block.vector
        def _(dve):
            n = [0]

            def link(ins):
                n[0] += 1
                ins.then_inc(tail, 1)
                dve.wait_ge(tail, n[0])

            dve.wait_ge(laid, 4)
            link(nc.vector.tensor_scalar(thr[:, :], thr_i[:, :], float(N_NODES), None, ALU.min))
            link(nc.vector.tensor_copy(C["place"][:, :], C["place_i"][:, :]))
            dve.wait_ge(loaded, 48)
            link(nc.vector.tensor_copy(ends[:, :, 0:1], rows[:, :, 0:1]))
            link(nc.vector.tensor_copy(ends[:, :, 1:2], rows[:, :, P - 1:P]))
            for k in range(8):
                link(nc.vector.tensor_scalar(below[k][:, :], thr[0:NB, :], ends[:, k % 4, 1 - k // 4:2 - k // 4], None, ALU.is_gt))
            link(nc.vector.memset(bad[:, :], 0.0))
            dve.wait_ge(loaded2, 32)
            link(nc.vector.tensor_tensor(a_gt_b[0:NODE_SPLIT, :], a[:, :], b[:, :], ALU.is_gt))
            link(nc.vector.tensor_reduce(bad[0:NODE_SPLIT, 0:1], a_gt_b[0:NODE_SPLIT, :], AX.X, ALU.add))
            dve.wait_ge(summed, 1)
            link(nc.vector.tensor_copy(f[:, :], full[:, 0:W]))
            link(nc.vector.tensor_scalar(t0[:, :], lo_i[:, :], 0.0, None, ALU.max))
            link(nc.vector.tensor_tensor(t0[:, :], t0[:, :], f[:, :], ALU.max))
            link(nc.vector.tensor_scalar(x[:, :], hi_i[:, :], float(COLS - WT), None, ALU.min))
            link(nc.vector.tensor_tensor(t0[:, :], t0[:, :], x[:, :], ALU.min))
            link(nc.vector.tensor_tensor(x[:, :], t0[:, :], f[:, :], ALU.is_gt))
            link(nc.vector.tensor_reduce(bad[:, 1:2], x[:, :], AX.X, ALU.add))
            link(nc.vector.tensor_scalar(q[:, :], t0[:, :], float(WT), None, ALU.add))
            link(nc.vector.tensor_tensor(x[:, :], q[:, :], begun[:, 1:W + 1], ALU.is_lt))
            link(nc.vector.tensor_reduce(bad[:, 2:3], x[:, :], AX.X, ALU.add))
            nc.vector.engine_nop().then_inc(packed, 1)
            for i in range(WT):
                link(nc.vector.tensor_scalar(x[:, :], t0[:, :], float(i), None, ALU.add))
                link(nc.vector.memset(q[:, :], 0.0))
                for k in range(1, COLS // RT):
                    link(nc.vector.tensor_scalar(wrap[:, :], x[:, :], float(k * RT), float(RT), ALU.is_ge, ALU.mult))
                    link(nc.vector.tensor_tensor(q[:, :], q[:, :], wrap[:, :], ALU.add))
                link(nc.vector.tensor_tensor(x[:, :], x[:, :], q[:, :], ALU.subtract))
                link(nc.vector.tensor_copy(off[:, :, i:i + 1].rearrange("p w o -> p (w o)"), x[:, :]))
            link(nc.vector.tensor_copy(C["ring_off"][:, :], off[0:1, :, :].rearrange("p w o -> p (w o)")))
            link(nc.vector.tensor_copy(t0_i[:, :], t0[0:1, :]))
            dve.wait_ge(summed, 2)
            link(nc.vector.tensor_reduce(q[0:1, 0:1], verdict[0:1, 0:4], AX.X, ALU.add))
            link(nc.vector.tensor_copy(C["unfit"][:, :], q[0:1, 0:1]))

            def window_targets(w):
                _, firsts = nc.values_load_multi_w_load_instructions(t0_i[0:1, bass.ds(w, 4)], engines=[mybir.EngineType.DVE], min_val=0, max_val=COLS - WT,
                                                                           skip_runtime_bounds_check_because="clamped above")
                for k, first in enumerate(firsts):
                    last = nc.vector.tensor_copy(C["rel"][:, bass.ds((w + k) * WT, WT)], C["dst_f"][:, bass.ds(first, WT)])
                return last

            with dve.Fori(0, W // 4) as w4:
                window_targets(w4 * 4).then_inc(rel_done, 1)
            dve.wait_ge(rel_done, W // 4)
            rel = C["rel"][:, :].rearrange("p (w t) -> p w t", t=WT)
            nc.vector.tensor_tensor(rel, rel, thr_i[:, 0:W].unsqueeze(2).to_broadcast([P, W, WT]), ALU.subtract).then_inc(rel_done, 1)


def window_sum(nc, st, C, h_table, base_table):
    gathered, idx_ready = st.pair("gathered"), st.pair("idx_ready")
    hi_done, r_done, mid_done, lo_done = (st.pair(x) for x in ("hi_done", "r_done", "mid_done", "lo_done"))
    hot_ready, hot_used = st.pair("hot_ready"), st.pair("hot_used")
    base_loaded, t_ready, t_stored, rel_ready = (st.pair(x) for x in ("base_loaded", "t_ready", "t_stored", "rel_ready"))
    rel = [st.sb(f"rel{s}", [P, WPC * WT]) for s in range(2)]
    half_added = st.pair("half_added")
    admitted = st.sem("admitted")
    raw = [st.sb(f"raw{s}", [P, GROUP, D]) for s in range(2)]
    rest = [st.sb(f"rest{s}", [P, GROUP, D]) for s in range(2)]
    gi = [st.sb(f"gi{s}", [P, GROUP], INT32) for s in range(2)]
    ring_hm = st.sb("ring_high_middle", [P, RT, 2 * D], BF16)
    ring_l = st.sb("ring_low", [P, RT, D], BF16)
    HW = WPC // 2
    hot = [st.sb(f"hot{r}", [P, HW * WT, WIN], BF16) for r in range(2)]
    base = [st.sb(f"base{s}", [P, WPC, NPP * D]) for s in range(2)]
    agg = [st.ps(f"agg{s}", [P, WPC * NPP, 2 * D]) for s in range(2)]
    G1 = lambda i, s: (i + s, 1 - s)

    def windows(table, c):
        return table[bass.ds(c * CHUNK, CHUNK), :].rearrange("(w p k) f -> p w (k f)", w=WPC, k=NPP)

    def ring_part(i, s, part):
        tiles = bass.ds(((2 * i + s) % RING_GROUPS) * GROUP, GROUP)
        return ring_l[:, tiles, :] if part == 2 else ring_hm[:, tiles, part * D:(part + 1) * D]

    def pairs(eng, step):
        step(0, False)
        with eng.Fori(1, STEPS - 1) as i:
            step(i, False)
        step(STEPS - 1, True)

    with st.block() as block:
        @block.sync
        def _(sp):
            def load(i, s):
                wait(sp, t_stored[s], 16 * i)
                sp.dma_start(base[s][:, :, :], windows(base_table, 2 * i + s)).then_inc(base_loaded[s], 16)

            def step(i, last):
                for s in range(2):
                    wait(sp, t_ready[s], i + 1)
                    sp.dma_start(windows(base_table, 2 * i + s), base[s][:, :, :]).then_inc(t_stored[s], 16)
                    if not last:
                        load(i + 1, s)

            load(0, 0)
            load(0, 1)
            pairs(sp, step)
            for s in range(2):
                sp.wait_ge(t_stored[s], 16 * STEPS)

        @block.gpsimd
        def _(pool):
            def step(i, last):
                for s in range(2):
                    wait(pool, idx_ready[s], i + 1)
                    wait(pool, r_done[s], i)
                    nc.gpsimd.sem_inc(admitted, 1)
                    for k in range(GROUP):
                        pool.indirect_dma_start(out=raw[s][:, k, :], out_offset=None, in_=h_table,
                                                in_offset=bass.IndirectOffsetOnAxis(ap=gi[s][:, k:k + 1], axis=0)).then_inc(gathered[s], 16)

            pairs(pool, step)

        @block.scalar
        def _(act):
            def columns(i, s):
                wait(act, gathered[s], 16 * GROUP * i)
                nc.scalar.copy(gi[s][:, :], C["src_i"][:, bass.ds((2 * i + s) * GROUP, GROUP)]).then_inc(idx_ready[s], 1)

            def windows_of(i, s):
                wait(act, hot_ready[1], 2 * i + s - 1)
                nc.scalar.copy(rel[s][:, :], C["rel"][:, bass.ds((2 * i + s) * WPC * WT, WPC * WT)]).then_inc(rel_ready[s], 1)

            def split(i, s):
                wait(act, gathered[s], 16 * GROUP * (i + 1))
                wait(act, hot_used[1], 2 * i + s - 2)
                nc.scalar.copy(ring_part(i, s, 0), raw[s][:, :, :]).then_inc(hi_done[s], 1)
                wait(act, r_done[s], i + 1)
                nc.scalar.copy(ring_part(i, s, 1), rest[s][:, :, :]).then_inc(mid_done[s], 1)

            def step(i, last):
                for s in range(2):
                    if not last:
                        columns(i + 1, s)
                    if not (last and s):
                        split(*G1(i, s))
                        windows_of(*G1(i, s))

            columns(0, 0)
            columns(0, 1)
            split(0, 0)
            windows_of(0, 0)
            pairs(act, step)

        @block.vector
        def _(dve):
            def remainder(i, s):
                wait(dve, hi_done[s], i + 1)
                wait(dve, lo_done[s], i)
                nc.vector.tensor_tensor(rest[s][:, :, :], raw[s][:, :, :], ring_part(i, s, 0), ALU.subtract).then_inc(r_done[s], 1)

            def low(i, s):
                wait(dve, mid_done[s], i + 1)
                nc.vector.tensor_tensor(ring_part(i, s, 2), rest[s][:, :, :], ring_part(i, s, 1), ALU.subtract).then_inc(lo_done[s], 1)

            def one_hot(i, s, r):
                if r == 0:
                    wait(dve, rel_ready[s], i + 1)
                wait(dve, hot_used[r], 2 * i + s)
                for k in range(HW * WT):
                    last = nc.vector.tensor_scalar(hot[r][:, k, :], C["place"][:, :], rel[s][:, r * HW * WT + k:r * HW * WT + k + 1], None, ALU.is_equal)
                last.then_inc(hot_ready[r], 1)

            def combine(i, s):
                wait(dve, base_loaded[s], 16 * (i + 1))
                wait(dve, hot_used[1], 2 * i + s + 1)
                total = base[s][:, :, :].rearrange("p w (k f) -> p (w k) f", f=D)
                nc.vector.tensor_tensor(total, total, agg[s][:, :, 0:D], ALU.add).then_inc(half_added[s], 1)
                wait(dve, half_added[s], i + 1)
                nc.vector.tensor_tensor(total, total, agg[s][:, :, D:2 * D], ALU.add).then_inc(t_ready[s], 1)

            def step(i, last):
                for s in range(2):
                    if not (last and s):
                        remainder(*G1(i, s))
                    one_hot(i, s, 0)
                    if not (last and s):
                        low(*G1(i, s))
                    one_hot(i, s, 1)
                    if s or not (isinstance(i, int) and i == 0):
                        combine(i - 1 + s, 1 - s)

            remainder(0, 0)
            low(0, 0)
            pairs(dve, step)
            combine(STEPS - 1, 1)

        @block.tensor
        def _(pe):
            def step(i, last):
                for s in range(2):
                    if not (last and s):
                        wait(pe, lo_done[1 - s], i + s + 1)
                    wait(pe, t_ready[s], i)
                    for r in range(2):
                        wait(pe, hot_ready[r], 2 * i + s + 1)
                        for j in range(HW):
                            w = (2 * i + s) * WPC + r * HW + j
                            _, at = nc.values_load_multi_w_load_instructions(
                                C["ring_off"][0:1, bass.ds(w * WT, WT)], engines=[mybir.EngineType.PE], min_val=0, max_val=RT - 1,
                                skip_runtime_bounds_check_because="the plan takes them modulo the ring")
                            for k in range(NPP):
                                to = agg[s][:, (r * HW + j) * NPP + k, :]
                                for t in range(WT):
                                    ones = hot[r][:, j * WT + t, k * P:(k + 1) * P]
                                    nc.tensor.matmul(to, ones, ring_hm[:, bass.ds(at[t], 1), :], start=t == 0, stop=False)
                                    mm = nc.tensor.matmul(to[:, D:2 * D], ones, ring_l[:, bass.ds(at[t], 1), :], start=False, stop=t == WT - 1)
                        mm.then_inc(hot_used[r], 1)

            pairs(pe, step)


def duplicates(nc, st, C, rows_dram, name):
    loaded, equal, masked, counted, used = (st.pair(x) for x in ("rows_loaded", "equal", "masked", "counted", "rows_used"))
    done = st.sem("scatter_cols")
    rows = [st.sb(f"row_bc{s}", [P, QT, P], INT32) for s in range(2)]
    eq = [st.sb(f"eq{s}", [P, QT, P]) for s in range(2)]
    count = st.sb("count", [P, COLS])
    dist = st.sb("dist", [P, COLS])

    with st.block() as block:
        @block.sync
        def _(sp):
            def step(i):
                for s in range(2):
                    wait(sp, used[s], i)
                    sp.dma_start(rows[s][:, :, :], rows_dram[bass.ds((2 * i + s) * QT, QT), :].rearrange("(a t) e -> a t e", a=1).partition_broadcast(P)).then_inc(loaded[s], 16)

            loop(sp, COLS // QT // 2, step)

        @block.vector
        def _(dve):
            def step(i):
                for s in range(2):
                    cols = C[name + "_f"][:, bass.ds((2 * i + s) * QT, QT)].unsqueeze(2).to_broadcast([P, QT, P])
                    wait(dve, loaded[s], 16 * i + 16)
                    wait(dve, counted[s], i)
                    nc.vector.tensor_tensor(eq[s][:, :, :], rows[s][:, :, :], cols, ALU.is_equal).then_inc(used[s], 1)
                for s in range(2):
                    wait(dve, used[s], i + 1)
                    nc.vector.tensor_tensor(eq[s][:, :, :], eq[s][:, :, :], C["lower"][:, :].unsqueeze(1).to_broadcast([P, QT, P]), ALU.mult).then_inc(masked[s], 1)
                for s in range(2):
                    wait(dve, masked[s], i + 1)
                    nc.vector.tensor_reduce(count[:, bass.ds((2 * i + s) * QT, QT)], eq[s][:, :, :], AX.X, ALU.add).then_inc(counted[s], 1)

            loop(dve, COLS // QT // 2, step)
            for s in range(2):
                dve.wait_ge(counted[s], COLS // QT // 2)
            nc.vector.tensor_scalar(count[:, :], count[:, :], 0.0, None, ALU.is_gt).then_inc(done, 1)
            nc.vector.tensor_scalar(dist[:, :], C[name + "_f"][:, :], -1.0, C["spare"][:, 0:1], ALU.mult, ALU.add).then_inc(done, 1)
            dve.wait_ge(done, 2)
            nc.vector.tensor_tensor(dist[:, :], dist[:, :], count[:, :], ALU.mult).then_inc(done, 1)
            dve.wait_ge(done, 3)
            nc.vector.tensor_tensor(C["scatter_" + name][:, :], dist[:, :], C[name + "_f"][:, :], ALU.add)


def layernorm(nc, st, C, source, h_table, base_table=None, eps_col=None, add_source=False):
    loaded, used, summed, mean_ready, centred, squared, ssum, var_ready, std_ready, rstd_ready, h_ready, base_ready, h_stored, base_stored = (
        st.pair(x) for x in ("x_loaded", "x_used", "summed", "mean_ready", "centred", "squared", "ssum", "var_ready",
                             "std_ready", "rstd_ready", "h_ready", "base_ready", "h_stored", "base_stored"))
    x = [st.sb(f"x{s}", [P, CH, D]) for s in range(2)]
    xc = [st.sb(f"xc{s}", [P, CH, D]) for s in range(2)]
    sq = [st.sb(f"sq{s}", [P, CH, D]) for s in range(2)]
    h = [st.sb(f"h{s}", [P, CH, D]) for s in range(2)]
    base = [st.sb(f"base{s}", [P, CH, D]) for s in range(2)]
    s1, mean, s2, var, rstd = ([st.sb(f"{x}{s}", [P, CH]) for s in range(2)] for x in ("s1", "mean", "s2", "var", "rstd"))
    padded = source.shape[0] == ROWS
    wide = lambda t: t[:, :].unsqueeze(2).to_broadcast([P, CH, D])

    with st.block() as block:
        @block.sync
        def _(sp):
            def step(i):
                for s in range(2):
                    wait(sp, used[s], i)
                    c = 2 * i + s
                    if padded or not isinstance(i, int) or c < NODE_CHUNKS:
                        sp.dma_start(x[s][:, :, :], chunk(source, c)).then_inc(loaded[s], 16)
                    elif c == NODE_CHUNKS:
                        rows = source[c * CHUNK:N_NODES, :].rearrange("(p j) f -> p j f", j=CH)
                        sp.dma_start(x[s][0:NODE_PARTS, :, :], rows).then_inc(loaded[s], 16)
                    else:
                        sp.dma_start(x[s][:, :, :], chunk(source, s)).then_inc(loaded[s], 16)

            loop(sp, STEPS, step, peel_last=True)

        @block.vector
        def _(dve):
            def step(i):
                for s in range(2):
                    wait(dve, loaded[s], 16 * i + 16)
                    wait(dve, h_ready[s], i)
                    nc.vector.tensor_reduce(s1[s][:, :], x[s][:, :, :], AX.X, ALU.add).then_inc(summed[s], 1)
                    wait(dve, summed[s], i + 1)
                    nc.vector.tensor_scalar(mean[s][:, :], s1[s][:, :], 1.0 / D, None, ALU.mult).then_inc(mean_ready[s], 1)
                    wait(dve, mean_ready[s], i + 1)
                    last = nc.vector.tensor_tensor(xc[s][:, :, :], x[s][:, :, :], wide(mean[s]), ALU.subtract)
                    last.then_inc(centred[s], 1)
                    if not add_source:
                        wait(dve, centred[s], i + 1)
                        nc.vector.sem_inc(used[s], 1)
                for s in range(2):
                    wait(dve, squared[s], i + 1)
                    nc.vector.tensor_reduce(s2[s][:, :], sq[s][:, :, :], AX.X, ALU.add).then_inc(ssum[s], 1)
                    wait(dve, ssum[s], i + 1)
                    nc.vector.tensor_scalar(var[s][:, :], s2[s][:, :], 1.0 / D, LN_EPS, ALU.mult, ALU.add).then_inc(var_ready[s], 1)
                for s in range(2):
                    wait(dve, std_ready[s], i + 1)
                    nc.vector.reciprocal(rstd[s][:, :], var[s][:, :]).then_inc(rstd_ready[s], 1)
                    wait(dve, rstd_ready[s], i + 1)
                    wait(dve, h_stored[s], 16 * i)
                    nc.vector.scalar_tensor_tensor(h[s][:, :, :], xc[s][:, :, :], 0.0, wide(rstd[s]), ALU.max, ALU.mult).then_inc(h_ready[s], 1)
                    if add_source:
                        wait(dve, h_ready[s], i + 1)
                        wait(dve, base_stored[s], 16 * i)
                        nc.vector.scalar_tensor_tensor(base[s][:, :, :], h[s][:, :, :], eps_col, x[s][:, :, :], ALU.mult, ALU.add).then_inc(base_ready[s], 1)
                        wait(dve, base_ready[s], i + 1)
                        nc.vector.sem_inc(used[s], 1)

            loop(dve, STEPS, step)

        @block.scalar
        def _(act):
            def step(i):
                for s in range(2):
                    wait(act, centred[s], i + 1)
                    nc.scalar.activation(sq[s][:, :, :], xc[s][:, :, :], ACT.Square).then_inc(squared[s], 1)
                for s in range(2):
                    wait(act, var_ready[s], i + 1)
                    nc.scalar.activation(var[s][:, :], var[s][:, :], ACT.Sqrt).then_inc(std_ready[s], 1)
                for s in range(2):
                    wait(act, h_ready[s], i + 1)
                    act.dma_start(chunk(h_table, 2 * i + s), h[s][:, :, :]).then_inc(h_stored[s], 16)
                    if base_table is not None:
                        if not add_source:
                            wait(act, base_stored[s], 16 * i)
                            nc.scalar.activation(base[s][:, :, :], h[s][:, :, :], ACT.Copy, scale=eps_col).then_inc(base_ready[s], 1)
                        wait(act, base_ready[s], i + 1)
                        act.dma_start(chunk(base_table, 2 * i + s), base[s][:, :, :]).then_inc(base_stored[s], 16)

            loop(act, STEPS, step)
            for s in range(2):
                act.wait_ge(h_stored[s], 16 * STEPS)
                if base_table is not None:
                    act.wait_ge(base_stored[s], 16 * STEPS)


def batch_stats(nc, st, C, table, l):
    loaded, used = st.pair("t_loaded"), st.pair("t_used")
    added, summed, tail = st.pair("added"), st.sem("summed"), st.sem("tail")
    zeroed, mm, std_ready = st.sem("zeroed"), st.sem("mm"), st.sem("std_ready")
    t = [st.sb(f"t{s}", [P, CHW]) for s in range(2)]
    acc = [st.sb(f"acc{s}", [P, CHW]) for s in range(2)]
    gram_sb = st.sb("gram_sb", [P, P])
    sum_sb = st.sb("sum_sb", [P, 1])
    prod = st.sb("prod", [P, HID])
    cols = st.sb("cols", [P, 8])
    gram, tsum, wg, moments = (st.ps(x, [P, 512]) for x in ("gram", "tsum", "wg", "moments"))
    bn, w1 = C["bn"], C["w1"][l]
    PAIR = 2 * D
    SUMS = [STEPS, STEPS - 1]

    with st.block() as block:
        @block.sync
        def _(sp):
            def step(i):
                for s in range(2):
                    wait(sp, used[s], i)
                    wait(sp, added[s], i)
                    sp.dma_start(t[s][:, :], flat_chunk(table, 2 * i + s)).then_inc(loaded[s], 16)

            loop(sp, STEPS, step)

        @block.tensor
        def _(pe):
            nc.tensor.matmul(gram[:, 0:P], C["zeros"][:, :], C["zeros"][:, :], start=True, stop=False)
            def step(i):
                for s in range(2):
                    wait(pe, loaded[s], 16 * i + 16)
                    c = 2 * i + s
                    n = P if not isinstance(i, int) or c < NODE_CHUNKS else NODE_PARTS if c == NODE_CHUNKS else 0
                    for q in range(CH // 2) if n else ():
                        two = t[s][0:n, q * PAIR:(q + 1) * PAIR]
                        last = nc.tensor.matmul(gram[:, 0:P], two, two, start=False, stop=False)
                    if n:
                        last.then_inc(used[s], 1)

            loop(pe, STEPS, step, peel_last=True)
            nc.tensor.matmul(gram[:, 0:P], C["zeros"][:, :], C["zeros"][:, :], start=False, stop=True)
            for s in range(2):
                pe.wait_ge(added[s], SUMS[s])
                for q in range(CH // 2):
                    last = nc.tensor.matmul(tsum[:, 0:1], acc[s][:, q * PAIR:(q + 1) * PAIR], C["ones"][:, 0:1], start=s == q == 0, stop=s == 1 and q == CH // 2 - 1)
            last.then_inc(summed, 1)
            pe.wait_ge(tail, 2)
            nc.tensor.matmul(wg[:, 0:HID], gram_sb[:, :], w1[:, :], start=True, stop=True)
            nc.tensor.matmul(moments[:, 0:1], w1[:, :], sum_sb[:, :], start=True, stop=True).then_inc(mm, 1)
            pe.wait_ge(tail, 3)
            nc.tensor.matmul(wg[:, HID:HID + 1], prod[:, :], C["ones"][:, 0:1], start=True, stop=True).then_inc(mm, 1)

        @block.vector
        def _(dve):
            n = [0]

            def link(ins):
                n[0] += 1
                ins.then_inc(tail, 1)
                dve.wait_ge(tail, n[0])

            for s in range(2):
                nc.vector.memset(acc[s][:, :], 0.0).then_inc(zeroed, 1)
            dve.wait_ge(zeroed, 2)

            def step(i):
                for s in range(2):
                    c = 2 * i + s
                    n = P if not isinstance(i, int) or c < NODE_CHUNKS else NODE_PARTS if c == NODE_CHUNKS else 0
                    if n:
                        wait(dve, loaded[s], 16 * i + 16)
                        wait(dve, added[s], i)
                        nc.vector.tensor_tensor(acc[s][0:n, :], acc[s][0:n, :], t[s][0:n, :], ALU.add).then_inc(added[s], 1)

            loop(dve, STEPS, step, peel_last=True)
            nc.vector.memset(gram_sb[:, :], 0.0).then_inc(mm, 1)
            dve.wait_ge(mm, 1)
            dve.wait_ge(summed, 1)
            nc.vector.tensor_copy(gram_sb[0:D, 0:D], gram[0:D, 0:D])
            link(nc.vector.tensor_copy(gram_sb[D:P, D:P], gram[D:P, D:P]))
            link(nc.vector.tensor_copy(sum_sb[:, :], tsum[:, 0:1]))
            dve.wait_ge(mm, 2)
            link(nc.vector.tensor_tensor(prod[:, :], wg[:, 0:HID], w1[:, :], ALU.mult))
            dve.wait_ge(mm, 3)
            c = lambda k: cols[:, k:k + 1]
            link(nc.vector.tensor_scalar(c(0), moments[:, 0:1], 1.0 / N_NODES, None, ALU.mult))
            link(nc.vector.tensor_scalar(c(1), wg[:, HID:HID + 1], 1.0 / N_NODES, None, ALU.mult))
            link(nc.vector.tensor_tensor(c(2), c(0), c(0), ALU.mult))
            link(nc.vector.tensor_tensor(c(2), c(1), c(2), ALU.subtract))
            link(nc.vector.tensor_scalar(c(2), c(2), 0.0, BN_EPS, ALU.max, ALU.add))
            dve.wait_ge(std_ready, 1)
            link(nc.vector.reciprocal(c(2), c(2)))
            link(nc.vector.tensor_tensor(C["bn_scale"][:, :], c(2), bn[:, 4 * l + 1:4 * l + 2], ALU.mult))
            link(nc.vector.tensor_tensor(c(4), c(0), bn[:, 4 * l:4 * l + 1], ALU.add))
            link(nc.vector.tensor_tensor(c(5), bn[:, 4 * l:4 * l + 1], c(4), ALU.subtract))
            link(nc.vector.tensor_tensor(c(6), c(5), C["bn_scale"][:, :], ALU.mult))
            link(nc.vector.tensor_tensor(C["bn_shift"][:, :], c(6), bn[:, 4 * l + 2:4 * l + 3], ALU.add))

        @block.scalar
        def _(act):
            act.wait_ge(tail, 8)
            nc.scalar.activation(cols[:, 2:3], cols[:, 2:3], ACT.Sqrt).then_inc(std_ready, 1)


def mlp(nc, st, C, table, l, h_table=None, base_table=None, eps_col=None, residual=None, out=None):
    final = out is not None
    loaded, t_used = st.pair("t_loaded"), st.pair("t_used")
    x_loaded, x_used = st.pair("x_loaded"), st.pair("x_used")
    y_stored, b_stored, y_ready, b_ready = st.pair("y_stored"), st.pair("b_stored"), st.pair("y_ready"), st.pair("b_ready")
    units = lambda n: [[st.sem(f"{n}{s}{r}") for r in range(2)] for s in range(2)]
    turned, tt_ready, hid_ps_ready, hid_ready, y_ps_ready, y_done = (
        units(n) for n in ("turned", "tt_ready", "hid_ps_ready", "hid_ready", "y_ps_ready", "y_done"))
    t = [st.sb(f"t{s}", [P, CHW]) for s in range(2)]
    y = [st.sb(f"y{s}", [P, CHW]) for s in range(2)]
    b = [st.sb(f"b{s}", [P, CHW]) for s in range(2)]
    tt = [st.sb(f"tt{r}", [P, 512]) for r in range(2)]
    hid = [[st.sb(f"hid{r}{e}", [P, 512]) for e in range(2)] for r in range(2)]
    t_ps = [st.ps(f"t_ps{r}", [P, 512]) for r in range(2)]
    hid_ps = [[st.ps(f"hid_ps{r}{e}", [P, 512]) for e in range(2)] for r in range(2)]
    y_ps = [st.ps(f"y_ps{r}", [P, 512]) for r in range(2)]
    w1, w2, b2 = C["w1"][l], C["w2"][l], C["b2"][l]
    PAIR, HALF = 2 * D, CHW // 2
    UNITS = [(s, r) for s in range(2) for r in range(2)]

    with st.block() as block:
        @block.sync
        def _(sp):
            def step(i):
                for s in range(2):
                    wait(sp, t_used[s], 2 * i)
                    sp.dma_start(t[s][:, :], flat_chunk(table, 2 * i + s)).then_inc(loaded[s], 16)
                    if final:
                        wait(sp, y_stored[s], 16 * i)
                        sp.dma_start(b[s][:, :], flat_chunk(residual, 2 * i + s)).then_inc(x_loaded[s], 16)

            loop(sp, STEPS, step)

        @block.tensor
        def _(pe):
            def turn(i, s, r):
                wait(pe, loaded[s], 16 * i + 16)
                wait(pe, tt_ready[1 - s][r], i + s)
                for q in range(4):
                    lo = r * HALF + q * PAIR
                    last = nc.tensor.transpose(t_ps[r][:, q * P:(q + 1) * P], t[s][:, lo:lo + PAIR], C["iden"][:, :])
                last.then_inc(turned[s][r], 1)

            def hidden(i, s, r):
                wait(pe, tt_ready[s][r], i + 1)
                wait(pe, hid_ready[1 - s][r], i + s)
                for e in range(2):
                    last = nc.tensor.matmul(hid_ps[r][e][:, :], w1[e * D:(e + 1) * D, :], tt[r][e * D:(e + 1) * D, :], start=True, stop=True)
                last.then_inc(hid_ps_ready[s][r], 1)

            def output(i, s, r):
                wait(pe, hid_ready[s][r], i + 1)
                wait(pe, y_done[1 - s][r], i + s)
                for q in range(4):
                    for e in range(2):
                        k = 2 * q + e
                        last = nc.tensor.matmul(y_ps[r][:, k * D:(k + 1) * D], hid[r][e][:, q * P:(q + 1) * P], w2[:, :], start=True, stop=True)
                last.then_inc(y_ps_ready[s][r], 1)

            def step(i, first, last):
                for k, (s, r) in enumerate(UNITS):
                    if k < 3:
                        turn(i, *UNITS[k + 1])
                    elif not last:
                        turn(i + 1, *UNITS[0])
                    hidden(i, s, r)
                    if k:
                        output(i, *UNITS[k - 1])
                    elif not first:
                        output(i - 1, *UNITS[3])

            turn(0, *UNITS[0])
            step(0, True, False)
            with pe.Fori(1, STEPS - 1) as i:
                step(i, False, False)
            step(STEPS - 1, False, True)
            output(STEPS - 1, *UNITS[3])

        @block.scalar
        def _(act):
            def relu(i, s, r):
                wait(act, hid_ps_ready[s][r], i + 1)
                wait(act, y_ps_ready[1 - s][r], i + s)
                for e in range(2):
                    last = nc.scalar.activation(hid[r][e][:, :], hid_ps[r][e][:, :], ACT.Relu, bias=C["bn_shift"][:, 0:1], scale=C["bn_scale"][:, 0:1])
                last.then_inc(hid_ready[s][r], 1)

            def step(i):
                for s, r in UNITS:
                    relu(i, s, r)

            loop(act, STEPS, step)

        @block.vector
        def _(dve):
            def evict(i, s, r):
                wait(dve, turned[s][r], i + 1)
                wait(dve, hid_ps_ready[1 - s][r], i + s)
                nc.vector.tensor_copy(tt[r][:, :], t_ps[r][:, :]).then_inc(tt_ready[s][r], 1)
                wait(dve, tt_ready[s][r], i + 1)
                nc.vector.sem_inc(t_used[s], 1)

            def finish(i, s, r):
                wait(dve, y_ps_ready[s][r], i + 1)
                half = slice(r * HALF, (r + 1) * HALF)
                if final:
                    wait(dve, x_loaded[s], 16 * i + 16)
                elif r == 0:
                    wait(dve, b_stored[s], 16 * i)
                if r == 0:
                    wait(dve, y_stored[s], 16 * i)
                yh = y[s][:, half]
                nc.vector.tensor_tensor(yh.rearrange("p (k f) -> p k f", f=D), y_ps[r][:, :].rearrange("p (k f) -> p k f", f=D),
                                        b2[:, :].unsqueeze(1).to_broadcast([P, 8, D]), ALU.add).then_inc(y_done[s][r], 1)
                if final:
                    wait(dve, y_done[s][r], i + 1)
                    nc.vector.tensor_tensor(b[s][:, half], yh, b[s][:, half], ALU.add).then_inc(b_ready[s], 1)
                else:
                    wait(dve, y_done[s][r], i + 1)
                    nc.vector.tensor_scalar(b[s][:, half], yh, eps_col, None, ALU.mult).then_inc(b_ready[s], 1)

            def step(i, first, last):
                for k, (s, r) in enumerate(UNITS):
                    if k < 3:
                        evict(i, *UNITS[k + 1])
                    elif not last:
                        evict(i + 1, *UNITS[0])
                    if k:
                        finish(i, *UNITS[k - 1])
                    elif not first:
                        finish(i - 1, *UNITS[3])

            evict(0, *UNITS[0])
            step(0, True, False)
            with dve.Fori(1, STEPS - 1) as i:
                step(i, False, False)
            step(STEPS - 1, False, True)
            finish(STEPS - 1, *UNITS[3])

        @block.gpsimd
        def _(pool):
            def step(i):
                for s in range(2):
                    wait(pool, b_ready[s], 2 * i + 2)
                    if final:
                        pool.dma_start(flat_chunk(out, 2 * i + s), b[s][:, :]).then_inc(y_stored[s], 16)
                    else:
                        pool.dma_start(flat_chunk(h_table, 2 * i + s), y[s][:, :]).then_inc(y_stored[s], 16)
                        pool.dma_start(flat_chunk(base_table, 2 * i + s), b[s][:, :]).then_inc(b_stored[s], 16)

            loop(pool, STEPS, step)
            for s in range(2):
                pool.wait_ge(y_stored[s], 16 * STEPS)
                if not final:
                    pool.wait_ge(b_stored[s], 16 * STEPS)


def edges(nc, st, C, kind, h_table, base_table, rows_dram, gather_cols, target, edge_attr=None):
    K = len(gather_cols)
    WIDE = K * D
    gathered = [st.pair(f"gathered_{name}") for name in gather_cols]
    admitted = st.sem("admitted")
    scattered, g_idx, s_idx = st.pair("scattered"), st.pair("gather_idx"), st.pair("scatter_idx")
    rows_loaded, eq_ready, merged_ps, merged_ready = (st.pair(x) for x in ("rows_loaded", "eq_ready", "merged_ps", "merged_ready"))
    rows = [st.sb(f"row_bc{s}", [P, QT, P], INT32) for s in range(2)]
    eq = [st.sb(f"eq{s}", [P, QT, P]) for s in range(2)]
    G = [st.sb(f"G{s}", [P, QT, WIDE]) for s in range(2)]
    gi = [[st.sb(f"gi{s}{g}", [P, QT], INT32) for g in range(K)] for s in range(2)]
    si = [st.sb(f"si{s}", [P, QT], INT32) for s in range(2)]
    merged = [st.sb(f"merged{s}", [P, QT, D]) for s in range(2)]
    m_ps = [st.ps(f"m_ps{s}", [P, 512]) for s in range(2)]
    tiles = lambda c: bass.ds(c * QT, QT)
    if K == 2:
        turned, gt_ready, prod_ps, read, act_in, act_out, msg_ready, worked = (
            st.pair(x) for x in ("turned", "gt_ready", "prod_ps", "prod_read", "act_in", "act_out", "msg_ready", "worked"))
        GT = [st.sb(f"GT{s}", [P, QT * P]) for s in range(2)]
        msg = [st.sb(f"msg{s}", [P, QT, D]) for s in range(2)]
        gt_ps = st.ps("gt_ps", [P, 512])
        g_free = turned
    else:
        msg, g_free = G, merged_ps
    if kind == "attention":
        scored = st.pair("scored")
        ea_loaded, et_ready = st.pair("ea_loaded"), st.pair("et_ready")
        ea = [st.sb(f"ea{s}", [P, QT, D]) for s in range(2)]
        ET = [st.sb(f"ET{s}", [P, 2 * P]) for s in range(2)]
        et_ps, e_ps = st.ps("et_ps", [P, 512]), [st.ps(f"e_ps{x}", [P, 512]) for x in range(2)]
        kvq_ps = [st.ps(f"kvq_ps{x}", [P, 512]) for x in range(2)]
        kvq = [st.sb(f"kvq{s}", [P, QT, 3 * D]) for s in range(2)]
        ee = [st.sb(f"ee{s}", [P, QT, D]) for s in range(2)]
        score = [st.sb(f"score{s}", [P, QT * HEADS]) for s in range(2)]
        ex = [st.sb(f"ex{s}", [P, QT * HEADS]) for s in range(2)]
    if kind == "conv":
        diff_ready = st.pair("diff_ready")
        z_ps = st.ps("z_ps", [P, 512])
        z = [st.sb(f"z{s}", [P, QT, D]) for s in range(2)]
        sg = [st.sb(f"sg{s}", [P, QT, D]) for s in range(2)]

    with st.block() as block:
        @block.sync
        def _(sp):
            def attributes(i, s):
                wait(sp, turned[s], i)
                first = (2 * i + s) * QT
                if not isinstance(i, int):
                    sp.dma_start(ea[s][:, :, :], edge_attr[bass.ds(first * P, QT * P), :].rearrange("(t p) f -> p t f", p=P)).then_inc(ea_loaded[s], 16 * QT)
                else:
                    for k in range(QT):
                        n = min(N_EDGES - (first + k) * P, P)
                        at = (first + k) * P if n > 0 else 0
                        n = n if n > 0 else P
                        sp.dma_start(ea[s][0:n, k, :], edge_attr[at:at + n, :]).then_inc(ea_loaded[s], 16)

            def load(i, s):
                wait(sp, eq_ready[s], i)
                sp.dma_start(rows[s][:, :, :], rows_dram[tiles(2 * i + s), :].rearrange("(a t) e -> a t e", a=1).partition_broadcast(P)).then_inc(rows_loaded[s], 16)
                if kind == "attention":
                    attributes(i, s)

            def step(i):
                for s in range(2):
                    load(i, s)

            loop(sp, ESTEPS - 1, step)
            for s in range(2):
                load(ESTEPS - 1, s)

        @block.gpsimd
        def _(pool):
            def gather(i, s, k):
                if k == 0:
                    wait(pool, g_idx[s], i + 1)
                    wait(pool, g_free[s], i)
                    nc.gpsimd.sem_inc(admitted, 1)
                for g in range(K):
                    pool.indirect_dma_start(out=G[s][:, k, g * D:(g + 1) * D], out_offset=None, in_=h_table,
                                            in_offset=bass.IndirectOffsetOnAxis(ap=gi[s][g][:, k:k + 1], axis=0)).then_inc(gathered[g][s], 16)

            def scatter(i, s, k):
                if k == 0:
                    wait(pool, s_idx[s], i + 1)
                    wait(pool, merged_ready[s], i + 1)
                    wait(pool, scattered[1 - s], 16 * QT * (i + s))
                else:
                    wait(pool, scattered[s], 16 * (QT * i + k))
                nc.gpsimd.sem_inc(admitted, 1)
                pool.indirect_dma_start(out=base_table, out_offset=bass.IndirectOffsetOnAxis(ap=si[s][:, k:k + 1], axis=0),
                                        in_=merged[s][:, k, :], in_offset=None, compute_op=ALU.add).then_inc(scattered[s], 16)

            for k in range(QT):
                gather(0, 0, k)
            def step(i):
                for s in range(2):
                    gather(i + s, 1 - s, 0)
                    gather(i + s, 1 - s, 1)
                    for k in range(QT):
                        if k + 2 < QT:
                            gather(i + s, 1 - s, k + 2)
                        scatter(i, s, k)

            loop(pool, ESTEPS, step)
            for s in range(2):
                pool.wait_ge(scattered[s], 16 * QT * ESTEPS)
            for g in range(K):
                pool.wait_ge(gathered[g][0], 16 * QT * (ESTEPS + 1))

        @block.scalar
        def _(act):
            def gather_columns(i, s):
                wait(act, g_free[s], i)
                for g, name in enumerate(gather_cols):
                    last = nc.scalar.copy(gi[s][g][:, :], C[name + "_i"][:, tiles(2 * i + s)])
                    last.then_inc(g_idx[s], 1) if g == K - 1 else None

            def scatter_columns(i, s):
                wait(act, scattered[s], 16 * QT * i)
                nc.scalar.copy(si[s][:, :], C["scatter_" + target][:, tiles(2 * i + s)]).then_inc(s_idx[s], 1)

            def turned_rows(i, s):
                wait(act, turned[s], i + 1)
                wait(act, prod_ps[s], i)
                nc.scalar.copy(GT[s][:, :], gt_ps[:, :]).then_inc(gt_ready[s], 1)
                if kind == "attention":
                    nc.scalar.copy(ET[s][:, :], et_ps[:, 0:2 * P]).then_inc(et_ready[s], 1)

            gather_columns(0, 0)
            def step(i):
                for s in range(2):
                    gather_columns(i + s, 1 - s)
                    scatter_columns(i, s)
                    if K == 2:
                        turned_rows(i, s)
                        wait(act, act_in[s], i + 1)
                    if kind == "attention":
                        nc.scalar.activation(ex[s][:, :], score[s][:, :], ACT.Exp).then_inc(act_out[s], 1)
                    if kind == "conv":
                        nc.scalar.activation(sg[s][:, :, :], z[s][:, :, :], ACT.Sigmoid).then_inc(act_out[s], 1)

            loop(act, ESTEPS, step)

        @block.tensor
        def _(pe):
            def merge(i, s):
                wait(pe, eq_ready[s], i + 1)
                wait(pe, merged_ready[s], i)
                if K == 2:
                    wait(pe, msg_ready[s], i + 1)
                else:
                    wait(pe, gathered[0][s], 16 * QT * (i + 1))
                for k in range(QT):
                    last = nc.tensor.matmul(m_ps[s][:, k * D:(k + 1) * D], eq[s][:, k, :], msg[s][:, k, :], start=True, stop=True)
                last.then_inc(merged_ps[s], 1)

            def turn(i, s):
                wait(pe, gt_ready[1 - s], i + s)
                if kind == "attention":
                    for g in range(K):
                        wait(pe, gathered[g][s], 16 * QT * (i + 1))
                    wait(pe, ea_loaded[s], 16 * QT * (i + 1))
                    wait(pe, et_ready[1 - s], i + s)
                    for k in range(QT // 2):
                        two = ea[s][:, 2 * k:2 * k + 2, :].rearrange("p t f -> p (t f)")
                        nc.tensor.transpose(et_ps[:, k * P:(k + 1) * P], two, C["iden"][:, :])
                else:
                    wait(pe, diff_ready[s], i + 1)
                for k in range(QT):
                    last = nc.tensor.transpose(gt_ps[:, k * P:(k + 1) * P], G[s][:, k, :], C["iden"][:, :])
                last.then_inc(turned[s], 1)

            def products(i, s):
                wait(pe, gt_ready[s], i + 1)
                wait(pe, read[1 - s], i + s)
                if kind == "attention":
                    wait(pe, et_ready[s], i + 1)
                    for k in range(QT):
                        half = slice((k % 2) * D, (k % 2 + 1) * D)
                        nc.tensor.matmul(kvq_ps[k // 2][:, (k % 2) * 3 * D:(k % 2 + 1) * 3 * D], GT[s][:, k * P:(k + 1) * P], C["kvq"][:, :], start=True, stop=True)
                        last = nc.tensor.matmul(e_ps[k % 2][:, (k // 2) * D:(k // 2 + 1) * D], ET[s][half, (k // 2) * P:(k // 2 + 1) * P], C["we"][half, :], start=True, stop=True)
                else:
                    for k in range(QT):
                        last = nc.tensor.matmul(z_ps[:, k * D:(k + 1) * D], GT[s][:, k * P:(k + 1) * P], C["w3"][:, :], start=True, stop=True)
                last.then_inc(prod_ps[s], 1)

            def step(i):
                for s in range(2):
                    if K == 2:
                        turn(i, s)
                        products(i, s)
                    merge(i, s)

            loop(pe, ESTEPS, step)

        @block.vector
        def _(dve):
            def equal(i, s):
                wait(dve, rows_loaded[s], 16 * i + 16)
                wait(dve, merged_ps[s], i)
                cols = C[target + "_f"][:, tiles(2 * i + s)].unsqueeze(2).to_broadcast([P, QT, P])
                nc.vector.tensor_tensor(eq[s][:, :, :], rows[s][:, :, :], cols, ALU.is_equal).then_inc(eq_ready[s], 1)

            def evict(i, s):
                wait(dve, merged_ps[s], i + 1)
                wait(dve, scattered[s], 16 * QT * i)
                nc.vector.tensor_copy(merged[s][:, :, :].rearrange("p t f -> p (t f)"), m_ps[s][:, 0:QT * D]).then_inc(merged_ready[s], 1)

            def attention(i, s):
                wait(dve, prod_ps[s], i + 1)
                bias = C["kvqe_b"]
                for x in range(2):
                    nc.vector.tensor_tensor(kvq[s][:, 2 * x:2 * x + 2, :], kvq_ps[x][:, 0:6 * D].rearrange("p (t f) -> p t f", t=2),
                                            bias[:, 0:3 * D].unsqueeze(1).to_broadcast([P, 2, 3 * D]), ALU.add)
                    last = nc.vector.tensor_tensor(ee[s][:, x:QT:2, :], e_ps[x][:, 0:2 * D].rearrange("p (t f) -> p t f", t=2),
                                                   bias[:, 3 * D:4 * D].unsqueeze(1).to_broadcast([P, 2, D]), ALU.add)
                last.then_inc(read[s], 1)
                wait(dve, read[s], i + 1)
                q = kvq[s][:, :, 2 * D:3 * D]
                nc.vector.tensor_tensor(q, kvq[s][:, :, 0:D], q, ALU.mult).then_inc(worked[s], 1)
                wait(dve, worked[s], 2 * i + 1)
                nc.vector.scalar_tensor_tensor(ee[s][:, :, :], q, float((D // HEADS) ** -0.5), ee[s][:, :, :], ALU.mult, ALU.mult).then_inc(worked[s], 1)
                wait(dve, worked[s], 2 * i + 2)
                nc.vector.tensor_reduce(score[s][:, :], ee[s][:, :, :].rearrange("p t (h d) -> p (t h) d", h=HEADS), AX.X, ALU.add).then_inc(scored[s], 1)
                wait(dve, scored[s], i + 1)
                nc.vector.tensor_scalar(score[s][:, :], score[s][:, :], -5.0, 5.0, ALU.max, ALU.min).then_inc(act_in[s], 1)
                wait(dve, act_out[s], i + 1)
                wait(dve, merged_ps[s], i)
                for k in range(QT):
                    last = nc.vector.tensor_tensor(msg[s][:, k, :].rearrange("p (h d) -> p h d", h=HEADS),
                                                   kvq[s][:, k, D:2 * D].rearrange("p (h d) -> p h d", h=HEADS),
                                                   ex[s][:, k * HEADS:(k + 1) * HEADS].unsqueeze(2).to_broadcast([P, HEADS, D // HEADS]), ALU.mult)
                last.then_inc(msg_ready[s], 1)

            def difference(i, s):
                for g in range(K):
                    wait(dve, gathered[g][s], 16 * QT * (i + 1))
                nc.vector.tensor_tensor(G[s][:, :, D:2 * D], G[s][:, :, D:2 * D], G[s][:, :, 0:D], ALU.subtract).then_inc(diff_ready[s], 1)

            def convolution(i, s):
                wait(dve, prod_ps[s], i + 1)
                row = lambda k: C["ec"][:, k * D:(k + 1) * D].unsqueeze(1).to_broadcast([P, QT, D])
                nc.vector.tensor_tensor(z[s][:, :, :], z_ps[:, 0:QT * D].rearrange("p (t f) -> p t f", t=QT), row(0), ALU.subtract).then_inc(read[s], 1)
                wait(dve, read[s], i + 1)
                nc.vector.tensor_tensor(z[s][:, :, :], z[s][:, :, :], row(1), ALU.mult).then_inc(worked[s], 1)
                wait(dve, worked[s], i + 1)
                nc.vector.tensor_tensor(z[s][:, :, :], z[s][:, :, :], row(2), ALU.add).then_inc(act_in[s], 1)
                wait(dve, act_out[s], i + 1)
                wait(dve, merged_ps[s], i)
                nc.vector.tensor_tensor(msg[s][:, :, :], z[s][:, :, :], sg[s][:, :, :], ALU.mult).then_inc(msg_ready[s], 1)

            def step(i):
                for s in range(2):
                    equal(i, s)
                    if kind == "attention":
                        attention(i, s)
                    if kind == "conv":
                        difference(i, s)
                        convolution(i, s)
                    evict(i, s)

            loop(dve, ESTEPS, step)


def build(nc, I, out, stop=None):
    ctx = ExitStack()
    with ctx:
        sb = lambda name, shape, dt=FP32: ctx.enter_context(nc.sbuf_tensor(name, shape, dt))
        table = lambda name: nc.dram_tensor(name, (ROWS, D), FP32, kind="Internal").ap()
        h_table, sum_table, x_table = table("h_table"), table("sum_table"), table("x_table")
        src_rows, dst_rows = (nc.dram_tensor(n, (COLS, P), INT32, kind="Internal").ap() for n in ("src_rows", "dst_rows"))
        C = {n: sb(n, [P, P]) for n in ("iden", "lower", "zeros", "ones_sq")}
        C["ones"] = sb("ones", [P, 2])
        C["spare_i"], C["spare"] = sb("spare_i", [P, 1], INT32), sb("spare", [P, 1])
        for n in ("src", "dst"):
            C[n + "_f"], C[n + "_i"], C["scatter_" + n] = sb(n + "_f", [P, COLS]), sb(n + "_i", [P, COLS], INT32), sb("scatter_" + n, [P, COLS], INT32)
        C["w1"] = [sb(f"w1_{l}", [P, HID]) for l in range(3)]
        C["w2"] = [sb(f"w2_{l}", [HID, D]) for l in range(3)]
        C["b2"] = [sb(f"b2_{l}", [P, D]) for l in range(3)]
        C["bn"] = sb("bn", [P, 12])
        C["bn_scale"], C["bn_shift"] = sb("bn_scale", [P, 1]), sb("bn_shift", [P, 1])
        C["eps1"] = sb("eps1", [P, 4])
        C["we"], C["kvq"], C["kvqe_b"] = sb("we", [P, D]), sb("kvq", [P, 3 * D]), sb("kvqe_b", [P, 4 * D])
        C["w3"], C["ec"] = sb("w3", [P, D]), sb("ec", [P, 4 * D])
        eps = lambda k: C["eps1"][:, k:k + 1]

        names = (f"stage{n}" for n in range(99))

        def run(f, *a, **k):
            with Stage(nc, next(names)) as st:
                f(nc, st, *a, **k)

        run(setup, I, C, src_rows, dst_rows)
        C["place_i"], C["place"] = sb("place_i", [P, WIN], INT32), sb("place", [P, WIN], FP16)
        C["rel"], C["ring_off"], C["unfit"] = sb("rel", [P, WINDOWS * WT]), sb("ring_off", [1, WINDOWS * WT], INT32), sb("unfit", [1, 1], INT32)
        run(plan, I, C, dst_rows)
        run(duplicates, C, src_rows, "src")
        run(duplicates, C, dst_rows, "dst")

        def program(sum_edges):
            nc.all_engine_barrier()
            run(layernorm, C, I["x"], h_table, x_table, eps(0), add_source=True)
            sum_edges(x_table)
            run(layernorm, C, x_table, h_table, sum_table, eps(1))
            for l in range(3):
                sum_edges(sum_table)
                run(batch_stats, C, sum_table, l)
                if l < 2:
                    run(mlp, C, sum_table, l, h_table=h_table, base_table=sum_table, eps_col=eps(l + 2))
                else:
                    run(mlp, C, sum_table, l, residual=x_table, out=out)
            run(layernorm, C, out, h_table)
            run(edges, C, "attention", h_table, out, dst_rows, ["src", "dst"], "dst", edge_attr=I["edge_attr_64"])
            run(layernorm, C, out, h_table)
            run(edges, C, "conv", h_table, out, src_rows, ["src", "dst"], "src")
            nc.all_engine_barrier()

        unfit = nc.values_load(C["unfit"][0:1, 0:1], min_val=0, max_val=1 << 20)
        with nc.If(unfit == 0):
            program(lambda table: run(window_sum, C, h_table, table))
        with nc.Else():
            program(lambda table: run(edges, C, "sum", h_table, table, dst_rows, ["src"], "dst"))


_INS = ["x", "src", "dst", "edge_attr_64", "L0_gnn_eps", "L1_gnn_W1", "L1_gnn_b1", "L1_gnn_gamma", "L1_gnn_beta",
        "L1_gnn_W2", "L1_gnn_b2", "L1_gnn_eps", "L2_gnn_WQ", "L2_gnn_bQ", "L2_gnn_WK", "L2_gnn_bK", "L2_gnn_WE",
        "L2_gnn_bE", "L2_gnn_WV", "L2_gnn_bV", "L3_gnn_W", "L3_gnn_gamma", "L3_gnn_beta", "L3_gnn_running_mean",
        "L3_gnn_running_var"]


def kernel(**inputs):
    import numpy as _np
    import concourse.bacc as _bacc
    from concourse.bass_utils import run_bass_kernel_spmd as _run

    nc = _bacc.Bacc("TRN2", target_bir_lowering=False, num_devices=1)
    arrays, I = {}, {}
    for name in _INS:
        a = _np.ascontiguousarray(inputs[name])
        arrays[f"in_{name}"] = a
        I[name] = nc.dram_tensor(f"in_{name}", a.shape, mybir.dt.from_np(a.dtype), kind="ExternalInput").ap()
    out = nc.dram_tensor("out_nodes", (ROWS, D), FP32, kind="ExternalOutput").ap()
    build(nc, I, out)
    r = _run(nc, [arrays], core_ids=[0])
    return r.results[0]["out_nodes"][:N_NODES]
```

```python
import concourse.bass as bass
from concourse import mybir
from contextlib import ExitStack, contextmanager

FP32 = mybir.dt.float32
INT32 = mybir.dt.int32
BF16 = mybir.dt.bfloat16
FP16 = mybir.dt.float16
ALU = mybir.AluOpType
ACT = mybir.ActivationFunctionType
AX = mybir.AxisListType

P = 128
N_NODES, N_EDGES, D, HID, HEADS = 100000, 50000, 64, 128, 8
CH = 16
CHUNK = P * CH
STEPS = 25
CHUNKS = 2 * STEPS
ROWS = CHUNKS * CHUNK
CHW = CH * D
NODE_CHUNKS = N_NODES // CHUNK
NODE_PARTS = (N_NODES - NODE_CHUNKS * CHUNK) // CH
assert NODE_CHUNKS == CHUNKS - 2 and NODE_CHUNKS * CHUNK + NODE_PARTS * CH == N_NODES and ROWS - N_NODES >= P
TILES = -(-N_EDGES // P)
QT = 4
ESTEPS = -(-TILES // (2 * QT))
COLS = 400
assert COLS >= (ESTEPS * 2 + 1) * QT
NPP = 4
WIN = NPP * P
WPC = CHUNK // WIN
WINDOWS = CHUNKS * WPC
WT = 4
NODE_SPLIT = N_EDGES // 400
GROUP = 8
RING_GROUPS = 10
RT = RING_GROUPS * GROUP
assert GROUP * CHUNKS == COLS and WINDOWS % 4 == 0 and N_EDGES * CHUNK == N_NODES * GROUP * P
LN_EPS = 1e-5
BN_EPS = 1e-5


class Stage:

    def __init__(self, nc, name):
        self.nc, self.name, self.ctx, self.sems = nc, name, ExitStack(), []

    def __enter__(self):
        self.ctx.__enter__()
        return self

    def sem(self, name):
        self.sems.append(self.nc.alloc_semaphore(name=f"{self.name}_{name}"))
        return self.sems[-1]

    def pair(self, name):
        return [self.sem(f"{name}0"), self.sem(f"{name}1")]

    def sb(self, name, shape, dt=FP32):
        return self.ctx.enter_context(self.nc.sbuf_tensor(f"{self.name}_{name}", shape, dt))

    def ps(self, name, shape):
        return self.ctx.enter_context(self.nc.psum_tensor(f"{self.name}_{name}", shape, FP32))

    def block(self):
        return self.nc.Block()

    def __exit__(self, *a):
        self.ctx.__exit__(*a)
        if a[0] is None:
            self.nc.clear_and_free_semaphores(self.sems)
            self.nc.all_engine_barrier()


def wait(eng, sem, value):
    if not (isinstance(value, int) and value <= 0):
        eng.wait_ge(sem, value)


def loop(eng, steps, step, peel_last=False):
    step(0)
    with eng.Fori(1, steps - peel_last) as i:
        step(i)
    if peel_last:
        step(steps - 1)


def chunk(table, c):
    return table[bass.ds(c * CHUNK, CHUNK), :].rearrange("(p j) f -> p j f", p=P)


def flat_chunk(table, c):
    return table[bass.ds(c * CHUNK, CHUNK), :].rearrange("(p j) f -> p (j f)", p=P)


def setup(nc, st, I, C, src_rows, dst_rows):
    stage, loaded, built, turned = (st.sem(x) for x in ("stg_filled", "params_loaded", "consts_built", "turned"))
    rows_loaded, rows_stored, cols_ready = st.sem("rows_loaded"), st.sem("rows_stored"), st.sem("cols_ready")
    var_ready, std_ready, dve_done = st.sem("var_ready"), st.sem("std_ready"), st.sem("dve_done")
    NB = COLS // 4
    rows = [st.sb(f"idx_rows{k}", [NB, 4, P], INT32) for k in range(2)]
    rows_f = [st.sb(f"idx_rows_f{k}", [NB, 4, P]) for k in range(2)]
    cols_ps = [st.ps(f"cols_ps{k}", [P, 512]) for k in range(2)]
    w3 = st.sb("w3_rows", [D, 2 * D])
    w3_ps = st.ps("w3_ps", [P, 512])
    one_eps = st.sb("eps_raw", [P, 4])
    iden0 = st.sb("iden0", [P, P])
    row1 = lambda a: a.rearrange("(a n) -> a n", a=1)
    NLOAD = 0

    loads = [(w3[:, :], I["L3_gnn_W"])]
    for l in range(3):
        for half in range(2):
            loads.append((C["w1"][l][half * D:(half + 1) * D, :], I["L1_gnn_W1"][l, :, :]))
        loads.append((C["w2"][l][:, :], I["L1_gnn_W2"][l, :, :]))
        loads.append((C["b2"][l][:, :], I["L1_gnn_b2"][l:l + 1, :].partition_broadcast(P)))
        for k, name in enumerate(("b1", "gamma", "beta")):
            loads.append((C["bn"][:, 4 * l + k:4 * l + k + 1],
                          I["L1_gnn_" + name][l, :].rearrange("(p a) -> p a", a=1)))
    loads.append((one_eps[:, 0:1], row1(I["L0_gnn_eps"]).partition_broadcast(P)))
    loads.append((one_eps[:, 1:4], row1(I["L1_gnn_eps"]).partition_broadcast(P)))
    for half in range(2):
        loads.append((C["we"][half * D:(half + 1) * D, :], I["L2_gnn_WE"]))
    loads.append((C["kvq"][0:D, 0:D], I["L2_gnn_WK"]))
    loads.append((C["kvq"][0:D, D:2 * D], I["L2_gnn_WV"]))
    loads.append((C["kvq"][D:2 * D, 2 * D:3 * D], I["L2_gnn_WQ"]))
    for k, name in enumerate(("bK", "bV", "bQ", "bE")):
        loads.append((C["kvqe_b"][:, k * D:(k + 1) * D], row1(I["L2_gnn_" + name]).partition_broadcast(P)))
    for k, name in enumerate(("running_mean", "gamma", "beta", "running_var")):
        loads.append((C["ec"][:, k * D:(k + 1) * D], row1(I["L3_gnn_" + name]).partition_broadcast(P)))
    NL = len(loads)
    full = N_EDGES // P
    tail = N_EDGES - full * P

    with st.block() as block:
        @block.gpsimd
        def _(pool):
            for k in range(2):
                nc.gpsimd.iota(rows[k][:, :, :], pattern=[[0, 4], [1, P]], base=N_NODES,
                               channel_multiplier=0).then_inc(stage, 1)
            nc.gpsimd.iota(C["spare_i"][:, :], pattern=[[0, 1]], base=N_NODES, channel_multiplier=1).then_inc(stage, 1)
            nc.gpsimd.memset(iden0[:, :], 0.0).then_inc(stage, 1)
            nc.gpsimd.memset(C["lower"][:, :], 1.0).then_inc(stage, 1)
            nc.gpsimd.memset(C["zeros"][:, :], 0.0).then_inc(stage, 1)
            nc.gpsimd.memset(C["ones"][:, :], 1.0).then_inc(stage, 1)
            nc.gpsimd.memset(C["ones_sq"][:, :], 1.0).then_inc(stage, 1)
            nc.gpsimd.memset(C["kvq"][:, :], 0.0).then_inc(stage, 1)
            pool.wait_ge(stage, 9)
            nc.gpsimd.affine_select(out=C["iden"][:, :], in_=iden0[:, :], compare_op=ALU.not_equal, fill=1.0,
                                    base=0, pattern=[[-1, P]], channel_multiplier=1).then_inc(built, 1)
            nc.gpsimd.affine_select(out=C["lower"][:, :], in_=C["lower"][:, :], compare_op=ALU.is_gt, fill=0.0,
                                    base=0, pattern=[[-1, P]], channel_multiplier=1).then_inc(built, 1)

        @block.sync
        def _(sp):
            sp.wait_ge(stage, 9)
            for k, name in enumerate(("src", "dst")):
                whole = I[name][0:full * P].rearrange("(t e) -> t e", e=P)
                sp.dma_start(rows[k][:, 0:3, :], whole[0:3 * NB, :].rearrange("(b t) e -> t b e", b=3)).then_inc(rows_loaded, 16)
                sp.dma_start(rows[k][0:full - 3 * NB, 3, :], whole[3 * NB:full, :]).then_inc(rows_loaded, 16)
                sp.dma_start(rows[k][full - 3 * NB:full - 3 * NB + 1, 3, 0:tail], row1(I[name][full * P:N_EDGES])).then_inc(rows_loaded, 16)
            for to, of in loads:
                sp.dma_start(to, of).then_inc(loaded, 16)
            sp.wait_ge(rows_loaded, 96)
            for k, table in enumerate((src_rows, dst_rows)):
                sp.dma_start(table.rearrange("(b t) e -> t b e", b=4), rows[k][:, :, :]).then_inc(rows_stored, 16)
            sp.wait_ge(rows_stored, 32)
            sp.wait_ge(loaded, 16 * NL)

        @block.tensor
        def _(pe):
            pe.wait_ge(built, 2)
            for k in range(2):
                pe.wait_ge(cols_ready, k + 1)
                for b in range(4):
                    last = nc.tensor.transpose(cols_ps[k][:, b * NB:(b + 1) * NB], rows_f[k][:, b, :], C["iden"][0:NB, 0:NB])
                last.then_inc(turned, 1)
            pe.wait_ge(loaded, 16 * NL)
            nc.tensor.transpose(w3_ps[:, 0:D], w3[:, :], C["iden"][0:D, 0:D]).then_inc(turned, 1)

        @block.vector
        def _(dve):
            dve.wait_ge(rows_loaded, 96)
            for k in range(2):
                nc.vector.tensor_copy(rows_f[k][:, :, :], rows[k][:, :, :]).then_inc(cols_ready, 1)
            for k, name in enumerate(("src", "dst")):
                dve.wait_ge(turned, k + 1)
                nc.vector.tensor_copy(C[name + "_f"][:, :], cols_ps[k][:, 0:COLS])
                nc.vector.tensor_copy(C[name + "_i"][:, :], cols_ps[k][:, 0:COLS])
            dve.wait_ge(stage, 9)
            nc.vector.tensor_copy(C["spare"][:, :], C["spare_i"][:, :])
            dve.wait_ge(turned, 3)
            nc.vector.tensor_copy(C["w3"][:, :], w3_ps[:, 0:D])
            nc.vector.tensor_scalar(C["eps1"][:, :], one_eps[:, :], 1.0, None, ALU.add)
            var, gam = C["ec"][:, 3 * D:4 * D], C["ec"][:, D:2 * D]
            nc.vector.tensor_scalar(var, var, BN_EPS, None, ALU.add).then_inc(var_ready, 1)
            dve.wait_ge(std_ready, 1)
            nc.vector.reciprocal(var, var).then_inc(dve_done, 1)
            dve.wait_ge(dve_done, 1)
            nc.vector.tensor_tensor(gam, gam, var, ALU.mult)

        @block.scalar
        def _(act):
            act.wait_ge(var_ready, 1)
            nc.scalar.activation(C["ec"][:, 3 * D:4 * D], C["ec"][:, 3 * D:4 * D], ACT.Sqrt).then_inc(std_ready, 1)


def plan(nc, st, I, C, dst_rows):
    loaded, loaded2, laid, tail, summed, packed = (st.sem(x) for x in ("loaded", "loaded2", "laid", "tail", "summed", "packed"))
    rel_done = st.sem("rel_done")
    NB, W = COLS // 4, WINDOWS
    rows = st.sb("rows", [NB, 4, P], INT32)
    ends = st.sb("ends", [NB, 4, 2])
    a, b = st.sb("a", [NODE_SPLIT, COLS], INT32), st.sb("b", [NODE_SPLIT, COLS], INT32)
    a_gt_b = st.sb("a_gt_b", [P, COLS])
    bad = st.sb("bad", [P, 4])
    thr_i, thr = st.sb("thr_i", [P, W + 1], INT32), st.sb("thr", [P, W + 1])
    lo_i, hi_i = st.sb("lo_i", [P, W], INT32), st.sb("hi_i", [P, W], INT32)
    below = [st.sb(f"below{k}", [NB, W + 1]) for k in range(8)]
    full, begun = st.ps("full", [P, 512]), st.ps("begun", [P, 512])
    verdict = st.ps("verdict", [P, 512])
    f, t0, x, q, wrap = (st.sb(n, [P, W]) for n in ("f", "t0", "x", "q", "wrap"))
    t0_i = st.sb("t0_i", [1, W], INT32)
    off = st.sb("off", [P, W, WT])

    with st.block() as block:
        @block.sync
        def _(sp):
            sp.dma_start(rows[:, :, :], dst_rows.rearrange("(b t) e -> t b e", b=4)).then_inc(loaded, 16)
            sp.dma_start(a[:, :], I["dst"].rearrange("(p j) -> p j", j=COLS)).then_inc(loaded, 16)
            sp.dma_start(b[:, :], I["dst"].rearrange("(p j) -> p j", j=COLS)).then_inc(loaded, 16)
            sp.wait_ge(loaded, 48)
            n = NODE_SPLIT - 1
            sp.dma_start(b[0:n, :], I["dst"][1:1 + n * COLS].rearrange("(p j) -> p j", j=COLS)).then_inc(loaded2, 16)
            sp.dma_start(b[n:n + 1, 0:COLS - 1], I["dst"][1 + n * COLS:N_EDGES].rearrange("(p j) -> p j", p=1)).then_inc(loaded2, 16)
            sp.wait_ge(loaded2, 32)

        @block.gpsimd
        def _(pool):
            nc.gpsimd.iota(thr_i[:, :], pattern=[[WIN, W + 1]], base=0, channel_multiplier=0).then_inc(laid, 1)
            nc.gpsimd.iota(lo_i[:, :], pattern=[[GROUP, CHUNKS], [0, WPC]], base=-GROUP, channel_multiplier=0).then_inc(laid, 1)
            nc.gpsimd.iota(hi_i[:, :], pattern=[[GROUP, CHUNKS], [0, WPC]], base=2 * GROUP - WT, channel_multiplier=0).then_inc(laid, 1)
            nc.gpsimd.iota(C["place_i"][:, :], pattern=[[1, NPP], [NPP, P]], base=0, channel_multiplier=0).then_inc(laid, 1)

        @block.tensor
        def _(pe):
            pe.wait_ge(tail, 12)
            for k in range(8):
                ps = full if k < 4 else begun
                last = nc.tensor.matmul(ps[:, 0:W + 1], C["ones_sq"][0:NB, :], below[k][:, :], start=k % 4 == 0, stop=k % 4 == 3)
            last.then_inc(summed, 1)
            pe.wait_ge(packed, 1)
            nc.tensor.matmul(verdict[:, 0:4], C["ones_sq"][:, :], bad[:, :], start=True, stop=True).then_inc(summed, 1)

        @block.vector
        def _(dve):
            n = [0]

            def link(ins):
                n[0] += 1
                ins.then_inc(tail, 1)
                dve.wait_ge(tail, n[0])

            dve.wait_ge(laid, 4)
            link(nc.vector.tensor_scalar(thr[:, :], thr_i[:, :], float(N_NODES), None, ALU.min))
            link(nc.vector.tensor_copy(C["place"][:, :], C["place_i"][:, :]))
            dve.wait_ge(loaded, 48)
            link(nc.vector.tensor_copy(ends[:, :, 0:1], rows[:, :, 0:1]))
            link(nc.vector.tensor_copy(ends[:, :, 1:2], rows[:, :, P - 1:P]))
            for k in range(8):
                link(nc.vector.tensor_scalar(below[k][:, :], thr[0:NB, :], ends[:, k % 4, 1 - k // 4:2 - k // 4], None, ALU.is_gt))
            link(nc.vector.memset(bad[:, :], 0.0))
            dve.wait_ge(loaded2, 32)
            link(nc.vector.tensor_tensor(a_gt_b[0:NODE_SPLIT, :], a[:, :], b[:, :], ALU.is_gt))
            link(nc.vector.tensor_reduce(bad[0:NODE_SPLIT, 0:1], a_gt_b[0:NODE_SPLIT, :], AX.X, ALU.add))
            dve.wait_ge(summed, 1)
            link(nc.vector.tensor_copy(f[:, :], full[:, 0:W]))
            link(nc.vector.tensor_scalar(t0[:, :], lo_i[:, :], 0.0, None, ALU.max))
            link(nc.vector.tensor_tensor(t0[:, :], t0[:, :], f[:, :], ALU.max))
            link(nc.vector.tensor_scalar(x[:, :], hi_i[:, :], float(COLS - WT), None, ALU.min))
            link(nc.vector.tensor_tensor(t0[:, :], t0[:, :], x[:, :], ALU.min))
            link(nc.vector.tensor_tensor(x[:, :], t0[:, :], f[:, :], ALU.is_gt))
            link(nc.vector.tensor_reduce(bad[:, 1:2], x[:, :], AX.X, ALU.add))
            link(nc.vector.tensor_scalar(q[:, :], t0[:, :], float(WT), None, ALU.add))
            link(nc.vector.tensor_tensor(x[:, :], q[:, :], begun[:, 1:W + 1], ALU.is_lt))
            link(nc.vector.tensor_reduce(bad[:, 2:3], x[:, :], AX.X, ALU.add))
            nc.vector.engine_nop().then_inc(packed, 1)
            for i in range(WT):
                link(nc.vector.tensor_scalar(x[:, :], t0[:, :], float(i), None, ALU.add))
                link(nc.vector.memset(q[:, :], 0.0))
                for k in range(1, COLS // RT):
                    link(nc.vector.tensor_scalar(wrap[:, :], x[:, :], float(k * RT), float(RT), ALU.is_ge, ALU.mult))
                    link(nc.vector.tensor_tensor(q[:, :], q[:, :], wrap[:, :], ALU.add))
                link(nc.vector.tensor_tensor(x[:, :], x[:, :], q[:, :], ALU.subtract))
                link(nc.vector.tensor_copy(off[:, :, i:i + 1].rearrange("p w o -> p (w o)"), x[:, :]))
            link(nc.vector.tensor_copy(C["ring_off"][:, :], off[0:1, :, :].rearrange("p w o -> p (w o)")))
            link(nc.vector.tensor_copy(t0_i[:, :], t0[0:1, :]))
            dve.wait_ge(summed, 2)
            link(nc.vector.tensor_reduce(q[0:1, 0:1], verdict[0:1, 0:4], AX.X, ALU.add))
            link(nc.vector.tensor_copy(C["unfit"][:, :], q[0:1, 0:1]))

            def window_targets(w):
                _, firsts = nc.values_load_multi_w_load_instructions(t0_i[0:1, bass.ds(w, 4)], engines=[mybir.EngineType.DVE], min_val=0, max_val=COLS - WT,
                                                                           skip_runtime_bounds_check_because="clamped above")
                for k, first in enumerate(firsts):
                    last = nc.vector.tensor_copy(C["rel"][:, bass.ds((w + k) * WT, WT)], C["dst_f"][:, bass.ds(first, WT)])
                return last

            with dve.Fori(0, W // 4) as w4:
                window_targets(w4 * 4).then_inc(rel_done, 1)
            dve.wait_ge(rel_done, W // 4)
            rel = C["rel"][:, :].rearrange("p (w t) -> p w t", t=WT)
            nc.vector.tensor_tensor(rel, rel, thr_i[:, 0:W].unsqueeze(2).to_broadcast([P, W, WT]), ALU.subtract).then_inc(rel_done, 1)


def window_sum(nc, st, C, base_table, h_table=None, messages=None):
    gathered, idx_ready = st.pair("gathered"), st.pair("idx_ready")
    hi_done, r_done, mid_done, lo_done = (st.pair(x) for x in ("hi_done", "r_done", "mid_done", "lo_done"))
    hot_ready, hot_used = st.pair("hot_ready"), st.pair("hot_used")
    base_loaded, t_ready, t_stored, rel_ready = (st.pair(x) for x in ("base_loaded", "t_ready", "t_stored", "rel_ready"))
    rel = [st.sb(f"rel{s}", [P, WPC * WT]) for s in range(2)]
    half_added = st.pair("half_added")
    admitted = st.sem("admitted")
    raw = [st.sb(f"raw{s}", [P, GROUP, D]) for s in range(2)]
    rest = [st.sb(f"rest{s}", [P, GROUP, D]) for s in range(2)]
    gi = [st.sb(f"gi{s}", [P, GROUP], INT32) for s in range(2)]
    ring_hm = st.sb("ring_high_middle", [P, RT, 2 * D], BF16)
    ring_l = st.sb("ring_low", [P, RT, D], BF16)
    HW = WPC // 2
    hot = [st.sb(f"hot{r}", [P, HW * WT, WIN], BF16) for r in range(2)]
    base = [st.sb(f"base{s}", [P, WPC, NPP * D]) for s in range(2)]
    agg = [st.ps(f"agg{s}", [P, WPC * NPP, 2 * D]) for s in range(2)]
    G1 = lambda i, s: (i + s, 1 - s)
    GATHERED = 16 * (GROUP if messages is None else 1)

    def windows(table, c):
        return table[bass.ds(c * CHUNK, CHUNK), :].rearrange("(w p k) f -> p w (k f)", w=WPC, k=NPP)

    def ring_part(i, s, part):
        tiles = bass.ds(((2 * i + s) % RING_GROUPS) * GROUP, GROUP)
        return ring_l[:, tiles, :] if part == 2 else ring_hm[:, tiles, part * D:(part + 1) * D]

    def pairs(eng, step):
        step(0, False)
        with eng.Fori(1, STEPS - 1) as i:
            step(i, False)
        step(STEPS - 1, True)

    with st.block() as block:
        @block.sync
        def _(sp):
            def load(i, s):
                wait(sp, t_stored[s], 16 * i)
                sp.dma_start(base[s][:, :, :], windows(base_table, 2 * i + s)).then_inc(base_loaded[s], 16)

            def step(i, last):
                for s in range(2):
                    wait(sp, t_ready[s], i + 1)
                    sp.dma_start(windows(base_table, 2 * i + s), base[s][:, :, :]).then_inc(t_stored[s], 16)
                    if not last:
                        load(i + 1, s)

            load(0, 0)
            load(0, 1)
            pairs(sp, step)
            for s in range(2):
                sp.wait_ge(t_stored[s], 16 * STEPS)

        @block.gpsimd
        def _(pool):
            def step(i, last):
                for s in range(2):
                    if messages is not None:
                        wait(pool, r_done[s], i)
                        group = messages[bass.ds((2 * i + s) * (GROUP // QT), GROUP // QT), :, :].rearrange("q p f -> p q f")
                        pool.dma_start(raw[s][:, :, :].rearrange("p (q t) f -> p q (t f)", t=QT), group).then_inc(gathered[s], 16)
                        continue
                    wait(pool, idx_ready[s], i + 1)
                    wait(pool, r_done[s], i)
                    nc.gpsimd.sem_inc(admitted, 1)
                    for k in range(GROUP):
                        pool.indirect_dma_start(out=raw[s][:, k, :], out_offset=None, in_=h_table,
                                                in_offset=bass.IndirectOffsetOnAxis(ap=gi[s][:, k:k + 1], axis=0)).then_inc(gathered[s], 16)

            pairs(pool, step)

        @block.scalar
        def _(act):
            def columns(i, s):
                wait(act, gathered[s], GATHERED * i)
                nc.scalar.copy(gi[s][:, :], C["src_i"][:, bass.ds((2 * i + s) * GROUP, GROUP)]).then_inc(idx_ready[s], 1)

            def windows_of(i, s):
                wait(act, hot_ready[1], 2 * i + s - 1)
                nc.scalar.copy(rel[s][:, :], C["rel"][:, bass.ds((2 * i + s) * WPC * WT, WPC * WT)]).then_inc(rel_ready[s], 1)

            def split(i, s):
                wait(act, gathered[s], GATHERED * (i + 1))
                wait(act, hot_used[1], 2 * i + s - 2)
                nc.scalar.copy(ring_part(i, s, 0), raw[s][:, :, :]).then_inc(hi_done[s], 1)
                wait(act, r_done[s], i + 1)
                nc.scalar.copy(ring_part(i, s, 1), rest[s][:, :, :]).then_inc(mid_done[s], 1)

            def step(i, last):
                for s in range(2):
                    if not last and messages is None:
                        columns(i + 1, s)
                    if not (last and s):
                        split(*G1(i, s))
                        windows_of(*G1(i, s))

            if messages is None:
                columns(0, 0)
                columns(0, 1)
            split(0, 0)
            windows_of(0, 0)
            pairs(act, step)

        @block.vector
        def _(dve):
            def remainder(i, s):
                wait(dve, hi_done[s], i + 1)
                wait(dve, lo_done[s], i)
                nc.vector.tensor_tensor(rest[s][:, :, :], raw[s][:, :, :], ring_part(i, s, 0), ALU.subtract).then_inc(r_done[s], 1)

            def low(i, s):
                wait(dve, mid_done[s], i + 1)
                nc.vector.tensor_tensor(ring_part(i, s, 2), rest[s][:, :, :], ring_part(i, s, 1), ALU.subtract).then_inc(lo_done[s], 1)

            def one_hot(i, s, r):
                if r == 0:
                    wait(dve, rel_ready[s], i + 1)
                wait(dve, hot_used[r], 2 * i + s)
                for k in range(HW * WT):
                    last = nc.vector.tensor_scalar(hot[r][:, k, :], C["place"][:, :], rel[s][:, r * HW * WT + k:r * HW * WT + k + 1], None, ALU.is_equal)
                last.then_inc(hot_ready[r], 1)

            def combine(i, s):
                wait(dve, base_loaded[s], 16 * (i + 1))
                wait(dve, hot_used[1], 2 * i + s + 1)
                total = base[s][:, :, :].rearrange("p w (k f) -> p (w k) f", f=D)
                nc.vector.tensor_tensor(total, total, agg[s][:, :, 0:D], ALU.add).then_inc(half_added[s], 1)
                wait(dve, half_added[s], i + 1)
                nc.vector.tensor_tensor(total, total, agg[s][:, :, D:2 * D], ALU.add).then_inc(t_ready[s], 1)

            def step(i, last):
                for s in range(2):
                    if not (last and s):
                        remainder(*G1(i, s))
                    one_hot(i, s, 0)
                    if not (last and s):
                        low(*G1(i, s))
                    one_hot(i, s, 1)
                    if s or not (isinstance(i, int) and i == 0):
                        combine(i - 1 + s, 1 - s)

            remainder(0, 0)
            low(0, 0)
            pairs(dve, step)
            combine(STEPS - 1, 1)

        @block.tensor
        def _(pe):
            def step(i, last):
                for s in range(2):
                    if not (last and s):
                        wait(pe, lo_done[1 - s], i + s + 1)
                    wait(pe, t_ready[s], i)
                    for r in range(2):
                        wait(pe, hot_ready[r], 2 * i + s + 1)
                        for j in range(HW):
                            w = (2 * i + s) * WPC + r * HW + j
                            _, at = nc.values_load_multi_w_load_instructions(
                                C["ring_off"][0:1, bass.ds(w * WT, WT)], engines=[mybir.EngineType.PE], min_val=0, max_val=RT - 1,
                                skip_runtime_bounds_check_because="the plan takes them modulo the ring")
                            for k in range(NPP):
                                to = agg[s][:, (r * HW + j) * NPP + k, :]
                                for t in range(WT):
                                    ones = hot[r][:, j * WT + t, k * P:(k + 1) * P]
                                    nc.tensor.matmul(to, ones, ring_hm[:, bass.ds(at[t], 1), :], start=t == 0, stop=False)
                                    mm = nc.tensor.matmul(to[:, D:2 * D], ones, ring_l[:, bass.ds(at[t], 1), :], start=False, stop=t == WT - 1)
                        mm.then_inc(hot_used[r], 1)

            pairs(pe, step)


def layernorm(nc, st, C, source, h_table, base_table=None, eps_col=None, add_source=False):
    loaded, summed, mean_ready, centred, squared, ssum, var_ready, std_ready, rstd_ready, h_ready, base_ready, h_stored, base_stored = (
        st.pair(x) for x in ("x_loaded", "summed", "mean_ready", "centred", "squared", "ssum", "var_ready",
                             "std_ready", "rstd_ready", "h_ready", "base_ready", "h_stored", "base_stored"))
    kept = st.pair("kept")
    x = [st.sb(f"x{s}", [P, CH, D]) for s in range(2)]
    xc = [st.sb(f"xc{s}", [P, CH, D]) for s in range(2)]
    sq = [st.sb(f"sq{s}", [P, CH, D]) for s in range(2)]
    h = [st.sb(f"h{s}", [P, CH, D]) for s in range(2)]
    base = [st.sb(f"base{s}", [P, CH, D]) for s in range(2)]
    s1, mean, s2, var, rstd = ([st.sb(f"{x}{s}", [P, CH]) for s in range(2)] for x in ("s1", "mean", "s2", "var", "rstd"))
    padded = source.shape[0] == ROWS
    wide = lambda t: t[:, :].unsqueeze(2).to_broadcast([P, CH, D])

    with st.block() as block:
        @block.sync
        def _(sp):
            def step(i):
                for s in range(2):
                    wait(sp, centred[s], i)
                    if add_source:
                        wait(sp, kept[s], i)
                    c = 2 * i + s
                    if padded or not isinstance(i, int) or c < NODE_CHUNKS:
                        sp.dma_start(x[s][:, :, :], chunk(source, c)).then_inc(loaded[s], 16)
                    elif c == NODE_CHUNKS:
                        rows = source[c * CHUNK:N_NODES, :].rearrange("(p j) f -> p j f", j=CH)
                        sp.dma_start(x[s][0:NODE_PARTS, :, :], rows).then_inc(loaded[s], 16)
                    else:
                        sp.dma_start(x[s][:, :, :], chunk(source, s)).then_inc(loaded[s], 16)

            loop(sp, STEPS, step, peel_last=True)

        @block.vector
        def _(dve):
            def step(i):
                for s in range(2):
                    wait(dve, loaded[s], 16 * i + 16)
                    wait(dve, h_ready[s], i)
                    nc.vector.tensor_reduce(s1[s][:, :], x[s][:, :, :], AX.X, ALU.add).then_inc(summed[s], 1)
                for s in range(2):
                    wait(dve, summed[s], i + 1)
                    nc.vector.tensor_scalar(mean[s][:, :], s1[s][:, :], 1.0 / D, None, ALU.mult).then_inc(mean_ready[s], 1)
                for s in range(2):
                    wait(dve, mean_ready[s], i + 1)
                    nc.vector.tensor_tensor(xc[s][:, :, :], x[s][:, :, :], wide(mean[s]), ALU.subtract).then_inc(centred[s], 1)
                for s in range(2):
                    wait(dve, squared[s], i + 1)
                    nc.vector.tensor_reduce(s2[s][:, :], sq[s][:, :, :], AX.X, ALU.add).then_inc(ssum[s], 1)
                    wait(dve, ssum[s], i + 1)
                    nc.vector.tensor_scalar(var[s][:, :], s2[s][:, :], 1.0 / D, LN_EPS, ALU.mult, ALU.add).then_inc(var_ready[s], 1)
                for s in range(2):
                    wait(dve, std_ready[s], i + 1)
                    nc.vector.reciprocal(rstd[s][:, :], var[s][:, :]).then_inc(rstd_ready[s], 1)
                for s in range(2):
                    wait(dve, rstd_ready[s], i + 1)
                    wait(dve, h_stored[s], 16 * i)
                    nc.vector.scalar_tensor_tensor(h[s][:, :, :], xc[s][:, :, :], 0.0, wide(rstd[s]), ALU.max, ALU.mult).then_inc(h_ready[s], 1)
                for s in range(2):
                    if add_source:
                        wait(dve, h_ready[s], i + 1)
                        wait(dve, kept[s], i + 1)
                        nc.vector.scalar_tensor_tensor(base[s][:, :, :], h[s][:, :, :], eps_col, base[s][:, :, :], ALU.mult, ALU.add).then_inc(base_ready[s], 1)

            loop(dve, STEPS, step)

        @block.scalar
        def _(act):
            def step(i):
                for s in range(2):
                    wait(act, centred[s], i + 1)
                    nc.scalar.activation(sq[s][:, :, :], xc[s][:, :, :], ACT.Square).then_inc(squared[s], 1)
                for s in range(2) if add_source else ():
                    wait(act, base_stored[s], 16 * i)
                    nc.scalar.copy(base[s][:, :, :], x[s][:, :, :]).then_inc(kept[s], 1)
                for s in range(2):
                    wait(act, var_ready[s], i + 1)
                    nc.scalar.activation(var[s][:, :], var[s][:, :], ACT.Sqrt).then_inc(std_ready[s], 1)
                for s in range(2):
                    wait(act, h_ready[s], i + 1)
                    act.dma_start(chunk(h_table, 2 * i + s), h[s][:, :, :]).then_inc(h_stored[s], 16)
                    if base_table is not None:
                        if not add_source:
                            wait(act, base_stored[s], 16 * i)
                            nc.scalar.activation(base[s][:, :, :], h[s][:, :, :], ACT.Copy, scale=eps_col).then_inc(base_ready[s], 1)
                        wait(act, base_ready[s], i + 1)
                        act.dma_start(chunk(base_table, 2 * i + s), base[s][:, :, :]).then_inc(base_stored[s], 16)

            loop(act, STEPS, step)
            for s in range(2):
                act.wait_ge(h_stored[s], 16 * STEPS)
                if base_table is not None:
                    act.wait_ge(base_stored[s], 16 * STEPS)


def batch_stats(nc, st, C, table, l):
    loaded, used = st.pair("t_loaded"), st.pair("t_used")
    added, summed, tail = st.pair("added"), st.sem("summed"), st.sem("tail")
    zeroed, mm, std_ready = st.sem("zeroed"), st.sem("mm"), st.sem("std_ready")
    t = [st.sb(f"t{s}", [P, CHW]) for s in range(2)]
    acc = [st.sb(f"acc{s}", [P, CHW]) for s in range(2)]
    gram_sb = st.sb("gram_sb", [P, P])
    sum_sb = st.sb("sum_sb", [P, 1])
    prod = st.sb("prod", [P, HID])
    cols = st.sb("cols", [P, 8])
    gram, tsum, wg, moments = (st.ps(x, [P, 512]) for x in ("gram", "tsum", "wg", "moments"))
    bn, w1 = C["bn"], C["w1"][l]
    PAIR = 2 * D
    SUMS = [STEPS, STEPS - 1]

    with st.block() as block:
        @block.sync
        def _(sp):
            def step(i):
                for s in range(2):
                    wait(sp, used[s], i)
                    wait(sp, added[s], i)
                    sp.dma_start(t[s][:, :], flat_chunk(table, 2 * i + s)).then_inc(loaded[s], 16)

            loop(sp, STEPS, step)

        @block.tensor
        def _(pe):
            nc.tensor.matmul(gram[:, 0:P], C["zeros"][:, :], C["zeros"][:, :], start=True, stop=False)
            def step(i):
                for s in range(2):
                    wait(pe, loaded[s], 16 * i + 16)
                    c = 2 * i + s
                    n = P if not isinstance(i, int) or c < NODE_CHUNKS else NODE_PARTS if c == NODE_CHUNKS else 0
                    for q in range(CH // 2) if n else ():
                        two = t[s][0:n, q * PAIR:(q + 1) * PAIR]
                        last = nc.tensor.matmul(gram[:, 0:P], two, two, start=False, stop=False)
                    if n:
                        last.then_inc(used[s], 1)

            loop(pe, STEPS, step, peel_last=True)
            nc.tensor.matmul(gram[:, 0:P], C["zeros"][:, :], C["zeros"][:, :], start=False, stop=True)
            for s in range(2):
                pe.wait_ge(added[s], SUMS[s])
                for q in range(CH // 2):
                    last = nc.tensor.matmul(tsum[:, 0:1], acc[s][:, q * PAIR:(q + 1) * PAIR], C["ones"][:, 0:1], start=s == q == 0, stop=s == 1 and q == CH // 2 - 1)
            last.then_inc(summed, 1)
            pe.wait_ge(tail, 2)
            nc.tensor.matmul(wg[:, 0:HID], gram_sb[:, :], w1[:, :], start=True, stop=True)
            nc.tensor.matmul(moments[:, 0:1], w1[:, :], sum_sb[:, :], start=True, stop=True).then_inc(mm, 1)
            pe.wait_ge(tail, 3)
            nc.tensor.matmul(wg[:, HID:HID + 1], prod[:, :], C["ones"][:, 0:1], start=True, stop=True).then_inc(mm, 1)

        @block.vector
        def _(dve):
            n = [0]

            def link(ins):
                n[0] += 1
                ins.then_inc(tail, 1)
                dve.wait_ge(tail, n[0])

            for s in range(2):
                nc.vector.memset(acc[s][:, :], 0.0).then_inc(zeroed, 1)
            dve.wait_ge(zeroed, 2)

            def step(i):
                for s in range(2):
                    c = 2 * i + s
                    n = P if not isinstance(i, int) or c < NODE_CHUNKS else NODE_PARTS if c == NODE_CHUNKS else 0
                    if n:
                        wait(dve, loaded[s], 16 * i + 16)
                        wait(dve, added[s], i)
                        nc.vector.tensor_tensor(acc[s][0:n, :], acc[s][0:n, :], t[s][0:n, :], ALU.add).then_inc(added[s], 1)

            loop(dve, STEPS, step, peel_last=True)
            nc.vector.memset(gram_sb[:, :], 0.0).then_inc(mm, 1)
            dve.wait_ge(mm, 1)
            dve.wait_ge(summed, 1)
            nc.vector.tensor_copy(gram_sb[0:D, 0:D], gram[0:D, 0:D])
            link(nc.vector.tensor_copy(gram_sb[D:P, D:P], gram[D:P, D:P]))
            link(nc.vector.tensor_copy(sum_sb[:, :], tsum[:, 0:1]))
            dve.wait_ge(mm, 2)
            link(nc.vector.tensor_tensor(prod[:, :], wg[:, 0:HID], w1[:, :], ALU.mult))
            dve.wait_ge(mm, 3)
            c = lambda k: cols[:, k:k + 1]
            link(nc.vector.tensor_scalar(c(0), moments[:, 0:1], 1.0 / N_NODES, None, ALU.mult))
            link(nc.vector.tensor_scalar(c(1), wg[:, HID:HID + 1], 1.0 / N_NODES, None, ALU.mult))
            link(nc.vector.tensor_tensor(c(2), c(0), c(0), ALU.mult))
            link(nc.vector.tensor_tensor(c(2), c(1), c(2), ALU.subtract))
            link(nc.vector.tensor_scalar(c(2), c(2), 0.0, BN_EPS, ALU.max, ALU.add))
            dve.wait_ge(std_ready, 1)
            link(nc.vector.reciprocal(c(2), c(2)))
            link(nc.vector.tensor_tensor(C["bn_scale"][:, :], c(2), bn[:, 4 * l + 1:4 * l + 2], ALU.mult))
            link(nc.vector.tensor_tensor(c(4), c(0), bn[:, 4 * l:4 * l + 1], ALU.add))
            link(nc.vector.tensor_tensor(c(5), bn[:, 4 * l:4 * l + 1], c(4), ALU.subtract))
            link(nc.vector.tensor_tensor(c(6), c(5), C["bn_scale"][:, :], ALU.mult))
            link(nc.vector.tensor_tensor(C["bn_shift"][:, :], c(6), bn[:, 4 * l + 2:4 * l + 3], ALU.add))

        @block.scalar
        def _(act):
            act.wait_ge(tail, 8)
            nc.scalar.activation(cols[:, 2:3], cols[:, 2:3], ACT.Sqrt).then_inc(std_ready, 1)


def mlp(nc, st, C, table, l, h_table=None, base_table=None, eps_col=None, residual=None, out=None):
    final = out is not None
    loaded, t_used = st.pair("t_loaded"), st.pair("t_used")
    x_loaded, x_used = st.pair("x_loaded"), st.pair("x_used")
    y_stored, b_stored, y_ready, b_ready = st.pair("y_stored"), st.pair("b_stored"), st.pair("y_ready"), st.pair("b_ready")
    units = lambda n: [[st.sem(f"{n}{s}{r}") for r in range(2)] for s in range(2)]
    turned, tt_ready, hid_ps_ready, hid_ready, y_ps_ready, y_done = (
        units(n) for n in ("turned", "tt_ready", "hid_ps_ready", "hid_ready", "y_ps_ready", "y_done"))
    high_ready, rest_ready, middle_ready, low_ready, w2_split = (*(units(n) for n in ("high_ready", "rest_ready", "middle_ready", "low_ready")), st.sem("w2_split"))
    t = [st.sb(f"t{s}", [P, CHW]) for s in range(2)]
    y = [st.sb(f"y{s}", [P, CHW]) for s in range(2)]
    b = [st.sb(f"b{s}", [P, CHW]) for s in range(2)]
    tt = [st.sb(f"tt{r}", [P, 512]) for r in range(2)]
    hid = [st.sb(f"hid{r}", [P, 2, 512]) for r in range(2)]
    hid_part = [[st.sb(f"hid_part{r}{x}", [P, 2, 512], BF16) for x in range(3)] for r in range(2)]
    w2_part = [st.sb(f"w2_part{x}", [HID, D], BF16) for x in range(3)]
    w2_rest = st.sb("w2_rest", [HID, D])
    ORDERS = [(a, b) for a in range(3) for b in range(3 - a)]
    t_ps = [st.ps(f"t_ps{r}", [P, 512]) for r in range(2)]
    hid_ps = [[st.ps(f"hid_ps{r}{e}", [P, 512]) for e in range(2)] for r in range(2)]
    y_ps = [st.ps(f"y_ps{r}", [P, 512]) for r in range(2)]
    w1, w2, b2 = C["w1"][l], C["w2"][l], C["b2"][l]
    PAIR, HALF = 2 * D, CHW // 2
    UNITS = [(s, r) for s in range(2) for r in range(2)]

    def earlier(i, k, back, first):
        return [(i, *UNITS[k - back])] if k >= back else [] if first else [(i - 1, *UNITS[k - back + 4])]

    with st.block() as block:
        @block.sync
        def _(sp):
            def step(i):
                for s in range(2):
                    wait(sp, t_used[s], 2 * i)
                    sp.dma_start(t[s][:, :], flat_chunk(table, 2 * i + s)).then_inc(loaded[s], 16)

            loop(sp, STEPS, step)

        @block.tensor
        def _(pe):
            def turn(i, s, r):
                wait(pe, loaded[s], 16 * i + 16)
                wait(pe, tt_ready[1 - s][r], i + s)
                for q in range(4):
                    lo = r * HALF + q * PAIR
                    last = nc.tensor.transpose(t_ps[r][:, q * P:(q + 1) * P], t[s][:, lo:lo + PAIR], C["iden"][:, :])
                last.then_inc(turned[s][r], 1)

            def hidden(i, s, r):
                wait(pe, tt_ready[s][r], i + 1)
                wait(pe, hid_ready[1 - s][r], i + s)
                for e in range(2):
                    last = nc.tensor.matmul(hid_ps[r][e][:, :], w1[e * D:(e + 1) * D, :], tt[r][e * D:(e + 1) * D, :], start=True, stop=True)
                last.then_inc(hid_ps_ready[s][r], 1)

            def output(i, s, r):
                wait(pe, low_ready[s][r], i + 1)
                wait(pe, y_done[1 - s][r], i + s)
                for q in range(4):
                    for e in range(2):
                        k = 2 * q + e
                        for a, b in ORDERS:
                            last = nc.tensor.matmul(y_ps[r][:, k * D:(k + 1) * D], hid_part[r][a][:, e, q * P:(q + 1) * P], w2_part[b][:, :],
                                                    start=(a, b) == ORDERS[0], stop=(a, b) == ORDERS[-1])
                last.then_inc(y_ps_ready[s][r], 1)

            def step(i, first, last):
                for k, (s, r) in enumerate(UNITS):
                    if k < 3:
                        turn(i, *UNITS[k + 1])
                    elif not last:
                        turn(i + 1, *UNITS[0])
                    hidden(i, s, r)
                    for unit in earlier(i, k, 2, first):
                        output(*unit)

            pe.wait_ge(w2_split, 5)
            turn(0, *UNITS[0])
            step(0, True, False)
            with pe.Fori(1, STEPS - 1) as i:
                step(i, False, False)
            step(STEPS - 1, False, True)
            output(STEPS - 1, *UNITS[2])
            output(STEPS - 1, *UNITS[3])

        @block.scalar
        def _(act):
            def relu(i, s, r):
                wait(act, hid_ps_ready[s][r], i + 1)
                wait(act, low_ready[1 - s][r], i + s)
                for e in range(2):
                    last = nc.scalar.activation(hid[r][:, e, :], hid_ps[r][e][:, :], ACT.Relu, bias=C["bn_shift"][:, 0:1], scale=C["bn_scale"][:, 0:1])
                last.then_inc(hid_ready[s][r], 1)

            def high(i, s, r):
                wait(act, hid_ready[s][r], i + 1)
                wait(act, y_ps_ready[1 - s][r], i + s)
                nc.scalar.copy(hid_part[r][0][:, :, :], hid[r][:, :, :]).then_inc(high_ready[s][r], 1)

            def middle(i, s, r):
                wait(act, rest_ready[s][r], i + 1)
                nc.scalar.copy(hid_part[r][1][:, :, :], hid[r][:, :, :]).then_inc(middle_ready[s][r], 1)

            def step(i, first):
                for k, (s, r) in enumerate(UNITS):
                    relu(i, s, r)
                    for unit in earlier(i, k, 1, first):
                        middle(*unit)
                    high(i, s, r)

            step(0, True)
            with act.Fori(1, STEPS) as i:
                step(i, False)
            middle(STEPS - 1, *UNITS[3])

        @block.vector
        def _(dve):
            def evict(i, s, r):
                wait(dve, turned[s][r], i + 1)
                wait(dve, hid_ps_ready[1 - s][r], i + s)
                nc.vector.tensor_copy(tt[r][:, :], t_ps[r][:, :]).then_inc(tt_ready[s][r], 1)
                wait(dve, tt_ready[s][r], i + 1)
                nc.vector.sem_inc(t_used[s], 1)

            def rest(i, s, r):
                wait(dve, high_ready[s][r], i + 1)
                nc.vector.tensor_tensor(hid[r][:, :, :], hid[r][:, :, :], hid_part[r][0][:, :, :], ALU.subtract).then_inc(rest_ready[s][r], 1)

            def low(i, s, r):
                wait(dve, middle_ready[s][r], i + 1)
                nc.vector.tensor_tensor(hid_part[r][2][:, :, :], hid[r][:, :, :], hid_part[r][1][:, :, :], ALU.subtract).then_inc(low_ready[s][r], 1)

            def finish(i, s, r):
                wait(dve, y_ps_ready[s][r], i + 1)
                half = slice(r * HALF, (r + 1) * HALF)
                if final:
                    wait(dve, x_loaded[s], 16 * i + 16)
                elif r == 0:
                    wait(dve, b_stored[s], 16 * i)
                if r == 0:
                    wait(dve, y_stored[s], 16 * i)
                yh = y[s][:, half]
                nc.vector.tensor_tensor(yh.rearrange("p (k f) -> p k f", f=D), y_ps[r][:, :].rearrange("p (k f) -> p k f", f=D),
                                        b2[:, :].unsqueeze(1).to_broadcast([P, 8, D]), ALU.add).then_inc(y_done[s][r], 1)
                if final:
                    wait(dve, y_done[s][r], i + 1)
                    nc.vector.tensor_tensor(b[s][:, half], yh, b[s][:, half], ALU.add).then_inc(b_ready[s], 1)
                else:
                    wait(dve, y_done[s][r], i + 1)
                    nc.vector.tensor_scalar(b[s][:, half], yh, eps_col, None, ALU.mult).then_inc(b_ready[s], 1)

            def step(i, first, last):
                for k, (s, r) in enumerate(UNITS):
                    if k < 3:
                        evict(i, *UNITS[k + 1])
                    elif not last:
                        evict(i + 1, *UNITS[0])
                    for unit in earlier(i, k, 2, first):
                        finish(*unit)
                    for unit in earlier(i, k, 1, first):
                        low(*unit)
                    rest(i, s, r)

            nc.vector.tensor_copy(w2_part[0][:, :], w2[:, :]).then_inc(w2_split, 1)
            dve.wait_ge(w2_split, 1)
            nc.vector.tensor_tensor(w2_rest[:, :], w2[:, :], w2_part[0][:, :], ALU.subtract).then_inc(w2_split, 1)
            dve.wait_ge(w2_split, 2)
            nc.vector.tensor_copy(w2_part[1][:, :], w2_rest[:, :]).then_inc(w2_split, 1)
            dve.wait_ge(w2_split, 3)
            nc.vector.tensor_tensor(w2_rest[:, :], w2_rest[:, :], w2_part[1][:, :], ALU.subtract).then_inc(w2_split, 1)
            dve.wait_ge(w2_split, 4)
            nc.vector.tensor_copy(w2_part[2][:, :], w2_rest[:, :]).then_inc(w2_split, 1)
            evict(0, *UNITS[0])
            step(0, True, False)
            with dve.Fori(1, STEPS - 1) as i:
                step(i, False, False)
            step(STEPS - 1, False, True)
            low(STEPS - 1, *UNITS[3])
            finish(STEPS - 1, *UNITS[2])
            finish(STEPS - 1, *UNITS[3])

        @block.gpsimd
        def _(pool):
            def residual_rows(i, s):
                pool.dma_start(b[s][:, :], flat_chunk(residual, 2 * i + s)).then_inc(x_loaded[s], 16)

            def step(i):
                for s in range(2):
                    wait(pool, b_ready[s], 2 * i + 2)
                    if final:
                        pool.dma_start(flat_chunk(out, 2 * i + s), b[s][:, :]).then_inc(y_stored[s], 16)
                        if not isinstance(i, int) or i + 1 < STEPS:
                            wait(pool, y_stored[s], 16 * (i + 1))
                            residual_rows(i + 1, s)
                    else:
                        pool.dma_start(flat_chunk(h_table, 2 * i + s), y[s][:, :]).then_inc(y_stored[s], 16)
                        pool.dma_start(flat_chunk(base_table, 2 * i + s), b[s][:, :]).then_inc(b_stored[s], 16)

            for s in range(2) if final else ():
                residual_rows(0, s)
            loop(pool, STEPS, step, peel_last=True)
            for s in range(2):
                pool.wait_ge(y_stored[s], 16 * STEPS)
                if not final:
                    pool.wait_ge(b_stored[s], 16 * STEPS)


def edges(nc, st, C, kind, h_table, base_table, rows_dram, gather_cols, target, edge_attr=None, messages=None):
    scatters = messages is None
    K = len(gather_cols)
    WIDE = K * D
    gathered = [st.pair(f"gathered_{name}") for name in gather_cols]
    admitted = st.sem("admitted")
    scattered, g_idx, s_idx = st.pair("scattered"), st.pair("gather_idx"), st.pair("scatter_idx")
    rows_loaded, eq_ready, merged_ps, merged_ready = (st.pair(x) for x in ("rows_loaded", "eq_ready", "merged_ps", "merged_ready"))
    msg_stored, zeros_stored = st.pair("msg_stored"), st.sem("zeros_stored")
    if scatters:
        rows = [st.sb(f"row_bc{s}", [P, QT, P], INT32) for s in range(2)]
        eq = [st.sb(f"eq{s}", [P, QT, P]) for s in range(2)]
        si = [st.sb(f"si{s}", [P, QT], INT32) for s in range(2)]
        before = [st.sb(f"before{s}", [P, QT, P]) for s in range(2)]
        count, dist = ([st.sb(f"{x}{s}", [P, QT]) for s in range(2)] for x in ("count", "dist"))
        masked, counted, placed = (st.pair(x) for x in ("masked", "counted", "placed"))
        merged = [st.sb(f"merged{s}", [P, QT, D]) for s in range(2)]
        m_ps = [st.ps(f"m_ps{s}", [P, 512]) for s in range(2)]
    G = [st.sb(f"G{s}", [P, QT, WIDE]) for s in range(2)]
    gi = [[st.sb(f"gi{s}{g}", [P, QT], INT32) for g in range(K)] for s in range(2)]
    tiles = lambda c: bass.ds(c * QT, QT)
    if K == 2:
        turned, gt_ready, prod_ps, read, act_in, act_out, msg_ready, worked = (
            st.pair(x) for x in ("turned", "gt_ready", "prod_ps", "prod_read", "act_in", "act_out", "msg_ready", "worked"))
        GT = [st.sb(f"GT{s}", [P, QT * P]) for s in range(2)]
        msg = [st.sb(f"msg{s}", [P, QT, D]) for s in range(2)]
        gt_ps = st.ps("gt_ps", [P, 512])
        g_free = turned
    else:
        msg, g_free = G, merged_ps
    if kind == "attention":
        scored = st.pair("scored")
        ea_loaded, et_ready = st.pair("ea_loaded"), st.pair("et_ready")
        ea = [st.sb(f"ea{s}", [P, QT, D]) for s in range(2)]
        ET = [st.sb(f"ET{s}", [P, 2 * P]) for s in range(2)]
        et_ps, e_ps = st.ps("et_ps", [P, 512]), [st.ps(f"e_ps{x}", [P, 512]) for x in range(2)]
        kvq_ps = [st.ps(f"kvq_ps{x}", [P, 512]) for x in range(2)]
        kvq = [st.sb(f"kvq{s}", [P, QT, 3 * D]) for s in range(2)]
        ee = [st.sb(f"ee{s}", [P, QT, D]) for s in range(2)]
        score = [st.sb(f"score{s}", [P, QT * HEADS]) for s in range(2)]
        ex = [st.sb(f"ex{s}", [P, QT * HEADS]) for s in range(2)]
    if kind == "conv":
        diff_ready = st.pair("diff_ready")
        z_ps = st.ps("z_ps", [P, 512])
        z = [st.sb(f"z{s}", [P, QT, D]) for s in range(2)]
        sg = [st.sb(f"sg{s}", [P, QT, D]) for s in range(2)]

    with st.block() as block:
        @block.sync
        def _(sp):
            def attributes(i, s):
                wait(sp, turned[s], i)
                first = (2 * i + s) * QT
                if not isinstance(i, int):
                    sp.dma_start(ea[s][:, :, :], edge_attr[bass.ds(first * P, QT * P), :].rearrange("(t p) f -> p t f", p=P)).then_inc(ea_loaded[s], 16 * QT)
                else:
                    for k in range(QT):
                        n = min(N_EDGES - (first + k) * P, P)
                        at = (first + k) * P if n > 0 else 0
                        n = n if n > 0 else P
                        sp.dma_start(ea[s][0:n, k, :], edge_attr[at:at + n, :]).then_inc(ea_loaded[s], 16)

            def load(i, s):
                if scatters:
                    wait(sp, eq_ready[s], i)
                    sp.dma_start(rows[s][:, :, :], rows_dram[tiles(2 * i + s), :].rearrange("(a t) e -> a t e", a=1).partition_broadcast(P)).then_inc(rows_loaded[s], 16)
                if kind == "attention":
                    attributes(i, s)

            def store(i, s):
                wait(sp, msg_ready[s], i + 1)
                sp.dma_start(messages[bass.ds(2 * i + s, 1), :, :].rearrange("a p f -> p (a f)"), msg[s][:, :, :].rearrange("p t f -> p (t f)")).then_inc(msg_stored[s], 16)

            def step(i):
                for s in range(2):
                    load(i, s)
                    if not scatters and (s or not (isinstance(i, int) and i == 0)):
                        store(i - 1 + s, 1 - s)

            loop(sp, ESTEPS - 1, step)
            step(ESTEPS - 1)
            if not scatters:
                store(ESTEPS - 1, 1)
                rest = [(c, h) for c in range(2 * ESTEPS, COLS // QT) for h in range(QT * D // P)]
                for c, h in rest:
                    sp.dma_start(messages[c, :, h * P:(h + 1) * P], C["zeros"][:, :]).then_inc(zeros_stored, 16)
                sp.wait_ge(zeros_stored, 16 * len(rest))
                for s in range(2):
                    sp.wait_ge(msg_stored[s], 16 * ESTEPS)

        @block.gpsimd
        def _(pool):
            def gather(i, s, k):
                if k == 0:
                    wait(pool, g_idx[s], i + 1)
                    wait(pool, g_free[s], i)
                    nc.gpsimd.sem_inc(admitted, 1)
                for g in range(K):
                    pool.indirect_dma_start(out=G[s][:, k, g * D:(g + 1) * D], out_offset=None, in_=h_table,
                                            in_offset=bass.IndirectOffsetOnAxis(ap=gi[s][g][:, k:k + 1], axis=0)).then_inc(gathered[g][s], 16)

            def scatter(i, s, k):
                if k == 0:
                    wait(pool, s_idx[s], i + 1)
                    wait(pool, merged_ready[s], i + 1)
                    wait(pool, scattered[1 - s], 16 * QT * (i + s))
                else:
                    wait(pool, scattered[s], 16 * (QT * i + k))
                nc.gpsimd.sem_inc(admitted, 1)
                pool.indirect_dma_start(out=base_table, out_offset=bass.IndirectOffsetOnAxis(ap=si[s][:, k:k + 1], axis=0),
                                        in_=merged[s][:, k, :], in_offset=None, compute_op=ALU.add).then_inc(scattered[s], 16)

            for k in range(QT):
                gather(0, 0, k)
            def step(i):
                for s in range(2):
                    if not scatters:
                        for k in range(QT):
                            gather(i + s, 1 - s, k)
                        continue
                    for k in range(QT):
                        gather(i + s, 1 - s, k)
                        if s or not (isinstance(i, int) and i == 0):
                            scatter(i - 1 + s, 1 - s, k)

            loop(pool, ESTEPS, step)
            for k in range(QT) if scatters else ():
                scatter(ESTEPS - 1, 1, k)
            for s in range(2) if scatters else ():
                pool.wait_ge(scattered[s], 16 * QT * ESTEPS)
            for g in range(K):
                pool.wait_ge(gathered[g][0], 16 * QT * (ESTEPS + 1))

        @block.scalar
        def _(act):
            def gather_columns(i, s):
                wait(act, g_free[s], i)
                for g, name in enumerate(gather_cols):
                    last = nc.scalar.copy(gi[s][g][:, :], C[name + "_i"][:, tiles(2 * i + s)])
                    last.then_inc(g_idx[s], 1) if g == K - 1 else None

            def turned_rows(i, s):
                wait(act, turned[s], i + 1)
                wait(act, prod_ps[s], i)
                nc.scalar.copy(GT[s][:, :], gt_ps[:, :]).then_inc(gt_ready[s], 1)
                if kind == "attention":
                    nc.scalar.copy(ET[s][:, :], et_ps[:, 0:2 * P]).then_inc(et_ready[s], 1)

            gather_columns(0, 0)
            if K == 2:
                gather_columns(0, 1)

            def step(i):
                for s in range(2):
                    if K == 1:
                        gather_columns(i + s, 1 - s)
                    if K == 2:
                        turned_rows(i, s)
                        gather_columns(i + 1, s)
                        wait(act, act_in[s], i + 1)
                    if kind == "attention":
                        nc.scalar.activation(ex[s][:, :], score[s][:, :], ACT.Exp).then_inc(act_out[s], 1)
                    if kind == "conv":
                        nc.scalar.activation(sg[s][:, :, :], z[s][:, :, :], ACT.Sigmoid).then_inc(act_out[s], 1)

            loop(act, ESTEPS, step)

        @block.tensor
        def _(pe):
            def merge(i, s):
                wait(pe, eq_ready[s], i + 1)
                wait(pe, merged_ready[s], i)
                if K == 2:
                    wait(pe, msg_ready[s], i + 1)
                else:
                    wait(pe, gathered[0][s], 16 * QT * (i + 1))
                for k in range(QT):
                    last = nc.tensor.matmul(m_ps[s][:, k * D:(k + 1) * D], eq[s][:, k, :], msg[s][:, k, :], start=True, stop=True)
                last.then_inc(merged_ps[s], 1)

            def turn(i, s):
                wait(pe, gt_ready[1 - s], i + s)
                if kind == "attention":
                    for g in range(K):
                        wait(pe, gathered[g][s], 16 * QT * (i + 1))
                    wait(pe, ea_loaded[s], 16 * QT * (i + 1))
                    wait(pe, et_ready[1 - s], i + s)
                    for k in range(QT // 2):
                        two = ea[s][:, 2 * k:2 * k + 2, :].rearrange("p t f -> p (t f)")
                        nc.tensor.transpose(et_ps[:, k * P:(k + 1) * P], two, C["iden"][:, :])
                else:
                    wait(pe, diff_ready[s], i + 1)
                for k in range(QT):
                    last = nc.tensor.transpose(gt_ps[:, k * P:(k + 1) * P], G[s][:, k, :], C["iden"][:, :])
                last.then_inc(turned[s], 1)

            def products(i, s):
                wait(pe, gt_ready[s], i + 1)
                wait(pe, read[1 - s], i + s)
                if kind == "attention":
                    wait(pe, et_ready[s], i + 1)
                    for k in range(QT):
                        half = slice((k % 2) * D, (k % 2 + 1) * D)
                        nc.tensor.matmul(kvq_ps[k // 2][:, (k % 2) * 3 * D:(k % 2 + 1) * 3 * D], GT[s][:, k * P:(k + 1) * P], C["kvq"][:, :], start=True, stop=True)
                        last = nc.tensor.matmul(e_ps[k % 2][:, (k // 2) * D:(k // 2 + 1) * D], ET[s][half, (k // 2) * P:(k // 2 + 1) * P], C["we"][half, :], start=True, stop=True)
                else:
                    for k in range(QT):
                        last = nc.tensor.matmul(z_ps[:, k * D:(k + 1) * D], GT[s][:, k * P:(k + 1) * P], C["w3"][:, :], start=True, stop=True)
                last.then_inc(prod_ps[s], 1)

            def step(i):
                for s in range(2):
                    if K == 2:
                        turn(i, s)
                        products(i, s)
                    if scatters:
                        merge(i, s)

            loop(pe, ESTEPS, step)

        @block.vector
        def _(dve):
            def equal(i, s):
                wait(dve, rows_loaded[s], 16 * i + 16)
                wait(dve, merged_ps[s], i)
                cols = C[target + "_f"][:, tiles(2 * i + s)].unsqueeze(2).to_broadcast([P, QT, P])
                nc.vector.tensor_tensor(eq[s][:, :, :], rows[s][:, :, :], cols, ALU.is_equal).then_inc(eq_ready[s], 1)

            def scatter_rows(i, s):
                col = C[target + "_f"][:, tiles(2 * i + s)]
                wait(dve, eq_ready[s], i + 1)
                nc.vector.tensor_tensor(before[s][:, :, :], eq[s][:, :, :], C["lower"][:, :].unsqueeze(1).to_broadcast([P, QT, P]), ALU.mult).then_inc(masked[s], 1)
                wait(dve, masked[s], i + 1)
                nc.vector.tensor_reduce(count[s][:, :], before[s][:, :, :], AX.X, ALU.add).then_inc(counted[s], 1)
                wait(dve, counted[s], i + 1)
                nc.vector.tensor_scalar(count[s][:, :], count[s][:, :], 0.0, None, ALU.is_gt).then_inc(placed[s], 1)
                nc.vector.tensor_scalar(dist[s][:, :], col, -1.0, C["spare"][:, 0:1], ALU.mult, ALU.add).then_inc(placed[s], 1)
                wait(dve, placed[s], 3 * i + 2)
                nc.vector.tensor_tensor(dist[s][:, :], dist[s][:, :], count[s][:, :], ALU.mult).then_inc(placed[s], 1)
                wait(dve, placed[s], 3 * i + 3)
                wait(dve, scattered[s], 16 * QT * i)
                nc.vector.tensor_tensor(si[s][:, :], dist[s][:, :], col, ALU.add).then_inc(s_idx[s], 1)

            def evict(i, s):
                wait(dve, merged_ps[s], i + 1)
                wait(dve, scattered[s], 16 * QT * i)
                nc.vector.tensor_copy(merged[s][:, :, :].rearrange("p t f -> p (t f)"), m_ps[s][:, 0:QT * D]).then_inc(merged_ready[s], 1)

            def msg_free(i, s):
                wait(dve, *((merged_ps[s], i) if scatters else (msg_stored[s], 16 * i)))

            def attention(i, s):
                wait(dve, prod_ps[s], i + 1)
                bias = C["kvqe_b"]
                for x in range(2):
                    nc.vector.tensor_tensor(kvq[s][:, 2 * x:2 * x + 2, :], kvq_ps[x][:, 0:6 * D].rearrange("p (t f) -> p t f", t=2),
                                            bias[:, 0:3 * D].unsqueeze(1).to_broadcast([P, 2, 3 * D]), ALU.add)
                    last = nc.vector.tensor_tensor(ee[s][:, x:QT:2, :], e_ps[x][:, 0:2 * D].rearrange("p (t f) -> p t f", t=2),
                                                   bias[:, 3 * D:4 * D].unsqueeze(1).to_broadcast([P, 2, D]), ALU.add)
                last.then_inc(read[s], 1)
                wait(dve, read[s], i + 1)
                q = kvq[s][:, :, 2 * D:3 * D]
                nc.vector.tensor_tensor(q, kvq[s][:, :, 0:D], q, ALU.mult).then_inc(worked[s], 1)
                wait(dve, worked[s], 2 * i + 1)
                nc.vector.scalar_tensor_tensor(ee[s][:, :, :], q, float((D // HEADS) ** -0.5), ee[s][:, :, :], ALU.mult, ALU.mult).then_inc(worked[s], 1)
                wait(dve, worked[s], 2 * i + 2)
                nc.vector.tensor_reduce(score[s][:, :], ee[s][:, :, :].rearrange("p t (h d) -> p (t h) d", h=HEADS), AX.X, ALU.add).then_inc(scored[s], 1)
                wait(dve, scored[s], i + 1)
                nc.vector.tensor_scalar(score[s][:, :], score[s][:, :], -5.0, 5.0, ALU.max, ALU.min).then_inc(act_in[s], 1)
                wait(dve, act_out[s], i + 1)
                msg_free(i, s)
                for k in range(QT):
                    last = nc.vector.tensor_tensor(msg[s][:, k, :].rearrange("p (h d) -> p h d", h=HEADS),
                                                   kvq[s][:, k, D:2 * D].rearrange("p (h d) -> p h d", h=HEADS),
                                                   ex[s][:, k * HEADS:(k + 1) * HEADS].unsqueeze(2).to_broadcast([P, HEADS, D // HEADS]), ALU.mult)
                last.then_inc(msg_ready[s], 1)

            def difference(i, s):
                for g in range(K):
                    wait(dve, gathered[g][s], 16 * QT * (i + 1))
                nc.vector.tensor_tensor(G[s][:, :, D:2 * D], G[s][:, :, D:2 * D], G[s][:, :, 0:D], ALU.subtract).then_inc(diff_ready[s], 1)

            def convolution(i, s):
                wait(dve, prod_ps[s], i + 1)
                row = lambda k: C["ec"][:, k * D:(k + 1) * D].unsqueeze(1).to_broadcast([P, QT, D])
                nc.vector.tensor_tensor(z[s][:, :, :], z_ps[:, 0:QT * D].rearrange("p (t f) -> p t f", t=QT), row(0), ALU.subtract).then_inc(read[s], 1)
                wait(dve, read[s], i + 1)
                nc.vector.tensor_tensor(z[s][:, :, :], z[s][:, :, :], row(1), ALU.mult).then_inc(worked[s], 1)
                wait(dve, worked[s], i + 1)
                nc.vector.tensor_tensor(z[s][:, :, :], z[s][:, :, :], row(2), ALU.add).then_inc(act_in[s], 1)
                wait(dve, act_out[s], i + 1)
                msg_free(i, s)
                nc.vector.tensor_tensor(msg[s][:, :, :], z[s][:, :, :], sg[s][:, :, :], ALU.mult).then_inc(msg_ready[s], 1)

            def step(i):
                for s in range(2):
                    if scatters:
                        equal(i, s)
                    if kind == "attention":
                        attention(i, s)
                    if kind == "conv":
                        difference(i, s)
                        convolution(i, s)
                    if scatters:
                        scatter_rows(i, s)
                        evict(i, s)

            loop(dve, ESTEPS, step)


def build(nc, I, out, stop=None):
    ctx = ExitStack()
    with ctx:
        sb = lambda name, shape, dt=FP32: ctx.enter_context(nc.sbuf_tensor(name, shape, dt))
        table = lambda name: nc.dram_tensor(name, (ROWS, D), FP32, kind="Internal").ap()
        h_table, sum_table, x_table = table("h_table"), table("sum_table"), table("x_table")
        messages = nc.dram_tensor("messages", (COLS // QT, P, QT * D), FP32, kind="Internal").ap()
        src_rows, dst_rows = (nc.dram_tensor(n, (COLS, P), INT32, kind="Internal").ap() for n in ("src_rows", "dst_rows"))
        C = {n: sb(n, [P, P]) for n in ("iden", "lower", "zeros", "ones_sq")}
        C["ones"] = sb("ones", [P, 2])
        C["spare_i"], C["spare"] = sb("spare_i", [P, 1], INT32), sb("spare", [P, 1])
        for n in ("src", "dst"):
            C[n + "_f"], C[n + "_i"] = sb(n + "_f", [P, COLS]), sb(n + "_i", [P, COLS], INT32)
        C["w1"] = [sb(f"w1_{l}", [P, HID]) for l in range(3)]
        C["w2"] = [sb(f"w2_{l}", [HID, D]) for l in range(3)]
        C["b2"] = [sb(f"b2_{l}", [P, D]) for l in range(3)]
        C["bn"] = sb("bn", [P, 12])
        C["bn_scale"], C["bn_shift"] = sb("bn_scale", [P, 1]), sb("bn_shift", [P, 1])
        C["eps1"] = sb("eps1", [P, 4])
        C["we"], C["kvq"], C["kvqe_b"] = sb("we", [P, D]), sb("kvq", [P, 3 * D]), sb("kvqe_b", [P, 4 * D])
        C["w3"], C["ec"] = sb("w3", [P, D]), sb("ec", [P, 4 * D])
        eps = lambda k: C["eps1"][:, k:k + 1]

        names = (f"stage{n}" for n in range(99))

        def run(f, *a, **k):
            with Stage(nc, next(names)) as st:
                f(nc, st, *a, **k)

        run(setup, I, C, src_rows, dst_rows)
        C["place_i"], C["place"] = sb("place_i", [P, WIN], INT32), sb("place", [P, WIN], FP16)
        C["rel"], C["ring_off"], C["unfit"] = sb("rel", [P, WINDOWS * WT]), sb("ring_off", [1, WINDOWS * WT], INT32), sb("unfit", [1, 1], INT32)
        run(plan, I, C, dst_rows)

        def sum_edges(table, general):
            if general:
                run(edges, C, "sum", h_table, table, dst_rows, ["src"], "dst")
            else:
                run(window_sum, C, table, h_table=h_table)

        def program(general):
            nc.all_engine_barrier()
            run(layernorm, C, I["x"], h_table, x_table, eps(0), add_source=True)
            sum_edges(x_table, general)
            run(layernorm, C, x_table, h_table, sum_table, eps(1))
            for l in range(3):
                sum_edges(sum_table, general)
                run(batch_stats, C, sum_table, l)
                if l < 2:
                    run(mlp, C, sum_table, l, h_table=h_table, base_table=sum_table, eps_col=eps(l + 2))
                else:
                    run(mlp, C, sum_table, l, residual=x_table, out=out)
            run(layernorm, C, out, h_table)
            run(edges, C, "attention", h_table, out, dst_rows, ["src", "dst"], "dst", edge_attr=I["edge_attr_64"], messages=None if general else messages)
            if not general:
                run(window_sum, C, out, messages=messages)
            run(layernorm, C, out, h_table)
            run(edges, C, "conv", h_table, out, src_rows, ["src", "dst"], "src")
            nc.all_engine_barrier()

        unfit = nc.values_load(C["unfit"][0:1, 0:1], min_val=0, max_val=1 << 20)
        with nc.If(unfit == 0):
            program(general=False)
        with nc.Else():
            program(general=True)


_INS = ["x", "src", "dst", "edge_attr_64", "L0_gnn_eps", "L1_gnn_W1", "L1_gnn_b1", "L1_gnn_gamma", "L1_gnn_beta",
        "L1_gnn_W2", "L1_gnn_b2", "L1_gnn_eps", "L2_gnn_WQ", "L2_gnn_bQ", "L2_gnn_WK", "L2_gnn_bK", "L2_gnn_WE",
        "L2_gnn_bE", "L2_gnn_WV", "L2_gnn_bV", "L3_gnn_W", "L3_gnn_gamma", "L3_gnn_beta", "L3_gnn_running_mean",
        "L3_gnn_running_var"]


def kernel(**inputs):
    import numpy as _np
    import concourse.bacc as _bacc
    from concourse.bass_utils import run_bass_kernel_spmd as _run

    nc = _bacc.Bacc("TRN2", target_bir_lowering=False, num_devices=1)
    arrays, I = {}, {}
    for name in _INS:
        a = _np.ascontiguousarray(inputs[name])
        arrays[f"in_{name}"] = a
        I[name] = nc.dram_tensor(f"in_{name}", a.shape, mybir.dt.from_np(a.dtype), kind="ExternalInput").ap()
    out = nc.dram_tensor("out_nodes", (ROWS, D), FP32, kind="ExternalOutput").ap()
    build(nc, I, out)
    r = _run(nc, [arrays], core_ids=[0])
    return r.results[0]["out_nodes"][:N_NODES]
```
